# Optimizing a Trainium2 kernel written in Bass

```python
import numpy as np
import jax
import jax.numpy as jnp

def _softmax(x, axis=-1):
    return jax.nn.softmax(x, axis=axis)

def _gelu(x):
    return jax.nn.gelu(x, approximate=True)

def _silu(x):
    return jax.nn.silu(x)

def _sigmoid(x):
    return jax.nn.sigmoid(x)

def _layernorm(x, axis=-1, eps=1e-05):
    m = jnp.mean(x, axis=axis, keepdims=True)
    v = jnp.var(x, axis=axis, keepdims=True)
    return (x - m) / jnp.sqrt(v + eps)

def _scatter_add(tgt, idx, src, axis=0):
    return tgt.at[idx].add(src)

def _segment_sum(src, seg, n):
    return jax.ops.segment_sum(src, seg, n)
kernel_name = 'mk_decoder_preln_d2_seqx_r8_1857c7'

def setup_inputs(seed: int=0):
    np.random.seed(seed)
    _w = jnp.asarray

    def _rec_inputs():
        import jax
        import jax.numpy as jnp
        _rk = jax.random.key(seed)
        x = 7.22e-05 + 1 * jax.random.normal(jax.random.fold_in(_rk, 1), (16, 128, 128), jnp.float32)
        _lenS = 128 - jax.random.randint(jax.random.fold_in(_rk, 7), (16,), 0, max(1, 128 // 4) + 1, jnp.int32)
        _lenS2 = 128 - jax.random.randint(jax.random.fold_in(_rk, 8), (16,), 0, max(1, 128 // 4) + 1, jnp.int32)
        _ctx_1024P = jax.random.normal(jax.random.fold_in(_rk, 11), (16, 16, 128), jnp.float32)
        _ctx_1024c = jax.random.dirichlet(jax.random.fold_in(_rk, 511), 0.3 * jnp.ones((16,), jnp.float32), (16, 128))
        _ctx_1024t = jnp.einsum('bsk,bkd->bsd', _ctx_1024c, _ctx_1024P)
        _ctx_1024t = _ctx_1024t * jax.lax.rsqrt(jnp.mean(jnp.square(_ctx_1024t)) + 1e-12) * 0.953939
        ctx_1024 = 4.13588e-05 + 0.999923 * (_ctx_1024t + 0.3 * jax.random.normal(jax.random.fold_in(_rk, 611), (16, 128, 128), jnp.float32))
        _validS = jnp.arange(128)[None, :] < _lenS[:, None]
        _validS2 = jnp.arange(128)[None, :] < _lenS2[:, None]
        _causal = jnp.tril(jnp.ones((128, 128), dtype=bool))
        mask_1x1xSxS2_ik0 = jnp.where(jnp.broadcast_to(_validS2[0:1, None, None, :], (1, 1, 128, 128)), 0, 1).astype(jnp.int32)
        return (x, ctx_1024, mask_1x1xSxS2_ik0)
    x, ctx_1024, mask_1x1xSxS2_ik0 = _rec_inputs()

    def _L0_attn_setup():
        import math
        import jax, jax.numpy as jnp
        import numpy as np
        B, T, D, H, L = (8, 256, 128, 16, 4)
        DK = D // H
        EPS_LN = 1e-05
        EPS_ATTN = 1e-06

        def _layernorm(x, scale, bias):
            mu = jnp.mean(x, axis=-1, keepdims=True)
            var = jnp.mean(jnp.square(x - mu), axis=-1, keepdims=True)
            return (x - mu) * jax.lax.rsqrt(var + EPS_LN) * scale + bias

        def _sinusoidal_pos_emb(t, d):
            half = d // 2
            freq = jnp.exp(jnp.arange(half, dtype=jnp.float32) * (-math.log(10000.0) / (half - 1)))
            pos = (jnp.arange(t, dtype=jnp.float32) + 1.0)[:, None] * freq[None, :]
            return jnp.concatenate([jnp.sin(pos), jnp.cos(pos)], axis=-1)

        def _linear_attention(q, k, v):
            qp = jax.nn.elu(q) + 1.0
            kp = jax.nn.elu(k) + 1.0
            kv = jnp.einsum('bshd,bshm->bhmd', kp, v)
            ksum = jnp.sum(kp, axis=1)
            z = 1.0 / (jnp.einsum('blhd,bhd->blh', qp, ksum) + EPS_ATTN)
            return jnp.einsum('blhd,bhmd,blh->blhm', qp, kv, z)

        def _encoder_layer(x, Wq, bq, Wk, bk, Wv, bv, Wo, bo, W1, b1, W2, b2, ln1_s, ln1_b, ln2_s, ln2_b):
            b, t, d = x.shape
            h = _layernorm(x, ln1_s, ln1_b)
            q = (h @ Wq + bq).reshape(b, t, H, DK)
            k = (h @ Wk + bk).reshape(b, t, H, DK)
            v = (h @ Wv + bv).reshape(b, t, H, DK)
            attn = _linear_attention(q, k, v).reshape(b, t, d)
            x = x + (attn @ Wo + bo)
            h = _layernorm(x, ln2_s, ln2_b)
            h = jax.nn.relu(h @ W1 + b1) @ W2 + b2
            return x + h
        key = jax.random.key(seed)
        ks = jax.random.split(key, 8)
        w = lambda k, shape: jax.random.normal(k, shape, dtype=jnp.float32) * 0.02
        return {'x_in': jax.random.normal(ks[0], (B, T, D), dtype=jnp.float32), 'Wq': w(ks[1], (L, D, D)), 'bq': jnp.zeros((L, D), jnp.float32), 'Wk': w(ks[2], (L, D, D)), 'bk': jnp.zeros((L, D), jnp.float32), 'Wv': w(ks[3], (L, D, D)), 'bv': jnp.zeros((L, D), jnp.float32), 'Wo': w(ks[4], (L, D, D)), 'bo': jnp.zeros((L, D), jnp.float32), 'W1': w(ks[5], (L, D, 4 * D)), 'b1': jnp.zeros((L, 4 * D), jnp.float32), 'W2': w(ks[6], (L, 4 * D, D)), 'b2': jnp.zeros((L, D), jnp.float32), 'ln1_s': jnp.ones((L, D), jnp.float32), 'ln1_b': jnp.zeros((L, D), jnp.float32), 'ln2_s': jnp.ones((L, D), jnp.float32), 'ln2_b': jnp.zeros((L, D), jnp.float32), 'lnf_s': jnp.ones((D,), jnp.float32), 'lnf_b': jnp.zeros((D,), jnp.float32)}
    _L0_attn_all = _L0_attn_setup()
    _L0_attn_in = {k: v for k, v in _L0_attn_all.items() if k in ('Wq', 'bq', 'Wk', 'bk', 'Wv', 'bv', 'Wo', 'bo', 'W1', 'b1', 'W2', 'b2', 'ln1_s', 'ln1_b', 'ln2_s', 'ln2_b', 'lnf_s', 'lnf_b')}
    del _L0_attn_all

    def _L0_xattn_setup():
        import jax, jax.numpy as jnp
        import numpy as np
        D_MODEL = 128
        N_HEAD = 16
        DEPTH = D_MODEL // N_HEAD
        B, S = (4, 256)
        NEG = -1000000000.0
        key = jax.random.key(seed)
        ks = jax.random.split(key, 8)
        scale = 1.0 / np.sqrt(D_MODEL)
        Q = jax.random.normal(ks[0], (B, S, D_MODEL), dtype=jnp.float32)
        K = jax.random.normal(ks[1], (B, S, D_MODEL), dtype=jnp.float32)
        V = jax.random.normal(ks[2], (B, S, D_MODEL), dtype=jnp.float32)
        mask = jnp.tril(jnp.ones((S, S), dtype=jnp.int32))[None, None]
        Wq = jax.random.normal(ks[3], (D_MODEL, D_MODEL), dtype=jnp.float32) * scale
        Wk = jax.random.normal(ks[4], (D_MODEL, D_MODEL), dtype=jnp.float32) * scale
        Wv = jax.random.normal(ks[5], (D_MODEL, D_MODEL), dtype=jnp.float32) * scale
        Wo = jax.random.normal(ks[6], (D_MODEL, D_MODEL), dtype=jnp.float32) * scale
        bq = jnp.zeros((D_MODEL,), jnp.float32)
        bk = jnp.zeros((D_MODEL,), jnp.float32)
        bv = jnp.zeros((D_MODEL,), jnp.float32)
        bo = jnp.zeros((D_MODEL,), jnp.float32)
        return {'Q': Q, 'K': K, 'V': V, 'mask': mask, 'Wq': Wq, 'bq': bq, 'Wk': Wk, 'bk': bk, 'Wv': Wv, 'bv': bv, 'Wo': Wo, 'bo': bo}
    _L0_xattn_all = _L0_xattn_setup()
    _L0_xattn_in = {k: v for k, v in _L0_xattn_all.items() if k in ('Wq', 'bq', 'Wk', 'bk', 'Wv', 'bv', 'Wo', 'bo')}
    del _L0_xattn_all

    def _L0_ffn_setup():
        import jax, jax.numpy as jnp
        import numpy as np
        B, S, D_MODEL, D_HIDDEN = (4, 256, 128, 512)

        def act_quant(x):
            scale = 127.0 / jnp.clip(jnp.max(jnp.abs(x), axis=-1, keepdims=True), 1e-05)
            return jnp.clip(jnp.round(x * scale), -128, 127) / scale

        def weight_quant(w):
            scale = 1.0 / jnp.clip(jnp.mean(jnp.abs(w)), 1e-05)
            return jnp.clip(jnp.round(w * scale), -1, 1) / scale

        def bit_linear(x, w):
            xq = x + jax.lax.stop_gradient(act_quant(x) - x)
            wq = w + jax.lax.stop_gradient(weight_quant(w) - w)
            return jnp.einsum('bsd,hd->bsh', xq, wq)

        def depthwise_conv1d(x_bcl, w, b):
            y = jax.lax.conv_general_dilated(x_bcl, w, window_strides=(1,), padding=[(1, 1)], dimension_numbers=('NCH', 'OIH', 'NCH'), feature_group_count=x_bcl.shape[1])
            return y + b[None, :, None]
        key = jax.random.key(seed)
        ks = jax.random.split(key, 5)
        lim1 = 1.0 / np.sqrt(D_MODEL)
        lim2 = 1.0 / np.sqrt(D_HIDDEN)
        limc = 1.0 / np.sqrt(3.0)
        return {'x': jax.random.normal(ks[0], (B, S, D_MODEL), dtype=jnp.float32), 'w1': jax.random.uniform(ks[1], (D_HIDDEN, D_MODEL), jnp.float32, -lim1, lim1), 'conv_w': jax.random.uniform(ks[2], (D_HIDDEN, 1, 3), jnp.float32, -limc, limc), 'conv_b': jax.random.uniform(ks[3], (D_HIDDEN,), jnp.float32, -limc, limc), 'w2': jax.random.uniform(ks[4], (D_MODEL, D_HIDDEN), jnp.float32, -lim2, lim2)}
    _L0_ffn_all = _L0_ffn_setup()
    _L0_ffn_in = {k: v for k, v in _L0_ffn_all.items() if k in ('w1', 'conv_w', 'conv_b', 'w2')}
    del _L0_ffn_all

    def _L1_attn_setup():
        import jax, jax.numpy as jnp
        import numpy as np
        NUM_HEADS = 16
        D_MODEL = 128
        D_HEAD = D_MODEL // NUM_HEADS
        TOP_K = 64
        key = jax.random.key(seed)
        k0, k1, k2 = jax.random.split(key, 3)
        B, S = (2, 256)
        x = jax.random.normal(k0, (B, S, D_MODEL), dtype=jnp.float32)
        w_qkv_w = jax.random.normal(k1, (3 * D_MODEL, D_MODEL), dtype=jnp.float32) * (1.0 / np.sqrt(D_MODEL))
        w_qkv_b = jnp.zeros((3 * D_MODEL,), dtype=jnp.float32)
        w_out_w = jax.random.normal(k2, (D_MODEL, D_MODEL), dtype=jnp.float32) * (1.0 / np.sqrt(D_MODEL))
        w_out_b = jnp.zeros((D_MODEL,), dtype=jnp.float32)
        return {'x': x, 'w_qkv_w': w_qkv_w, 'w_qkv_b': w_qkv_b, 'w_out_w': w_out_w, 'w_out_b': w_out_b}
    _L1_attn_all = _L1_attn_setup()
    _L1_attn_in = {k: v for k, v in _L1_attn_all.items() if k in ('w_qkv_w', 'w_qkv_b', 'w_out_w', 'w_out_b')}
    del _L1_attn_all

    def _L1_xattn_setup():
        import jax, jax.numpy as jnp
        import numpy as np
        N_HEADS = 4
        IN_FEATURES = 128

        def _channel_attention(qm, km, vm, scale):
            b, n, c = qm.shape
            d = c // N_HEADS
            qh = qm.reshape(b, n, N_HEADS, d).transpose(0, 2, 3, 1)
            kh = km.reshape(b, n, N_HEADS, d).transpose(0, 2, 3, 1)
            vh = vm.reshape(b, n, N_HEADS, d).transpose(0, 2, 3, 1)
            scores = jnp.einsum('bhdn,bhen->bhde', qh, kh) * scale
            attn = jax.nn.softmax(scores, axis=-1)
            out = jnp.einsum('bhde,bhen->bhdn', attn, vh)
            return out.transpose(0, 3, 1, 2).reshape(b, n, c)
        key = jax.random.key(seed)
        ks = jax.random.split(key, 20)
        B, HW, C = (2, 2048, 128)
        inp = {'q': jax.random.normal(ks[0], (B, HW, C), dtype=jnp.float32), 'k': jax.random.normal(ks[1], (B, HW, C), dtype=jnp.float32), 'v': jax.random.normal(ks[2], (B, HW, C), dtype=jnp.float32)}
        names = ['wqg', 'bqg', 'wkg', 'bkg', 'wvg', 'bvg', 'wql', 'bql', 'wkl', 'bkl', 'wvl', 'bvl', 'wp', 'bp']
        for i, n in enumerate(names):
            inp[n] = jax.random.normal(ks[3 + i], (C,), dtype=jnp.float32)
        return inp
    _L1_xattn_all = _L1_xattn_setup()
    _L1_xattn_in = {k: v for k, v in _L1_xattn_all.items() if k in ('wqg', 'bqg', 'wkg', 'bkg', 'wvg', 'bvg', 'wql', 'bql', 'wkl', 'bkl', 'wvl', 'bvl', 'wp', 'bp')}
    del _L1_xattn_all

    def _L1_ffn_setup():
        import jax, jax.numpy as jnp
        import numpy as np
        NUM_EXPERTS = 8
        HIDDEN = 128
        FFN = 512
        BATCH = 2
        SEQ = 256
        key = jax.random.key(seed)
        k_x, k_g, k_u, k_d = jax.random.split(key, 4)
        scale_in = 1.0 / np.sqrt(HIDDEN)
        scale_mid = 1.0 / np.sqrt(FFN)
        return {'hidden_states': jax.random.normal(k_x, (BATCH, SEQ, HIDDEN), dtype=jnp.float32), 'Wg': jax.random.normal(k_g, (NUM_EXPERTS, HIDDEN, FFN), dtype=jnp.float32) * scale_in, 'Wu': jax.random.normal(k_u, (NUM_EXPERTS, HIDDEN, FFN), dtype=jnp.float32) * scale_in, 'Wd': jax.random.normal(k_d, (NUM_EXPERTS, FFN, HIDDEN), dtype=jnp.float32) * scale_mid}
    _L1_ffn_all = _L1_ffn_setup()
    _L1_ffn_in = {k: v for k, v in _L1_ffn_all.items() if k in ('Wg', 'Wu', 'Wd')}
    del _L1_ffn_all
    return {'x': x, 'ctx_1024': ctx_1024, 'mask_1x1xSxS2_ik0': mask_1x1xSxS2_ik0, 'L0_attn_Wq': _L0_attn_in['Wq'], 'L0_attn_bq': _L0_attn_in['bq'], 'L0_attn_Wk': _L0_attn_in['Wk'], 'L0_attn_bk': _L0_attn_in['bk'], 'L0_attn_Wv': _L0_attn_in['Wv'], 'L0_attn_bv': _L0_attn_in['bv'], 'L0_attn_Wo': _L0_attn_in['Wo'], 'L0_attn_bo': _L0_attn_in['bo'], 'L0_attn_W1': _L0_attn_in['W1'], 'L0_attn_b1': _L0_attn_in['b1'], 'L0_attn_W2': _L0_attn_in['W2'], 'L0_attn_b2': _L0_attn_in['b2'], 'L0_attn_ln1_s': _L0_attn_in['ln1_s'], 'L0_attn_ln1_b': _L0_attn_in['ln1_b'], 'L0_attn_ln2_s': _L0_attn_in['ln2_s'], 'L0_attn_ln2_b': _L0_attn_in['ln2_b'], 'L0_attn_lnf_s': _L0_attn_in['lnf_s'], 'L0_attn_lnf_b': _L0_attn_in['lnf_b'], 'L0_xattn_Wq': _L0_xattn_in['Wq'], 'L0_xattn_bq': _L0_xattn_in['bq'], 'L0_xattn_Wk': _L0_xattn_in['Wk'], 'L0_xattn_bk': _L0_xattn_in['bk'], 'L0_xattn_Wv': _L0_xattn_in['Wv'], 'L0_xattn_bv': _L0_xattn_in['bv'], 'L0_xattn_Wo': _L0_xattn_in['Wo'], 'L0_xattn_bo': _L0_xattn_in['bo'], 'L0_ffn_w1': _L0_ffn_in['w1'], 'L0_ffn_conv_w': _L0_ffn_in['conv_w'], 'L0_ffn_conv_b': _L0_ffn_in['conv_b'], 'L0_ffn_w2': _L0_ffn_in['w2'], 'L1_attn_w_qkv_w': _L1_attn_in['w_qkv_w'], 'L1_attn_w_qkv_b': _L1_attn_in['w_qkv_b'], 'L1_attn_w_out_w': _L1_attn_in['w_out_w'], 'L1_attn_w_out_b': _L1_attn_in['w_out_b'], 'L1_xattn_wqg': _L1_xattn_in['wqg'], 'L1_xattn_bqg': _L1_xattn_in['bqg'], 'L1_xattn_wkg': _L1_xattn_in['wkg'], 'L1_xattn_bkg': _L1_xattn_in['bkg'], 'L1_xattn_wvg': _L1_xattn_in['wvg'], 'L1_xattn_bvg': _L1_xattn_in['bvg'], 'L1_xattn_wql': _L1_xattn_in['wql'], 'L1_xattn_bql': _L1_xattn_in['bql'], 'L1_xattn_wkl': _L1_xattn_in['wkl'], 'L1_xattn_bkl': _L1_xattn_in['bkl'], 'L1_xattn_wvl': _L1_xattn_in['wvl'], 'L1_xattn_bvl': _L1_xattn_in['bvl'], 'L1_xattn_wp': _L1_xattn_in['wp'], 'L1_xattn_bp': _L1_xattn_in['bp'], 'L1_ffn_Wg': _L1_ffn_in['Wg'], 'L1_ffn_Wu': _L1_ffn_in['Wu'], 'L1_ffn_Wd': _L1_ffn_in['Wd']}

def reference(x, ctx_1024, mask_1x1xSxS2_ik0, L0_attn_Wq, L0_attn_bq, L0_attn_Wk, L0_attn_bk, L0_attn_Wv, L0_attn_bv, L0_attn_Wo, L0_attn_bo, L0_attn_W1, L0_attn_b1, L0_attn_W2, L0_attn_b2, L0_attn_ln1_s, L0_attn_ln1_b, L0_attn_ln2_s, L0_attn_ln2_b, L0_attn_lnf_s, L0_attn_lnf_b, L0_xattn_Wq, L0_xattn_bq, L0_xattn_Wk, L0_xattn_bk, L0_xattn_Wv, L0_xattn_bv, L0_xattn_Wo, L0_xattn_bo, L0_ffn_w1, L0_ffn_conv_w, L0_ffn_conv_b, L0_ffn_w2, L1_attn_w_qkv_w, L1_attn_w_qkv_b, L1_attn_w_out_w, L1_attn_w_out_b, L1_xattn_wqg, L1_xattn_bqg, L1_xattn_wkg, L1_xattn_bkg, L1_xattn_wvg, L1_xattn_bvg, L1_xattn_wql, L1_xattn_bql, L1_xattn_wkl, L1_xattn_bkl, L1_xattn_wvl, L1_xattn_bvl, L1_xattn_wp, L1_xattn_bp, L1_ffn_Wg, L1_ffn_Wu, L1_ffn_Wd):
    import jax
    import jax.numpy as jnp

    def _L0_attn_ref(x_in, Wq, bq, Wk, bk, Wv, bv, Wo, bo, W1, b1, W2, b2, ln1_s, ln1_b, ln2_s, ln2_b, lnf_s, lnf_b):
        import math
        import jax, jax.numpy as jnp
        import numpy as np
        B, T, D, H, L = (8, 256, 128, 16, 4)
        DK = D // H
        EPS_LN = 1e-05
        EPS_ATTN = 1e-06

        def _layernorm(x, scale, bias):
            mu = jnp.mean(x, axis=-1, keepdims=True)
            var = jnp.mean(jnp.square(x - mu), axis=-1, keepdims=True)
            return (x - mu) * jax.lax.rsqrt(var + EPS_LN) * scale + bias

        def _sinusoidal_pos_emb(t, d):
            half = d // 2
            freq = jnp.exp(jnp.arange(half, dtype=jnp.float32) * (-math.log(10000.0) / (half - 1)))
            pos = (jnp.arange(t, dtype=jnp.float32) + 1.0)[:, None] * freq[None, :]
            return jnp.concatenate([jnp.sin(pos), jnp.cos(pos)], axis=-1)

        def _linear_attention(q, k, v):
            qp = jax.nn.elu(q) + 1.0
            kp = jax.nn.elu(k) + 1.0
            kv = jnp.einsum('bshd,bshm->bhmd', kp, v)
            ksum = jnp.sum(kp, axis=1)
            z = 1.0 / (jnp.einsum('blhd,bhd->blh', qp, ksum) + EPS_ATTN)
            return jnp.einsum('blhd,bhmd,blh->blhm', qp, kv, z)

        def _encoder_layer(x, Wq, bq, Wk, bk, Wv, bv, Wo, bo, W1, b1, W2, b2, ln1_s, ln1_b, ln2_s, ln2_b):
            b, t, d = x.shape
            h = _layernorm(x, ln1_s, ln1_b)
            q = (h @ Wq + bq).reshape(b, t, H, DK)
            k = (h @ Wk + bk).reshape(b, t, H, DK)
            v = (h @ Wv + bv).reshape(b, t, H, DK)
            attn = _linear_attention(q, k, v).reshape(b, t, d)
            x = x + (attn @ Wo + bo)
            h = _layernorm(x, ln2_s, ln2_b)
            h = jax.nn.relu(h @ W1 + b1) @ W2 + b2
            return x + h
        b, t, d = x_in.shape
        x = math.sqrt(d) * x_in + _sinusoidal_pos_emb(t, d)[None, :, :]
        for i in range(L):
            x = _encoder_layer(x, Wq[i], bq[i], Wk[i], bk[i], Wv[i], bv[i], Wo[i], bo[i], W1[i], b1[i], W2[i], b2[i], ln1_s[i], ln1_b[i], ln2_s[i], ln2_b[i])
        return _layernorm(x, lnf_s, lnf_b)

    def _L0_xattn_ref(Q, K, V, mask, Wq, bq, Wk, bk, Wv, bv, Wo, bo):
        import jax, jax.numpy as jnp
        import numpy as np
        D_MODEL = 128
        N_HEAD = 16
        DEPTH = D_MODEL // N_HEAD
        B, S = (4, 256)
        NEG = -1000000000.0
        b, s, _ = Q.shape
        q = Q @ Wq.T + bq
        k = K @ Wk.T + bk
        v = V @ Wv.T + bv
        q = q.reshape(b, s, N_HEAD, DEPTH).transpose(0, 2, 1, 3)
        k = k.reshape(b, s, N_HEAD, DEPTH).transpose(0, 2, 1, 3)
        v = v.reshape(b, s, N_HEAD, DEPTH).transpose(0, 2, 1, 3)
        scores = jnp.einsum('bhqd,bhkd->bhqk', q, k) / jnp.sqrt(jnp.float32(DEPTH))
        scores = jnp.where(mask == 0, jnp.float32(NEG), scores)
        weights = jax.nn.softmax(scores, axis=-1)
        x = jnp.einsum('bhqk,bhkd->bhqd', weights, v)
        x = x.transpose(0, 2, 1, 3).reshape(b, s, D_MODEL)
        return x @ Wo.T + bo

    def _L0_ffn_ref(x, w1, conv_w, conv_b, w2):
        import jax, jax.numpy as jnp
        import numpy as np
        B, S, D_MODEL, D_HIDDEN = (4, 256, 128, 512)

        def act_quant(x):
            scale = 127.0 / jnp.clip(jnp.max(jnp.abs(x), axis=-1, keepdims=True), 1e-05)
            return jnp.clip(jnp.round(x * scale), -128, 127) / scale

        def weight_quant(w):
            scale = 1.0 / jnp.clip(jnp.mean(jnp.abs(w)), 1e-05)
            return jnp.clip(jnp.round(w * scale), -1, 1) / scale

        def bit_linear(x, w):
            xq = x + jax.lax.stop_gradient(act_quant(x) - x)
            wq = w + jax.lax.stop_gradient(weight_quant(w) - w)
            return jnp.einsum('bsd,hd->bsh', xq, wq)

        def depthwise_conv1d(x_bcl, w, b):
            y = jax.lax.conv_general_dilated(x_bcl, w, window_strides=(1,), padding=[(1, 1)], dimension_numbers=('NCH', 'OIH', 'NCH'), feature_group_count=x_bcl.shape[1])
            return y + b[None, :, None]
        h = bit_linear(x, w1)
        h = depthwise_conv1d(h.transpose(0, 2, 1), conv_w, conv_b)
        h = h.transpose(0, 2, 1)
        h = jax.nn.silu(h)
        return bit_linear(h, w2)

    def _L1_attn_ref(x, w_qkv_w, w_qkv_b, w_out_w, w_out_b):
        import jax, jax.numpy as jnp
        import numpy as np
        NUM_HEADS = 16
        D_MODEL = 128
        D_HEAD = D_MODEL // NUM_HEADS
        TOP_K = 64
        B, S, _ = x.shape
        qkv = x @ w_qkv_w.T + w_qkv_b
        qkv = qkv.reshape(B, S, NUM_HEADS, 3, D_HEAD)
        qkv = qkv.transpose(0, 2, 1, 3, 4)
        q, k, v = (qkv[..., 0, :], qkv[..., 1, :], qkv[..., 2, :])
        scores = jnp.einsum('bhqd,bhkd->bhqk', q, k) / np.sqrt(D_HEAD)
        _, idx = jax.lax.top_k(scores, TOP_K)
        knn_mask = jnp.zeros(scores.shape, dtype=bool).at[jnp.arange(B)[:, None, None, None], jnp.arange(NUM_HEADS)[None, :, None, None], jnp.arange(S)[None, None, :, None], idx].set(True)
        logits = jnp.where(knn_mask, scores, -jnp.inf)
        attn_w = jax.nn.softmax(logits, axis=-1)
        attn = jnp.einsum('bhqk,bhkd->bhqd', attn_w, v)
        attn = attn.transpose(0, 2, 1, 3).reshape(B, S, D_MODEL)
        return x + attn @ w_out_w.T + w_out_b

    def _L1_xattn_ref(q, k, v, wqg, bqg, wkg, bkg, wvg, bvg, wql, bql, wkl, bkl, wvl, bvl, wp, bp):
        import jax, jax.numpy as jnp
        import numpy as np
        N_HEADS = 4
        IN_FEATURES = 128

        def _channel_attention(qm, km, vm, scale):
            b, n, c = qm.shape
            d = c // N_HEADS
            qh = qm.reshape(b, n, N_HEADS, d).transpose(0, 2, 3, 1)
            kh = km.reshape(b, n, N_HEADS, d).transpose(0, 2, 3, 1)
            vh = vm.reshape(b, n, N_HEADS, d).transpose(0, 2, 3, 1)
            scores = jnp.einsum('bhdn,bhen->bhde', qh, kh) * scale
            attn = jax.nn.softmax(scores, axis=-1)
            out = jnp.einsum('bhde,bhen->bhdn', attn, vh)
            return out.transpose(0, 3, 1, 2).reshape(b, n, c)
        scale = IN_FEATURES ** (-0.5)
        att_global = _channel_attention(q * wqg + bqg, k * wkg + bkg, v * wvg + bvg, scale)
        att_local = _channel_attention(q * wql + bql, k * wkl + bkl, v * wvl + bvl, scale)
        att = att_global + att_local
        return 2.0 * att * wp + bp

    def _L1_ffn_ref(hidden_states, Wg, Wu, Wd):
        import jax, jax.numpy as jnp
        import numpy as np
        NUM_EXPERTS = 8
        HIDDEN = 128
        FFN = 512
        BATCH = 2
        SEQ = 256
        B, S, H = hidden_states.shape
        x = hidden_states.reshape(-1, H)

        def expert_step(acc, w):
            wg, wu, wd = w
            h = jax.nn.silu(x @ wg) * (x @ wu)
            return (acc + h @ wd, None)
        acc, _ = jax.lax.scan(expert_step, jnp.zeros_like(x), (Wg, Wu, Wd))
        return acc.reshape(B, S, H)
    x = x + _L0_attn_ref(_layernorm(x, axis=-1), L0_attn_Wq, L0_attn_bq, L0_attn_Wk, L0_attn_bk, L0_attn_Wv, L0_attn_bv, L0_attn_Wo, L0_attn_bo, L0_attn_W1, L0_attn_b1, L0_attn_W2, L0_attn_b2, L0_attn_ln1_s, L0_attn_ln1_b, L0_attn_ln2_s, L0_attn_ln2_b, L0_attn_lnf_s, L0_attn_lnf_b)
    x = x + _L0_xattn_ref(_layernorm(x, axis=-1), ctx_1024, ctx_1024, mask_1x1xSxS2_ik0, L0_xattn_Wq, L0_xattn_bq, L0_xattn_Wk, L0_xattn_bk, L0_xattn_Wv, L0_xattn_bv, L0_xattn_Wo, L0_xattn_bo)
    x = x + _L0_ffn_ref(_layernorm(x, axis=-1), L0_ffn_w1, L0_ffn_conv_w, L0_ffn_conv_b, L0_ffn_w2)
    x = x + _L1_attn_ref(_layernorm(x, axis=-1), L1_attn_w_qkv_w, L1_attn_w_qkv_b, L1_attn_w_out_w, L1_attn_w_out_b)
    x = x + _L1_xattn_ref(_layernorm(x, axis=-1), ctx_1024, ctx_1024, L1_xattn_wqg, L1_xattn_bqg, L1_xattn_wkg, L1_xattn_bkg, L1_xattn_wvg, L1_xattn_bvg, L1_xattn_wql, L1_xattn_bql, L1_xattn_wkl, L1_xattn_bkl, L1_xattn_wvl, L1_xattn_bvl, L1_xattn_wp, L1_xattn_bp)
    x = x + _L1_ffn_ref(_layernorm(x, axis=-1), L1_ffn_Wg, L1_ffn_Wu, L1_ffn_Wd)
    return x

_drawn_inputs = setup_inputs


def setup_inputs(seed=0):
    import zlib

    import numpy as np

    out = dict(_drawn_inputs(seed))
    spreads = {'L0_attn_bq': (0.0, 0.8),
     'L0_attn_bk': (0.0, 0.8),
     'L0_attn_bv': (0.0, 0.8),
     'L0_attn_bo': (0.0, 0.563),
     'L0_attn_b1': (0.0, 0.8),
     'L0_attn_b2': (0.0, 0.548),
     'L0_attn_ln1_s': (1.0, 0.6),
     'L0_attn_ln1_b': (0.0, 0.8),
     'L0_attn_ln2_s': (1.0, 0.6),
     'L0_attn_ln2_b': (0.0, 0.8),
     'L0_attn_lnf_s': (1.0, 0.2),
     'L0_attn_lnf_b': (0.0, 0.1),
     'L0_xattn_bq': (0.0, 0.1),
     'L0_xattn_bk': (0.0, 0.1),
     'L0_xattn_bv': (0.0, 0.1),
     'L0_xattn_bo': (0.0, 0.1),
     'L1_attn_w_qkv_b': (0.0, 0.1),
     'L1_attn_w_out_b': (0.0, 0.1)}
    factors = {'L0_attn_Wq': 8.0,
     'L0_attn_Wk': 8.0,
     'L0_attn_Wv': 8.0,
     'L0_attn_Wo': 8.0,
     'L0_attn_W1': 8.0,
     'L0_attn_W2': 7.079}
    for name, (base, spread) in spreads.items():
        noise = np.random.default_rng([zlib.crc32(name.encode()), seed]).standard_normal(out[name].shape)
        drawn = base * np.exp(spread * noise) if base else spread * noise
        out[name] = jnp.asarray(drawn.astype(out[name].dtype))
    for name, factor in factors.items():
        out[name] = (out[name] * factor).astype(out[name].dtype)
    return out
```

```python
from contextlib import ExitStack

import numpy as np

import concourse.bass as bass
from concourse import mybir

F32 = mybir.dt.float32
BF16 = mybir.dt.bfloat16
I32 = mybir.dt.int32
ALU = mybir.AluOpType
ACT = mybir.ActivationFunctionType
AX = mybir.AxisListType

P = 128
NSEQ = 16
SLOTS = 2
G = 4
HALVES = NSEQ // (SLOTS * G)
W = G * P
L = 4
H, DH = 16, 8
FH = 512
CH = FH // P
EH, ED = 4, 32
NEXP = 8
TOPK = 64
ROUNDS = TOPK // 8
EPS = 1e-5
EPS_ATTN = 1e-6
RSQRT_DH = float(1.0 / np.sqrt(np.float32(DH)))
MAGIC = 12582912.0
NEG = -1e9 * float(np.sqrt(DH))
TAKEN = -3.0e38
FAR = float(2 ** 100)
NEAR = 16
TSTEPS = 8
VA = DH + 2

LN_IN, LN_A, LN_F, LN_B, LN_C, LN_D, LN_E, LN_M = 0, 1, 2 * L + 1, 2 * L + 2, 2 * L + 3, 2 * L + 4, 2 * L + 5, 2 * L + 6
NLN = 2 * L + 7
TR_A, TR_B, TR_D, TR_M = 0, 2 * L, 2 * L + 1, 2 * L + 2
NTR = 2 * L + 3
NB = SLOTS * G


def decoder(nc, x, ctx, mask, aw, acolA, acolB, arow, w2a, bw, bcol, brow, cw, cconv, dw, dcol, drow,
            erow, ecol, mg, mu, md, ident_d, const_d, pos_d, out):
    stack = ExitStack()
    with stack:
        def sb(name, shape, dt=F32):
            return stack.enter_context(nc.sbuf_tensor(name, shape, dt))

        def sem(name):
            return stack.enter_context(nc.semaphore(name))

        def sems(name):
            return [sem(f"{name}{s}") for s in range(SLOTS)]

        def sbs(name, shape, dt=F32):
            return [sb(f"{name}{s}", shape, dt) for s in range(SLOTS)]

        psum = stack.enter_context(nc.psum_tensor("psum", [P, 8, 512], F32))

        def bank(k, n=1):
            return psum[:, k:k + n, :].rearrange("p a c -> p (a c)")

        def bank4(k):
            return psum[:, k, :].rearrange("p (b c) -> p b c", b=G)

        ident = sb("ident", [P, P])
        identb = sb("identb", [P, P], BF16)
        ones = sb("ones", [P, P])
        consts = sb("consts", [P, P + H + 4 + 4 + NEAR])
        same_head = consts[:, 0:P]
        head_of = consts[:, P:P + H]
        head_in_quad = consts[:, P + H:P + H + 4]
        quad_of = consts[:, P + H + 4:P + H + 8]
        half_count = consts[:, P + H + 8:P + H + 8 + NEAR]
        pos = sb("pos", [P, P])
        neg_half = sb("neg_half", [P, G])
        zeros = sb("zeros", [P, P])
        maskt = sb("maskt", [P, P], I32)

        wqkv = sb("wqkv", [P, 3 * P])
        wo = sb("wo", [P, P])
        w1 = sb("w1", [P, FH])
        w2 = sb("w2", [P, CH, P])
        colA = sb("colA", [P, 3])
        colB = sb("colB", [P, 2 + CH])
        rowkv = sb("rowkv", [P, 2 * P])
        rowo = sb("rowo", [P, P])
        row2 = sb("row2", [P, P])
        rowf = sb("rowf", [P, 2 * P])
        watt = [sb(f"watt{i}", [P, 4 * P]) for i in range(2)]
        catt = [sb(f"catt{i}", [P, 2]) for i in range(2)]
        ratt = [sb(f"ratt{i}", [P, 2 * P]) for i in range(2)]
        wcq = sb("wcq", [P, 2, FH], BF16)
        conv = sb("conv", [P, CH, 4])
        wsum = sb("wsum", [P, 2])
        wscale = sb("wscale", [P, 2])
        wrs = sb("wrs", [P, 2])
        rowe = sb("rowe", [P, 10, P])
        cole = sb("cole", [P, 4])
        wg = [sb(f"wg{k}", [P, FH]) for k in range(2)]
        wu = [sb(f"wu{k}", [P, FH]) for k in range(2)]
        wd = [sb(f"wd{k}", [P, CH, P]) for k in range(2)]

        xin = sbs("xin", [P, G, P])
        xs = sbs("xs", [P, G, P])
        xb = sbs("xb", [P, G, P])
        h = sbs("h", [P, G, P])
        hT = sbs("hT", [P, W])
        stats = sbs("stats", [P, G, 6])
        mv = sbs("mv", [P, G, 2])
        veps = sbs("veps", [P, G])
        rstd = sbs("rstd", [P, G])
        ctxt = sbs("ctxt", [P, G, P])
        ctxT = sbs("ctxT", [P, W])
        big = sbs("big", [P, CH, W])
        qT = sbs("qT", [P, W])
        kT = sbs("kT", [P, W])
        qe = sbs("qe", [P, W])
        kk = sbs("kk", [P, G, P])
        ke = sbs("ke", [P, G, P])
        kp = [t[:, 0, :].rearrange("p (b c) -> p b c", b=G) for t in big]
        vv = sbs("vv", [P, G, P + 2])
        kvs = sbs("kvs", [P, G, P + H])
        den = sbs("den", [P, G, H])
        at = sbs("at", [P, G, P])
        atT = hT
        vaug = sbs("vaug", [P, G, H, VA])
        hqb = [qe[s][:, 0:W // 2].bitcast(BF16).rearrange("p (b c) -> p b c", b=G) for s in range(SLOTS)]
        hqT = [qe[s][:, W // 2:W].bitcast(BF16) for s in range(SLOTS)]
        amax = sbs("amax", [P, G])
        asc = sbs("asc", [P, G])
        deq = sbs("deq", [P, G])
        rsb = [t[:, :, :].rearrange("p b c -> p (b c)") for t in ke]
        cbuf = sbs("cbuf", [P, G, P + 2])
        yT = kk
        kblk = [sb(f"kblk{i}", [P, 4, P]) for i in range(2)]
        S = [sb(f"S{i}", [P, H, P]) for i in range(3)]
        keep = sb("keep", [P, H, P], BF16)
        Wk = [sb(f"Wk{i}", [P, H, P]) for i in range(2)]
        far = [sb(f"far{i}", [P, H, P], BF16) for i in range(2)]
        wc_raw = far[0][:, :, :].rearrange("p h k -> p (h k)").bitcast(F32).rearrange("p (a c) -> p a c", a=2)
        cnt, dist, above, ngr, fmul, fadd, okd, okh, theta = ([sb(f"{n}{i}", [P, H]) for i in range(2)] for n in (
            "cnt", "dist", "above", "ngr", "fmul", "fadd", "okd", "okh", "theta"))
        near = sb("near", [P, H, NEAR])
        hit = [sb(f"hit{i}", [P, H, NEAR]) for i in range(2)]
        same = sb("same", [P, H, NEAR])
        picked = sb("picked", [P, H])
        okq = [sb(f"okq{i}", [P, 4]) for i in range(2)]
        bad = [sb(f"bad{i}", [1, 5], I32) for i in range(2)]
        settled_f = [sb(f"settled_f{i}", [1, 1]) for i in range(2)]
        ksum = sbs("ksum", [P, G])
        kmean = sbs("kmean", [P, G, H])
        tmean = sbs("tmean", [P, G, H])
        E = [sb(f"E{i}", [P, H, P]) for i in range(2)]
        PT = [t[:, :, :].rearrange("p c t -> p (c t)").rearrange("p (h k) -> p h k", h=H) for t in big]
        q2b = [t[:, :, :].rearrange("p h k -> p (h k)")[:, 0:G * FH // 2].bitcast(BF16).rearrange("p (b c) -> p b c", b=G) for t in E]
        q2T = [t[:, :, :].rearrange("p h k -> p (h k)")[:, 0:G * FH // 2].bitcast(BF16).rearrange("p (c t) -> p c t", c=CH) for t in PT]
        smax = [sb(f"smax{i}", [P, H]) for i in range(2)]
        zden = [sb(f"zden{i}", [P, H]) for i in range(2)]
        se = sbs("se", [P, 2 * G, ED])
        sm = sbs("sm", [P, 2 * G])
        seT = sbs("seT", [P, 2 * G, ED])
        ablk = [Wk[0][:, 2 * G * s:2 * G * (s + 1), :] for s in range(SLOTS)]
        sg = qe

        consts_in, attw_in, cw_in, ew_in = sem("consts_in"), sem("attw_in"), sem("cw_in"), sem("ew_in")
        preset = sem("preset")
        x_in, ctx_in, xin_used, ctx_used = sems("x_in"), sems("ctx_in"), sems("xin_used"), sems("ctx_used")
        x_upd, ln_stats, ln_var, ln_veps, ln_rstd, ln_h = (sem(n) for n in ("x_upd", "ln_stats", "ln_var", "ln_veps", "ln_rstd", "ln_h"))
        hT_mm, hT_done = sem("hT_mm"), sem("hT_done")
        wqkv_in, wo_in, w1_in, w2_in, rowf_in = sem("wqkv_in"), sem("wo_in"), sem("w1_in"), sem("w2_in"), sem("rowf_in")
        q_mm, kv_mm, kvs_mm, lin_mm, atT_mm, wo_mm, w1_mm, w2_mm = (sem(n) for n in ("q_mm", "kv_mm", "kvs_mm", "lin_mm", "atT_mm", "wo_mm", "w1_mm", "w2_mm"))
        q_exp, q_relu, q_pos, k_raw, v_raw, k_exp, k_relu, k_pos = (sem(n) for n in ("q_exp", "q_relu", "q_pos", "k_raw", "v_raw", "k_exp", "k_relu", "k_pos"))
        kv_sum, den_eps, den_inv, lin_done, atT_done, xbo_done, xb2_done, hid_done = (sem(n) for n in ("kv_sum", "den_eps", "den_inv", "lin_done", "atT_done", "xbo_done", "xb2_done", "hid_done"))
        f_scaled = sems("f_scaled")
        ctxT_mm, ctxT_done = sem("ctxT_mm"), sem("ctxT_done")
        pq_mm, pk_mm, pv_mm, pq_done, pk_done, pv_done = (sem(n) for n in ("pq_mm", "pk_mm", "pv_mm", "pq_done", "pk_done", "pv_done"))
        xba_done = sems("xba_done")
        kblk_done, s_mm, s_out, m_done, sub_done, exp_done, prob_done = (sem(n) for n in ("kblk_done", "s_mm", "s_out", "m_done", "sub_done", "exp_done", "prob_done"))
        pt_mm, pt_done, o_mm, z_done, o_done = (sem(n) for n in ("pt_mm", "pt_done", "o_mm", "z_done", "o_done"))
        ksum_done, kmean_done, tmean_mm, tmean_done = (sem(n) for n in ("ksum_done", "kmean_done", "tmean_mm", "tmean_done"))
        t_side, far_done, z_mul, z_ready, keep_done, t_step, ok_done, bad_mm, bad_done = (sem(n) for n in ("t_side", "far_done", "z_mul", "z_ready", "keep_done", "t_step", "ok_done", "bad_mm", "bad_done"))
        oT_mm, oT_done, ao_mm = sem("oT_mm"), sem("oT_done"), sem("ao_mm")
        wq_sem = sem("wq_step")
        wsum_mm, wq_done = sem("wsum_mm"), sem("wq_done")
        c_step = sems("c_step")
        c_q1, c_q1T_mm, c_q1T, c_diag, c_rs_mm, c_rs, c_f1_mm, c_deq, c_tap1, c_conv, c_yT_mm, c_silu = (sem(n) for n in (
            "c_q1", "c_q1T_mm", "c_q1T", "c_diag", "c_rs_mm", "c_rs", "c_f1_mm", "c_deq", "c_tap1", "c_conv", "c_yT_mm", "c_silu"))
        f_conv, s_preset = sem("f_conv"), sem("s_preset")
        c_q2, c_q2T_mm, c_q2T, c_f2_mm = sem("c_q2"), sem("c_q2T_mm"), sem("c_q2T"), sem("c_f2_mm")
        e_mul, e_qk, e_v, e_step = sems("e_mul"), sems("e_qk"), sems("e_v"), sems("e_step")
        e_s_mm, e_sub, e_exp, e_blk, e_o_mm, e_out, e_xb = (sem(n) for n in ("e_s_mm", "e_sub", "e_exp", "e_blk", "e_o_mm", "e_out", "e_xb"))
        wexp_in = [sem("wexp0_in"), sem("wexp1_in")]
        gu_mm, silu_done, hu_done, d_mm, y_mm, y_copy, yT_mm = sem("gu_mm"), sem("silu_done"), sem("hu_done"), sem("d_mm"), sem("y_mm"), sem("y_copy"), sem("yT_mm")
        stored = sem("stored")
        met_pool, met_dve, met_sp = sem("met_pool"), sem("met_dve"), sem("met_sp")

        def nth(s, n):
            return n * SLOTS + (s - (SLOTS - 1))

        def met(eng):
            eng.sem_inc({nc.gpsimd: met_pool, nc.vector: met_dve, nc.sync: met_sp}[eng], 1)

        block = stack.enter_context(nc.Block())
        SL = range(SLOTS)
        xv = x.rearrange("b t d -> t b d")
        cv = ctx.rearrange("b t d -> t b d")
        ov = out.rearrange("b t d -> t b d")

        @block.sync
        def _(sp):
            for dst, src in ((ident[:, :], ident_d), (consts[:, :], const_d), (pos[:, :], pos_d), (maskt[:, :], mask)):
                sp.dma_start(dst, src).then_inc(consts_in, 16)
            sp.dma_start(rowf[:, :], arow[L:L + 1, 0:2 * P].to_broadcast([P, 2 * P])).then_inc(rowf_in, 16)

            def load_x(s, first):
                sp.dma_start(xin[s][:, :, :], xv[:, bass.ds(first, G), :]).then_inc(x_in[s], 16)

            def load_ctx(s, first):
                sp.dma_start(ctxt[s][:, :, :], cv[:, bass.ds(first, G), :]).then_inc(ctx_in[s], 16)

            def layer(t, l):
                return t[bass.ds(l, 1)].rearrange("o p c -> (o p) c")

            def row(l, a, b):
                return arow[bass.ds(l, 1), a * P:b * P].to_broadcast([P, (b - a) * P])

            def load_qkv(l):
                sp.dma_start(wqkv[:, :], layer(aw, l)[:, 0:3 * P]).then_inc(wqkv_in, 16)
                sp.dma_start(colA[:, :], layer(acolA, l)).then_inc(wqkv_in, 16)
                sp.dma_start(rowkv[:, :], row(l, 0, 2)).then_inc(wqkv_in, 16)

            def load_out(l):
                sp.dma_start(wo[:, :], layer(aw, l)[:, 3 * P:4 * P]).then_inc(wo_in, 16)
                sp.dma_start(rowo[:, :], row(l, 2, 3)).then_inc(wo_in, 16)

            def load_up(l):
                sp.dma_start(w1[:, :], layer(aw, l)[:, 4 * P:8 * P]).then_inc(w1_in, 16)
                sp.dma_start(colB[:, :], layer(acolB, l)).then_inc(w1_in, 16)

            def load_down(l):
                sp.dma_start(w2[:, :, :].rearrange("p a c -> p (a c)"), layer(w2a, l)).then_inc(w2_in, 16)
                sp.dma_start(row2[:, :], row(l, 3, 4)).then_inc(w2_in, 16)

            def load_expert(k, e):
                sp.dma_start(wg[k][:, :], layer(mg, e)).then_inc(wexp_in[k], 16)
                sp.dma_start(wu[k][:, :], layer(mu, e)).then_inc(wexp_in[k], 16)
                sp.dma_start(wd[k][:, :, :].rearrange("p a c -> p (a c)"), layer(md, e)).then_inc(wexp_in[k], 16)

            for s in SL:
                load_x(s, s * G)
            for load in (load_qkv, load_out, load_up, load_down):
                load(0)
            for s in SL:
                load_ctx(s, s * G)
            for k in range(2):
                load_expert(k, k)
            with sp.Fori(0, HALVES) as hf:
                after = [sp.snap(((HALVES - 1) - hf) * NB + s * G) for s in SL]
                with sp.Fori(0, L) as l:
                    i = hf * L + l
                    nl = sp.snap((l + 1) % L)
                    sp.wait_ge(lin_mm, i * 2 + 2)
                    load_qkv(nl)
                    sp.wait_ge(w1_mm, i * (2 * CH) + 2 * CH)
                    load_out(nl)
                    sp.wait_ge(hid_done, i * (2 * CH) + 2 * CH)
                    load_up(nl)
                    sp.wait_ge(w2_mm, i * 2 + 2)
                    sp.wait_ge(xb2_done, i * 2 + 2)
                    load_down(nl)
                for s in SL:
                    sp.wait_ge(xin_used[s], hf + 1)
                    met(sp)
                    load_x(s, after[s])
                for s in SL:
                    sp.wait_ge(ctx_used[s], hf + 1)
                    load_ctx(s, after[s])
                with sp.Fori(0, NEXP // 2) as p:
                    n = hf * (NEXP // 2) + p
                    ne = [sp.snap((p * 2 + (k + 2)) % NEXP) for k in range(2)]
                    for k in range(2):
                        sp.wait_ge(d_mm, n * 2 + (k + 1))
                        load_expert(k, ne[k])
                for s in SL:
                    sp.wait_ge(x_upd, nth(s, hf * NLN + NLN))
                    sp.dma_start(ov[:, bass.ds(hf * NB + s * G, G), :], xs[s][:, :, :]).then_inc(stored, 16)
            sp.wait_ge(stored, HALVES * 16 * SLOTS)

        @block.gpsimd
        def _(pool):
            for i in range(2):
                pool.dma_start(watt[i][:, :], (bw, dw)[i]).then_inc(attw_in, 16)
                pool.dma_start(catt[i][:, :], (bcol, dcol)[i]).then_inc(attw_in, 16)
                pool.dma_start(ratt[i][:, :], (brow, drow)[i].to_broadcast([P, 2 * P])).then_inc(attw_in, 16)
            pool.dma_start(wc_raw[:, :, :].rearrange("p a c -> p (a c)"), cw).then_inc(cw_in, 16)
            pool.dma_start(conv[:, :, :].rearrange("p a c -> p (a c)"), cconv).then_inc(cw_in, 16)
            pool.dma_start(rowe[:, :, :].rearrange("p a c -> p (a c)"), erow.to_broadcast([P, 10 * P])).then_inc(ew_in, 16)
            pool.dma_start(cole[:, :], ecol).then_inc(ew_in, 16)
            pool.memset(neg_half[:, :], -0.5)
            pool.memset(ones[:, :], 1.0)
            for s in SL:
                pool.memset(vv[s][:, :, P:P + 2], 1.0)
                pool.memset(vaug[s][:, :, :, DH:VA], 1.0)
                pool.memset(cbuf[s][:, :, 0:1], 0.0)
                pool.memset(cbuf[s][:, :, P + 1:P + 2], 0.0)
            pool.memset(zeros[:, :], 0.0).then_inc(preset, 1)
            pool.wait_ge(preset, 1)
            pool.wait_ge(consts_in, 64)

            def ln_rsqrt(s, n):
                pool.wait_ge(ln_var, nth(s, n + 1))
                met(pool)
                pool.tensor_scalar(veps[s][:, :], mv[s][:, :, 1], EPS, None, ALU.add).then_inc(ln_veps, 1)
                pool.wait_ge(ln_veps, nth(s, n + 1))
                pool.tensor_tensor(rstd[s][:, :], veps[s][:, :], neg_half[:, :], ALU.pow).then_inc(ln_rstd, 1)

            def bc(row):
                return row.unsqueeze(1).to_broadcast([P, G, P])

            def core(off, hf, att):
                def spread(b):
                    s, c = b // G, b % G
                    if c == 0:
                        pool.wait_ge(pk_done, nth(s, hf * 2 + att + 1))
                    if b >= 2:
                        pool.wait_ge(s_mm, hf * (2 * NB) + (off + b - 1))
                    pool.tensor_tensor(kblk[b % 2][:, :, :],
                                       kT[s][:, c * P:(c + 1) * P].unsqueeze(1).to_broadcast([P, 4, P]),
                                       head_in_quad.unsqueeze(2).to_broadcast([P, 4, P]), ALU.mult).then_inc(kblk_done, 1)

                def candidates(b):
                    t = b % 2
                    n = hf * NB + b
                    pool.wait_ge(t_side, (hf * NB + b) * 4 + 3)
                    if b >= 2:
                        pool.wait_ge(prob_done, n - 1)
                    pool.tensor_tensor(Wk[t][:, :, :], S[b % 3][:, :, :], ngr[t][:, :].unsqueeze(2).to_broadcast([P, H, P]), ALU.mult).then_inc(z_mul, 1)
                    pool.wait_ge(z_mul, n + 1)
                    pool.wait_ge(far_done, n + 1)
                    pool.tensor_tensor(Wk[t][:, :, :], Wk[t][:, :, :], far[t][:, :, :], ALU.subtract).then_inc(z_ready, 1)

                for b in range(2):
                    spread(b)
                if att == 1:
                    candidates(0)
                for b in range(NB + att):
                    if b + 2 < NB and att == 1:
                        spread(b + 2)
                    if b < NB:
                        pool.wait_ge(m_done, hf * (2 * NB) + (off + b + 1))
                        if b >= 2:
                            pool.wait_ge(pt_mm, hf * (8 * NB) + 4 * (off + b - 1))
                        pool.tensor_tensor(E[b % 2][:, :, :], S[b % 3][:, :, :],
                                           smax[b % 2][:, :].unsqueeze(2).to_broadcast([P, H, P]), ALU.subtract).then_inc(sub_done, 1)
                    if b + 2 < NB and att == 0:
                        spread(b + 2)
                    if b >= 1 and att == 1:
                        pool.wait_ge(keep_done, hf * NB + b)
                        pool.wait_ge(exp_done, hf * (2 * NB) + (NB + b))
                        pool.tensor_tensor(E[(b - 1) % 2][:, :, :], E[(b - 1) % 2][:, :, :], keep[:, :, :], ALU.mult).then_inc(prob_done, 1)
                    if b + 1 < NB and att == 1:
                        candidates(b + 1)

            with pool.Fori(0, HALVES) as hf:
                n0 = hf * NLN
                for s in SL:
                    ln_rsqrt(s, n0 + LN_IN)
                with pool.Fori(0, L) as l:
                    i = hf * L + l
                    for s in SL:
                        ln_rsqrt(s, n0 + l * 2 + LN_A)
                    for s in SL:
                        pool.wait_ge(k_raw, nth(s, i + 1))
                        met(pool)
                        pool.tensor_scalar(kp[s][:, :, :], kk[s][:, :, :], 0.0, None, ALU.max).then_inc(k_relu, 1)
                    pool.wait_ge(wo_in, i * 32 + 32)
                    for s in SL:
                        pool.tensor_tensor(xb[s][:, :, :], xs[s][:, :, :], bc(rowo[:, :]), ALU.add).then_inc(xbo_done, 1)
                    for s in SL:
                        ln_rsqrt(s, n0 + l * 2 + (LN_A + 1))
                    pool.wait_ge(w2_in, i * 32 + 32)
                    for s in SL:
                        pool.tensor_tensor(xb[s][:, :, :], xs[s][:, :, :], bc(row2[:, :]), ALU.add).then_inc(xb2_done, 1)
                for s in SL:
                    ln_rsqrt(s, n0 + LN_F)
                for s in SL:
                    ln_rsqrt(s, n0 + LN_B)
                    if s == 0:
                        pool.wait_ge(attw_in, 16 * 6)
                    pool.tensor_tensor(xb[s][:, :, :], xs[s][:, :, :], bc(ratt[0][:, P:2 * P]), ALU.add).then_inc(xba_done[s], 1)
                core(0, hf, 0)
                for s in SL:
                    ln_rsqrt(s, n0 + LN_C)
                for s in SL:
                    ln_rsqrt(s, n0 + LN_D)
                    pool.tensor_tensor(xb[s][:, :, :], xs[s][:, :, :], bc(ratt[1][:, P:2 * P]), ALU.add).then_inc(xba_done[s], 1)
                    pool.wait_ge(ln_h, nth(s, n0 + (LN_D + 1)))
                    pool.wait_ge(xba_done[s], hf * 3 + 2)
                    pool.tensor_tensor(xb[s][:, :, :], xb[s][:, :, :], h[s][:, :, :], ALU.add).then_inc(xba_done[s], 1)
                core(NB, hf, 1)
                pool.wait_ge(ew_in, 32)
                for s in SL:
                    ln_rsqrt(s, n0 + LN_E)
                    pool.tensor_tensor(xb[s][:, :, :], xs[s][:, :, :], bc(rowe[:, 9, :]), ALU.add).then_inc(e_xb, 1)
                for s in SL:
                    for j in (2, 3, 0, 1):
                        src = h[s] if j < 2 else ctxt[s]
                        if j == 0:
                            pool.wait_ge(ln_h, nth(s, n0 + (LN_E + 1)))
                        if j == 2:
                            pool.wait_ge(ctx_in[s], hf * 16 + 16)
                        t = big[s][:, j, :].rearrange("p (b c) -> p b c", b=G)
                        pool.tensor_tensor(t, src[:, :, :], bc(rowe[:, 2 * j, :]), ALU.mult).then_inc(e_mul[s], 1)
                    for k, j in enumerate((2, 3, 0, 1)):
                        t = big[s][:, j, :].rearrange("p (b c) -> p b c", b=G)
                        pool.wait_ge(e_mul[s], hf * 4 + k + 1)
                        pool.tensor_tensor(t, t, bc(rowe[:, 2 * j + 1, :]), ALU.add).then_inc(e_qk[s], 1)
                for s in SL:
                    pool.wait_ge(e_step[s], hf * 5 + 5)
                    pool.tensor_tensor(ablk[s][:, :, :].rearrange("p a (q e) -> p a q e", q=EH),
                                       seT[s][:, :, :].unsqueeze(2).to_broadcast([P, 2 * G, EH, ED]),
                                       quad_of.unsqueeze(1).unsqueeze(3).to_broadcast([P, 2 * G, EH, ED]), ALU.mult).then_inc(e_blk, 1)
                for s in SL:
                    ln_rsqrt(s, n0 + LN_M)

        @block.scalar
        def _(act):
            def hT_copy(s, m, k, scale=None, bias=None):
                act.wait_ge(hT_mm, nth(s, m + 1))
                if scale is None:
                    act.copy(hT[s][:, :], bank(k)).then_inc(hT_done, 1)
                else:
                    act.activation(hT[s][:, :], bank(k), ACT.Identity, bias=bias, scale=scale).then_inc(hT_done, 1)

            def copy_probs(off, hf, a):
                for g in range(4):
                    act.wait_ge(pt_mm, hf * (8 * NB) + 4 * (off + a) + g + 1)
                    if g == 0 and a >= 2:
                        act.wait_ge(o_mm, hf * (2 * NB) + (off + a - 1))
                    act.copy(PT[a % 2][:, 4 * g:4 * g + 4, :].rearrange("p h k -> p (h k)"), bank(4 + g % 2)).then_inc(pt_done, 1)

            def exponentials(off, hf, a):
                act.wait_ge(sub_done, hf * (2 * NB) + (off + a + 1))
                act.activation(E[a % 2][:, :, :], E[a % 2][:, :, :], ACT.Exp, scale=RSQRT_DH).then_inc(exp_done, 1)

            def core_cross(hf):
                for b in range(NB + 2):
                    if 1 <= b <= NB:
                        exponentials(0, hf, b - 1)
                    if b >= 2:
                        copy_probs(0, hf, b - 2)

            def core_topk(hf):
                def scores_out(b):
                    act.wait_ge(s_mm, hf * (2 * NB) + (NB + b + 1))
                    if b >= 3:
                        act.wait_ge(prob_done, hf * NB + (b - 2))
                    act.copy(S[b % 3][:, :, :].rearrange("p h k -> p (h k)"), bank(0, 4)).then_inc(s_out, 1)

                scores_out(0)
                for b in range(NB + 2):
                    if 1 <= b <= NB:
                        exponentials(NB, hf, b - 1)
                    if b >= 2:
                        copy_probs(NB, hf, b - 2)
                    if b < NB:
                        act.wait_ge(t_side, hf * (4 * NB) + 4 * (b + 1))
                        for hd in range(H):
                            ins = act.activation(far[b % 2][:, hd, :], far[b % 2][:, hd, :], ACT.Identity,
                                                 bias=fadd[b % 2][:, hd:hd + 1], scale=fmul[b % 2][:, hd:hd + 1])
                        ins.then_inc(far_done, 1)
                    if b + 1 < NB:
                        scores_out(b + 1)

            act.wait_ge(preset, 1)
            with act.Fori(0, HALVES) as hf:
                with act.Fori(0, L) as l:
                    i = hf * L + l
                    m = hf * NTR + l * 2
                    act.wait_ge(wqkv_in, i * 48 + 48)
                    for s in SL:
                        hT_copy(s, m, 4 * s, colA[:, 0:1], colA[:, 1:2])
                    for s in SL:
                        act.wait_ge(q_mm, nth(s, i + 1))
                        act.activation(qe[s][:, :], bank(4 * s + 1), ACT.Exp, bias=colA[:, 2:3]).then_inc(q_exp, 1)
                        act.wait_ge(k_raw, nth(s, i + 1))
                        act.activation(ke[s][:, :, :], kk[s][:, :, :], ACT.Exp).then_inc(k_exp, 1)
                    for s in SL:
                        act.wait_ge(atT_mm, nth(s, i + 1))
                        act.copy(atT[s][:, :], bank(4 * s)).then_inc(atT_done, 1)
                    act.wait_ge(w1_in, i * 32 + 32)
                    for s in SL:
                        hT_copy(s, m + 1, 4 * s + 1, colB[:, 0:1], colB[:, 1:2])
                    for c in range(CH):
                        for s in SL:
                            act.wait_ge(w1_mm, nth(s, i * CH + c + 1))
                            act.activation(big[s][:, c, :], bank(4 * s + (2, 3, 0, 1)[c]), ACT.Relu, bias=colB[:, 2 + c:3 + c]).then_inc(hid_done, 1)
                act.wait_ge(attw_in, 16 * 6)
                for s in SL:
                    act.wait_ge(ctxT_mm, nth(s, hf + 1))
                    act.copy(ctxT[s][:, :], bank(4 * s + 1)).then_inc(ctxT_done, 1)
                for s in SL:
                    hT_copy(s, hf * NTR + TR_B, 4 * s)
                for s in SL:
                    act.wait_ge(pk_mm, nth(s, hf * 2 + 1))
                    act.activation(kT[s][:, :], bank(4 * s + 2), ACT.Identity, bias=catt[0][:, 1:2]).then_inc(pk_done, 1)
                    act.wait_ge(pq_mm, nth(s, hf * 2 + 1))
                    act.activation(qT[s][:, :], bank(4 * s + 1), ACT.Identity, bias=catt[0][:, 0:1]).then_inc(pq_done, 1)
                core_cross(hf)
                for s in SL:
                    act.wait_ge(oT_mm, nth(s, hf * 2 + 1))
                    act.copy(atT[s][:, :], bank(s)).then_inc(oT_done, 1)
                act.wait_ge(cw_in, 32)
                act.wait_ge(wq_done, 1)
                for s in SL:
                    act.wait_ge(c_q1T_mm, nth(s, hf + 1))
                    act.copy(hqT[s][:, :], bank(4 * s).bitcast(BF16)[:, 0:W]).then_inc(c_q1T, 1)
                    act.wait_ge(c_rs_mm, nth(s, hf + 1))
                    act.activation(rsb[s][:, :], bank(4 * s + 1), ACT.Copy, scale=wscale[:, 0:1]).then_inc(c_rs, 1)
                for c in range(CH):
                    for s in SL:
                        act.wait_ge(c_deq, nth(s, hf * CH + c + 1))
                        if c >= 1:
                            act.wait_ge(c_yT_mm, nth(s, hf * CH + c))
                        act.activation(yT[s][:, :, :], cbuf[s][:, :, 1:P + 1], ACT.Identity, bias=conv[:, c, 3:4], scale=conv[:, c, 1:2]).then_inc(c_tap1, 1)
                    for s in SL:
                        act.wait_ge(c_yT_mm, nth(s, hf * CH + c + 1))
                        act.activation(big[s][:, :, c * P:(c + 1) * P], bank4(4 * s + 3), ACT.Silu).then_inc(c_silu, 1)
                for c in range(CH):
                    for s in SL:
                        act.wait_ge(c_q2T_mm, nth(s, hf * CH + c + 1))
                        act.copy(q2T[s][:, c, :], bank(4 * s + c % 2).bitcast(BF16)[:, 0:W]).then_inc(c_q2T, 1)
                for s in SL:
                    hT_copy(s, hf * NTR + TR_D, 4 * s)
                for s in SL:
                    act.wait_ge(pk_mm, nth(s, hf * 2 + 2))
                    act.activation(kT[s][:, :], bank(4 * s + 2), ACT.Identity, bias=catt[1][:, 1:2]).then_inc(pk_done, 1)
                    act.wait_ge(pq_mm, nth(s, hf * 2 + 2))
                    act.activation(qT[s][:, :], bank(4 * s + 1), ACT.Identity, bias=catt[1][:, 0:1]).then_inc(pq_done, 1)
                for s in SL:
                    act.wait_ge(tmean_mm, nth(s, hf + 1))
                    act.mul(tmean[s][:, :, :].rearrange("p b h -> p (b h)"), bank(4 * s + 1)[:, 0:G * H], 1.0 / P).then_inc(tmean_done, 1)
                core_topk(hf)
                for s in SL:
                    act.wait_ge(oT_mm, nth(s, hf * 2 + 2))
                    act.copy(atT[s][:, :], bank(s)).then_inc(oT_done, 1)
                act.wait_ge(ew_in, 32)
                for s in SL:
                    act.activation(qT[s][:, :], ctxT[s][:, :], ACT.Identity, bias=cole[:, 1:2], scale=cole[:, 0:1]).then_inc(e_v[s], 1)
                    act.activation(kT[s][:, :], ctxT[s][:, :], ACT.Identity, bias=cole[:, 3:4], scale=cole[:, 2:3]).then_inc(e_v[s], 1)
                for s in SL:
                    act.wait_ge(e_sub, nth(s, hf + 1))
                    act.activation(se[s][:, :, :], se[s][:, :, :], ACT.Exp, scale=float(P) ** -0.5).then_inc(e_exp, 1)
                for s in SL:
                    hT_copy(s, hf * NTR + TR_M, 6 + s)
                with act.Fori(0, NEXP // 2) as p:
                    n = (hf * (NEXP // 2) + p) * 16
                    for u in range(16):
                        s = u % 2
                        act.wait_ge(gu_mm, n + u + 1)
                        if u >= 2:
                            act.wait_ge(hu_done, n + u - 1)
                        act.activation(sg[s][:, :], bank(2 + s), ACT.Silu).then_inc(silu_done, 1)
                for s in SL:
                    act.wait_ge(y_mm, nth(s, hf + 1))
                    act.copy(sg[s][:, :], bank(s)).then_inc(y_copy, 1)

        @block.tensor
        def _(pe):
            def transposes(dst, src, eye, last_sem):
                for b in range(G):
                    mm = pe.transpose(dst[:, b * P:(b + 1) * P], src[:, b, :], eye)
                mm.then_inc(last_sem, 1)

            def hT_tr(s, n, k):
                pe.wait_ge(ln_h, nth(s, n + 1))
                transposes(bank(k), h[s], ident[:, :], hT_mm)

            def project(att, hf):
                w = watt[att]
                for s in SL:
                    pe.wait_ge(hT_done, nth(s, hf * NTR + ((TR_B, TR_D)[att] + 1)))
                    kvT = ctxT[s] if att == 0 else hT[s]
                    pe.matmul(bank(4 * s + 2), w[:, P:2 * P], kvT[:, :], start=True, stop=True).then_inc(pk_mm, 1)
                    pe.matmul(bank(4 * s + 1), w[:, 0:P], hT[s][:, :], start=True, stop=True).then_inc(pq_mm, 1)
                    for b in range(G):
                        mm = pe.matmul(bank4(4 * s + 3)[:, b, :], kvT[:, b * P:(b + 1) * P], w[:, 2 * P:3 * P], start=True, stop=True)
                    mm.then_inc(pv_mm, 1)

            def mean_scores(hf):
                for s in SL:
                    pe.wait_ge(pq_done, nth(s, hf * 2 + 2))
                    pe.wait_ge(kmean_done, nth(s, hf + 1))
                    for b in range(G):
                        mm = pe.matmul(bank(4 * s + 1)[:, b * H:(b + 1) * H], qT[s][:, b * P:(b + 1) * P], kmean[s][:, b, :], start=True, stop=True)
                    mm.then_inc(tmean_mm, 1)

            def core(off, hf, att):
                probs = exp_done if att == 0 else prob_done
                nprobs = hf * NB if att == 1 else hf * (2 * NB)
                pe.wait_ge(pv_done, nth(SLOTS - 1, hf * 2 + att + 1))
                pe.wait_ge(pq_done, nth(SLOTS - 1, hf * 2 + att + 1))
                if att == 1:
                    pe.wait_ge(tmean_done, nth(SLOTS - 1, hf + 1))

                def scores(b):
                    s, c = b // G, b % G
                    n = hf * (2 * NB) + (off + b)
                    pe.wait_ge(kblk_done, n + 1)
                    if b >= 1:
                        pe.wait_ge(s_out, n)
                    for q in range(4):
                        mm = pe.matmul(bank(q), qT[s][32 * q:32 * q + 32, c * P:(c + 1) * P],
                                       kblk[b % 2][32 * q:32 * q + 32, :, :].rearrange("p h k -> p (h k)"), start=True, stop=True)
                    mm.then_inc(s_mm, 1)

                def outputs(a):
                    s, c = a // G, a % G
                    n = hf * (2 * NB) + (off + a)
                    pe.wait_ge(probs, nprobs + ((off if att == 0 else 0) + a + 1))
                    for g in range(4):
                        if a >= 1 or g >= 2:
                            pe.wait_ge(pt_done, n * 4 + (g - 1))
                        for j in range(4):
                            mm = pe.transpose(bank(4 + g % 2)[:, j * P:(j + 1) * P], E[a % 2][:, 4 * g + j, :], ident[:, :])
                        mm.then_inc(pt_mm, 1)
                    pe.wait_ge(pt_done, n * 4 + 4)
                    if a >= 2:
                        pe.wait_ge(o_done, n - 1)
                    for hd in range(H):
                        mm = pe.matmul(bank(6 + a % 2)[:, hd * VA:(hd + 1) * VA], PT[a % 2][:, hd, :], vaug[s][:, c, hd, :], start=True, stop=True)
                    mm.then_inc(o_mm, 1)

                def settled_rows(b):
                    pe.wait_ge(ok_done, hf * NB + (b + 1))
                    pe.matmul(bank(6 + b % 2)[:, 200:204], ones[:, :], okq[b % 2][:, :], start=True, stop=True).then_inc(bad_mm, 1)

                scores(0)
                for b in range(NB + 2):
                    if b + 1 < NB and att == 1:
                        scores(b + 1)
                    if b >= 2:
                        outputs(b - 2)
                    if b + 1 < NB and att == 0:
                        scores(b + 1)
                    if att == 1 and 1 <= b <= NB:
                        settled_rows(b - 1)
                for s in SL:
                    pe.wait_ge(o_done, hf * (2 * NB) + (off + G * (s + 1)))
                    transposes(bank(s), at[s], ident[:, :], oT_mm)
                for s in SL:
                    pe.wait_ge(oT_done, nth(s, hf * 2 + att + 1))
                    for b in range(G):
                        mm = pe.matmul(bank4(2 + s)[:, b, :], atT[s][:, b * P:(b + 1) * P], watt[att][:, 3 * P:4 * P], start=True, stop=True)
                    mm.then_inc(ao_mm, 1)

            pe.wait_ge(consts_in, 64)
            pe.wait_ge(preset, 1)
            pe.wait_ge(wq_sem, 2)
            pe.matmul(bank(7)[:, 0:2], ones[:, :], wsum[:, :], start=True, stop=True).then_inc(wsum_mm, 1)
            with pe.Fori(0, HALVES) as hf:
                n0 = hf * NLN
                with pe.Fori(0, L) as l:
                    i = hf * L + l
                    m = hf * NTR + l * 2
                    for s in SL:
                        hT_tr(s, n0 + l * 2 + LN_A, 4 * s)
                    pe.wait_ge(wqkv_in, i * 48 + 48)
                    for s in SL:
                        pe.wait_ge(hT_done, nth(s, m + 1))
                        for b in range(G):
                            mm = pe.matmul(bank(4 * s + 2, 2)[:, b * 2 * P:(b + 1) * 2 * P], hT[s][:, b * P:(b + 1) * P], wqkv[:, P:3 * P], start=True, stop=True)
                        mm.then_inc(kv_mm, 1)
                        pe.matmul(bank(4 * s + 1), wqkv[:, 0:P], hT[s][:, :], start=True, stop=True).then_inc(q_mm, 1)
                    for s in SL:
                        pe.wait_ge(k_pos, nth(s, i + 1))
                        pe.wait_ge(v_raw, nth(s, i + 1))
                        pe.wait_ge(q_pos, nth(s, i + 1))
                        for b in range(G):
                            mm = pe.matmul(bank(4 * s, 2)[:, b * 2 * P:b * 2 * P + P + 2], kp[s][:, b, :], vv[s][:, b, :], start=True, stop=True)
                        mm.then_inc(kvs_mm, 1)
                    for s in SL:
                        pe.wait_ge(kv_sum, nth(s, i + 1))
                        for b in range(G):
                            mm = pe.matmul(bank(4 * s + 2, 2)[:, b * 2 * P:b * 2 * P + P + H], qT[s][:, b * P:(b + 1) * P], kvs[s][:, b, :], start=True, stop=True)
                        mm.then_inc(lin_mm, 1)
                    for s in SL:
                        pe.wait_ge(lin_done, nth(s, i + 1))
                        transposes(bank(4 * s), at[s], ident[:, :], atT_mm)
                    pe.wait_ge(wo_in, i * 32 + 32)
                    for s in SL:
                        pe.wait_ge(atT_done, nth(s, i + 1))
                        for b in range(G):
                            mm = pe.matmul(bank4(4 * s + 2)[:, b, :], atT[s][:, b * P:(b + 1) * P], wo[:, :], start=True, stop=True)
                        mm.then_inc(wo_mm, 1)
                    for s in SL:
                        hT_tr(s, n0 + l * 2 + (LN_A + 1), 4 * s + 1)
                    pe.wait_ge(w1_in, i * 32 + 32)
                    for s in SL:
                        pe.wait_ge(hT_done, nth(s, m + 2))
                    for c in range(CH):
                        for s in SL:
                            pe.matmul(bank(4 * s + (2, 3, 0, 1)[c]), w1[:, c * P:(c + 1) * P], hT[s][:, :], start=True, stop=True).then_inc(w1_mm, 1)
                    pe.wait_ge(w2_in, i * 32 + 32)
                    for s in SL:
                        pe.wait_ge(hid_done, nth(s, i * CH + CH))
                        for b in range(G):
                            for c in range(CH):
                                mm = pe.matmul(bank4(4 * s + 2)[:, b, :], big[s][:, c, b * P:(b + 1) * P], w2[:, c, :], start=(c == 0), stop=(c == CH - 1))
                        mm.then_inc(w2_mm, 1)
                pe.wait_ge(attw_in, 16 * 6)
                for s in SL:
                    pe.wait_ge(ctx_in[s], hf * 16 + 16)
                    transposes(bank(4 * s + 1), ctxt[s], ident[:, :], ctxT_mm)
                for s in SL:
                    hT_tr(s, n0 + LN_B, 4 * s)
                for s in SL:
                    pe.wait_ge(ctxT_done, nth(s, hf + 1))
                project(0, hf)
                core(0, hf, 0)
                pe.wait_ge(wq_done, 1)
                for s in SL:
                    pe.wait_ge(c_q1, nth(s, hf + 1))
                    transposes(bank(4 * s).bitcast(BF16), hqb[s], identb[:, :], c_q1T_mm)
                    pe.wait_ge(c_diag, nth(s, hf + 1))
                    pe.matmul(bank(4 * s + 1), ones[:, :], yT[s][:, :, :].rearrange("p b t -> p (b t)"), start=True, stop=True).then_inc(c_rs_mm, 1)
                for c in range(CH):
                    for s in SL:
                        if c == 0:
                            pe.wait_ge(c_q1T, nth(s, hf + 1))
                        else:
                            pe.wait_ge(c_deq, nth(s, hf * CH + c))
                        pe.matmul(bank(4 * s + 2), wcq[:, 0, c * P:(c + 1) * P], hqT[s][:, :], start=True, stop=True).then_inc(c_f1_mm, 1)
                    for s in SL:
                        pe.wait_ge(c_conv, nth(s, hf * CH + c + 1))
                        if c >= 1:
                            pe.wait_ge(c_silu, nth(s, hf * CH + c))
                        transposes(bank(4 * s + 3), yT[s], ident[:, :], c_yT_mm)
                for c in range(CH):
                    for s in SL:
                        if c == 0:
                            pe.wait_ge(c_q2, nth(s, hf + 1))
                        if c >= 2:
                            pe.wait_ge(c_q2T, nth(s, hf * CH + c - 1))
                        for b in range(G):
                            mm = pe.transpose(bank(4 * s + c % 2).bitcast(BF16)[:, b * P:(b + 1) * P], q2b[s][:, b, c * P:(c + 1) * P], identb[:, :])
                        mm.then_inc(c_q2T_mm, 1)
                for s in SL:
                    pe.wait_ge(c_q2T, nth(s, hf * CH + CH))
                    for b in range(G):
                        for c in range(CH):
                            mm = pe.matmul(bank4(4 * s + 2)[:, b, :], q2T[s][:, c, b * P:(b + 1) * P], wcq[:, 1, c * P:(c + 1) * P], start=(c == 0), stop=(c == CH - 1))
                    mm.then_inc(c_f2_mm, 1)
                for s in SL:
                    hT_tr(s, n0 + LN_D, 4 * s)
                project(1, hf)
                mean_scores(hf)
                core(NB, hf, 1)
                for s in SL:
                    pe.wait_ge(e_qk[s], hf * 4 + 4)
                    for k in range(2):
                        for b in range(G):
                            for q in range(EH):
                                c = b * P + q * ED
                                mm = pe.matmul(bank(4 + s)[q * ED:(q + 1) * ED, (k * G + b) * ED:(k * G + b + 1) * ED],
                                               big[s][:, k, c:c + ED], big[s][:, 2 + k, c:c + ED], start=True, stop=True)
                    mm.then_inc(e_s_mm, 1)
                for s in SL:
                    pe.wait_ge(e_blk, nth(s, hf + 1))
                    pe.wait_ge(e_v[s], hf * 2 + 2)
                    for b in range(G):
                        pe.matmul(bank4(s)[:, b, :], qT[s][:, b * P:(b + 1) * P], ablk[s][:, b, :], start=True, stop=False)
                        mm = pe.matmul(bank4(s)[:, b, :], kT[s][:, b * P:(b + 1) * P], ablk[s][:, G + b, :], start=False, stop=True)
                    mm.then_inc(e_o_mm, 1)
                for s in SL:
                    hT_tr(s, n0 + LN_M, 6 + s)
                for s in SL:
                    pe.wait_ge(hT_done, nth(s, hf * NTR + (TR_M + 1)))
                    pe.matmul(bank(s), zeros[:, :], hT[s][:, :], start=True, stop=False, skip_group_check=True)
                with pe.Fori(0, NEXP // 2) as p:
                    e = hf * (NEXP // 2) + p
                    n = e * 16
                    for u in range(16 + 2):
                        if u < 16:
                            k, c, s = u // 8, u % 8 // 2, u % 2
                            if u % 8 == 0:
                                pe.wait_ge(wexp_in[k], e * 48 + 48)
                            if u >= 2:
                                pe.wait_ge(hu_done, n + u - 1)
                            pe.matmul(bank(2 + s), wg[k][:, c * P:(c + 1) * P], hT[s][:, :], start=True, stop=True)
                            pe.matmul(bank(4 + s), wu[k][:, c * P:(c + 1) * P], hT[s][:, :], start=True, stop=True).then_inc(gu_mm, 1)
                        if u >= 2:
                            v = u - 2
                            k, c, s = v // 8, v % 8 // 2, v % 2
                            if u >= 16:
                                pe.wait_ge(hu_done, n + v + 1)
                            mm = pe.matmul(bank(s), wd[k][:, c, :], big[s][:, c, :], start=False, stop=True, skip_group_check=True)
                            if v % 8 == 7:
                                mm.then_inc(d_mm, 1)
                for s in SL:
                    mm = pe.matmul(bank(s), zeros[:, :], hT[s][:, :], start=False, stop=True, skip_group_check=True)
                    mm.then_inc(y_mm, 1)
                for s in SL:
                    pe.wait_ge(y_copy, nth(s, hf + 1))
                    transposes(bank(2 + s), sg[s][:, :].rearrange("p (b t) -> p b t", b=G), ident[:, :], yT_mm)

        @block.vector
        def _(dve):
            def layer_norm(s, n, src=None):
                src = xs[s] if src is None else src
                for b in range(G):
                    ins = dve.bn_stats(stats[s][:, b, :], src[:, b, :])
                ins.then_inc(ln_stats, 1)
                dve.wait_ge(ln_stats, nth(s, n + 1))
                met(dve)
                for b in range(G):
                    ins = dve.bn_aggr(mv[s][:, b, :], stats[s][:, b, :])
                ins.then_inc(ln_var, 1)

            def normalize(s, n, src=None):
                src = xs[s] if src is None else src
                dve.wait_ge(ln_rstd, nth(s, n + 1))
                for b in range(G):
                    ins = dve.tensor_scalar(h[s][:, b, :], src[:, b, :], mv[s][:, b, 0:1], rstd[s][:, b:b + 1], ALU.subtract, ALU.mult)
                ins.then_inc(ln_h, 1)

            def ln(n):
                for s in SL:
                    dve.wait_ge(x_upd, nth(s, n))
                    layer_norm(s, n)
                for s in SL:
                    normalize(s, n)

            def values(att, hf):
                for s in SL:
                    dve.wait_ge(pv_mm, nth(s, hf * 2 + att + 1))
                    for b in range(G):
                        ins = dve.tensor_tensor(vaug[s][:, b, :, 0:DH], bank4(4 * s + 3)[:, b, :].rearrange("p (h d) -> p h d", h=H),
                                                ratt[att][:, 0:P].rearrange("p (h d) -> p h d", h=H), ALU.add)
                    ins.then_inc(pv_done, 1)

            def head_outputs(off, hf, a):
                n = hf * (2 * NB) + (off + a)
                dve.wait_ge(o_mm, n + 1)
                o = bank(6 + a % 2)[:, 0:H * VA].rearrange("p (h d) -> p h d", h=H)
                dve.reciprocal(zden[a % 2][:, :], o[:, :, DH]).then_inc(z_done, 1)
                dve.wait_ge(z_done, n + 1)
                dve.tensor_tensor(at[a // G][:, a % G, :].rearrange("p (h d) -> p h d", h=H), o[:, :, 0:DH],
                                  zden[a % 2][:, :].unsqueeze(2).to_broadcast([P, H, DH]), ALU.mult).then_inc(o_done, 1)


            def above_mean(hf, b):
                t, s, c = b % 2, b // G, b % G
                k = hf * (4 * NB) + 4 * b
                if c == 0:
                    dve.wait_ge(tmean_done, nth(s, hf + 1))
                dve.wait_ge(s_out, hf * (2 * NB) + (NB + b + 1))
                for hd in range(H):
                    ins = dve.tensor_scalar(far[t][:, hd, :], S[b % 3][:, hd, :], tmean[s][:, c, hd:hd + 1], 0.0, ALU.is_ge, ALU.add,
                                            accum_out=cnt[t][:, hd:hd + 1])
                ins.then_inc(t_side, 1)
                dve.wait_ge(t_side, k + 1)
                dve.tensor_scalar(above[t][:, :], cnt[t][:, :], float(TOPK), None, ALU.is_ge)
                dve.tensor_scalar(okd[t][:, :], cnt[t][:, :], -1.0, TOPK - 0.5, ALU.mult, ALU.add)
                dve.tensor_scalar(dist[t][:, :], cnt[t][:, :], TOPK - 0.5, None, ALU.subtract).then_inc(t_side, 1)
                dve.wait_ge(t_side, k + 2)
                dve.tensor_tensor(dist[t][:, :], dist[t][:, :], okd[t][:, :], ALU.max)
                dve.tensor_scalar(ngr[t][:, :], above[t][:, :], -2.0, 1.0, ALU.mult, ALU.add)
                dve.tensor_scalar(fmul[t][:, :], above[t][:, :], -2.0 * FAR, FAR, ALU.mult, ALU.add)
                dve.tensor_scalar(fadd[t][:, :], above[t][:, :], FAR, None, ALU.mult).then_inc(t_side, 1)
                dve.wait_ge(t_side, k + 3)
                dve.tensor_scalar(okd[t][:, :], dist[t][:, :], NEAR - 1.0, None, ALU.is_le)
                dve.tensor_tensor(hit[t][:, :, :], half_count.unsqueeze(1).to_broadcast([P, H, NEAR]),
                                  dist[t][:, :].unsqueeze(2).to_broadcast([P, H, NEAR]), ALU.is_equal).then_inc(t_side, 1)

            def short_way(hf, b):
                t = b % 2
                k = (hf * NB + b) * TSTEPS
                dve.wait_ge(z_ready, hf * NB + (b + 1))
                met(dve)
                for hd in range(H):
                    ins = dve.max(near[:, hd, 0:8], Wk[t][:, hd, :])
                ins.then_inc(t_step, 1)
                dve.wait_ge(t_step, k + 1)
                met(dve)
                for hd in range(H):
                    ins = dve.match_replace(Wk[t][:, hd, :], near[:, hd, 0:8], Wk[t][:, hd, :], TAKEN)
                ins.then_inc(t_step, 1)
                dve.wait_ge(t_step, k + 2)
                met(dve)
                for hd in range(H):
                    ins = dve.max(near[:, hd, 8:16], Wk[t][:, hd, :])
                ins.then_inc(t_step, 1)
                dve.wait_ge(t_step, k + 3)
                dve.tensor_tensor(same[:, :, :], hit[t][:, :, :], near[:, :, :], ALU.mult).then_inc(t_step, 1)
                dve.wait_ge(t_step, k + 4)
                dve.tensor_reduce(picked[:, :], same[:, :, :], AX.X, ALU.add).then_inc(t_step, 1)
                dve.wait_ge(t_step, k + 5)
                dve.tensor_tensor(theta[t][:, :], picked[:, :], ngr[t][:, :], ALU.mult)
                dve.tensor_tensor(same[:, :, :], near[:, :, :], picked[:, :].unsqueeze(2).to_broadcast([P, H, NEAR]), ALU.is_equal).then_inc(t_step, 1)
                dve.wait_ge(t_step, k + 6)
                dve.tensor_reduce(okh[t][:, :], same[:, :, :], AX.X, ALU.add).then_inc(t_step, 1)
                dve.wait_ge(t_step, k + 7)
                dve.scalar_tensor_tensor(okh[t][:, :], okh[t][:, :], 1.0, okd[t][:, :], ALU.is_equal, ALU.mult).then_inc(t_step, 1)
                dve.wait_ge(t_step, k + 8)
                dve.tensor_reduce(okq[t][:, :], okh[t][:, :].rearrange("p (q j) -> p q j", j=4), AX.X, ALU.add).then_inc(ok_done, 1)

            def long_way(b, q):
                t = b % 2
                heads = range(4 * q, 4 * q + 4)
                dve.drain()
                for r in range(ROUNDS):
                    src = S[b % 3] if r == 0 else Wk[t]
                    for hd in heads:
                        dve.max(near[:, hd, 0:8], src[:, hd, :])
                    dve.drain()
                    for hd in heads:
                        dve.match_replace(Wk[t][:, hd, :], near[:, hd, 0:8], src[:, hd, :], TAKEN)
                    dve.drain()
                for hd in heads:
                    dve.tensor_scalar(keep[:, hd, :], Wk[t][:, hd, :], TAKEN, None, ALU.is_equal)

            def mark_kept(hf, b):
                t = b % 2
                n = hf * NB + b
                if b >= 1:
                    dve.wait_ge(prob_done, n)
                dve.tensor_tensor(keep[:, :, :], S[b % 3][:, :, :], theta[t][:, :].unsqueeze(2).to_broadcast([P, H, P]), ALU.is_ge)
                dve.wait_ge(bad_mm, n + 1)
                dve.tensor_scalar(bad[t][0:1, 0:4], bank(6 + t)[0:1, 200:204], -1.0, float(4 * P), ALU.mult, ALU.add)
                dve.tensor_reduce(settled_f[t][0:1, 0:1], bank(6 + t)[0:1, 200:204], AX.X, ALU.add).then_inc(bad_done, 1)
                dve.wait_ge(bad_done, n * 2 + 1)
                dve.tensor_scalar(bad[t][0:1, 4:5], settled_f[t][0:1, 0:1], 1.0, None, ALU.mult).then_inc(bad_done, 1)
                dve.wait_ge(bad_done, n * 2 + 2)
                met(dve)
                settled = dve.value_load(bad[t][0:1, 4:5], min_val=0, max_val=H * P)
                with dve.If(settled < H * P):
                    for q in range(4):
                        unsettled = dve.value_load(bad[t][0:1, q:q + 1], min_val=0, max_val=4 * P)
                        with dve.If(unsettled > 0):
                            long_way(b, q)
                dve.drain()
                dve.sem_inc(keep_done, 1)

            def residual(att, hf, n):
                for s in SL:
                    dve.wait_ge(ao_mm, nth(s, hf * 2 + att + 1))
                    dve.wait_ge(xba_done[s], hf * 3 + (1, 3)[att])
                    dve.tensor_tensor(xs[s][:, :, :], bank4(2 + s), xb[s][:, :, :], ALU.add).then_inc(x_upd, 1)

            def act_scales(s, n):
                dve.wait_ge(c_step[s], n + 1)
                dve.tensor_scalar(amax[s][:, :], amax[s][:, :], 1e-5, None, ALU.max).then_inc(c_step[s], 1)
                dve.wait_ge(c_step[s], n + 2)
                dve.reciprocal(asc[s][:, :], amax[s][:, :]).then_inc(c_step[s], 1)
                dve.wait_ge(c_step[s], n + 3)
                dve.tensor_scalar(asc[s][:, :], asc[s][:, :], 127.0, None, ALU.mult).then_inc(c_step[s], 1)

            dve.wait_ge(consts_in, 64)
            dve.wait_ge(preset, 1)
            dve.tensor_copy(identb[:, :], ident[:, :])
            dve.wait_ge(cw_in, 32)
            for k in range(2):
                dve.tensor_reduce(wsum[:, k:k + 1], wc_raw[:, k, :], AX.X, ALU.add, apply_absolute_value=True).then_inc(wq_sem, 1)
            dve.wait_ge(wsum_mm, 1)
            dve.tensor_scalar(wscale[:, :], bank(7)[:, 0:2], 1.0 / (P * FH), 1e-5, ALU.mult, ALU.max).then_inc(wq_sem, 1)
            dve.wait_ge(wq_sem, 3)
            dve.reciprocal(wrs[:, :], wscale[:, :]).then_inc(wq_sem, 1)
            dve.wait_ge(wq_sem, 4)
            for k in range(2):
                dve.tensor_scalar(wc_raw[:, k, :], wc_raw[:, k, :], wrs[:, k:k + 1], MAGIC, ALU.mult, ALU.add).then_inc(wq_sem, 1)
            dve.wait_ge(wq_sem, 6)
            dve.tensor_scalar(wc_raw[:, :, :], wc_raw[:, :, :], MAGIC, 1.0, ALU.subtract, ALU.min).then_inc(wq_sem, 1)
            dve.wait_ge(wq_sem, 7)
            dve.tensor_scalar(wcq[:, :, :], wc_raw[:, :, :], -1.0, None, ALU.max).then_inc(wq_done, 1)
            dve.wait_ge(rowf_in, 16)
            dve.wait_ge(attw_in, 16 * 6)
            dve.wait_ge(ew_in, 32)

            with dve.Fori(0, HALVES) as hf:
                n0 = hf * NLN
                for s in SL:
                    dve.wait_ge(x_in[s], hf * 16 + 16)
                    layer_norm(s, n0 + LN_IN, xin[s])
                for s in SL:
                    normalize(s, n0 + LN_IN, xin[s])
                    dve.wait_ge(ln_h, nth(s, n0 + (LN_IN + 1)))
                    dve.scalar_tensor_tensor(xs[s][:, :, :], h[s][:, :, :], float(np.sqrt(P)), pos[:, :].unsqueeze(1).to_broadcast([P, G, P]),
                                             ALU.mult, ALU.add).then_inc(x_upd, 1)
                with dve.Fori(0, L) as l:
                    i = hf * L + l
                    ln(n0 + l * 2 + LN_A)
                    dve.wait_ge(wqkv_in, i * 48 + 48)
                    for s in SL:
                        dve.wait_ge(kv_mm, nth(s, i + 1))
                        kv = bank(4 * s + 2, 2).rearrange("p (b c) -> p b c", b=G)
                        dve.tensor_tensor(kk[s][:, :, :], kv[:, :, 0:P], rowkv[:, 0:P].unsqueeze(1).to_broadcast([P, G, P]), ALU.add).then_inc(k_raw, 1)
                        dve.tensor_tensor(vv[s][:, :, 0:P], kv[:, :, P:2 * P], rowkv[:, P:2 * P].unsqueeze(1).to_broadcast([P, G, P]), ALU.add).then_inc(v_raw, 1)
                        dve.wait_ge(q_exp, nth(s, i + 1))
                        dve.tensor_scalar(qT[s][:, :], bank(4 * s + 1), colA[:, 2:3], 0.0, ALU.add, ALU.max).then_inc(q_relu, 1)
                    for s in SL:
                        dve.wait_ge(k_exp, nth(s, i + 1))
                        dve.wait_ge(k_relu, nth(s, i + 1))
                        dve.scalar_tensor_tensor(kp[s][:, :, :], ke[s][:, :, :], 1.0, kp[s][:, :, :], ALU.min, ALU.add).then_inc(k_pos, 1)
                        dve.wait_ge(q_relu, nth(s, i + 1))
                        dve.scalar_tensor_tensor(qT[s][:, :], qe[s][:, :], 1.0, qT[s][:, :], ALU.min, ALU.add).then_inc(q_pos, 1)
                    for s in SL:
                        dve.wait_ge(kvs_mm, nth(s, i + 1))
                        kv = bank(4 * s, 2).rearrange("p (b c) -> p b c", b=G)
                        dve.tensor_tensor(kvs[s][:, :, 0:P], kv[:, :, 0:P], same_head.unsqueeze(1).to_broadcast([P, G, P]), ALU.mult)
                        dve.tensor_tensor(kvs[s][:, :, P:P + H], kv[:, :, P:P + 1].to_broadcast([P, G, H]),
                                          head_of.unsqueeze(1).to_broadcast([P, G, H]), ALU.mult).then_inc(kv_sum, 1)
                    for s in SL:
                        dve.wait_ge(lin_mm, nth(s, i + 1))
                        o = bank(4 * s + 2, 2).rearrange("p (b c) -> p b c", b=G)
                        dve.tensor_scalar(den[s][:, :, :], o[:, :, P:P + H], EPS_ATTN, None, ALU.add).then_inc(den_eps, 1)
                        dve.wait_ge(den_eps, nth(s, i + 1))
                        dve.reciprocal(den[s][:, :, :], den[s][:, :, :]).then_inc(den_inv, 1)
                        dve.wait_ge(den_inv, nth(s, i + 1))
                        dve.tensor_tensor(at[s][:, :, :].rearrange("p b (h d) -> p b h d", h=H), o[:, :, 0:P].rearrange("p b (h d) -> p b h d", h=H),
                                          den[s][:, :, :].unsqueeze(3).to_broadcast([P, G, H, DH]), ALU.mult).then_inc(lin_done, 1)
                    for s in SL:
                        dve.wait_ge(wo_mm, nth(s, i + 1))
                        dve.wait_ge(xbo_done, nth(s, i + 1))
                        dve.tensor_tensor(xs[s][:, :, :], bank4(4 * s + 2), xb[s][:, :, :], ALU.add).then_inc(x_upd, 1)
                    ln(n0 + l * 2 + (LN_A + 1))
                    for s in SL:
                        dve.wait_ge(w2_mm, nth(s, i + 1))
                        dve.wait_ge(xb2_done, nth(s, i + 1))
                        dve.tensor_tensor(xs[s][:, :, :], bank4(4 * s + 2), xb[s][:, :, :], ALU.add).then_inc(x_upd, 1)
                ln(n0 + LN_F)
                for s in SL:
                    dve.wait_ge(ln_h, nth(s, n0 + (LN_F + 1)))
                    dve.tensor_tensor(h[s][:, :, :], h[s][:, :, :], rowf[:, 0:P].unsqueeze(1).to_broadcast([P, G, P]), ALU.mult).then_inc(f_scaled[s], 1)
                    dve.wait_ge(f_scaled[s], hf * 2 + 1)
                    dve.tensor_tensor(h[s][:, :, :], h[s][:, :, :], rowf[:, P:2 * P].unsqueeze(1).to_broadcast([P, G, P]), ALU.add).then_inc(f_scaled[s], 1)
                    dve.wait_ge(f_scaled[s], hf * 2 + 2)
                    dve.tensor_tensor(xs[s][:, :, :], xin[s][:, :, :], h[s][:, :, :], ALU.add).then_inc(x_upd, 1)
                    dve.wait_ge(x_upd, nth(s, n0 + (LN_F + 1)))
                    dve.sem_inc(xin_used[s], 1)
                for t in range(3):
                    dve.memset(S[t][:, :, :], NEG).then_inc(s_preset, 1)
                ln(n0 + LN_B)
                values(0, hf)
                for b in range(NB + 3):
                    if b < NB:
                        n = hf * (2 * NB) + b
                        dve.wait_ge(s_mm, n + 1)
                        if b == 0:
                            dve.wait_ge(s_preset, hf * 3 + 3)
                        if b >= 2:
                            dve.wait_ge(sub_done, n - 1)
                        met(dve)
                        dve.copy_predicated(S[b % 3][:, :, :], maskt[:, :].unsqueeze(1).to_broadcast([P, H, P]),
                                            bank(0, 4).rearrange("p (h k) -> p h k", h=H)).then_inc(s_out, 1)
                        dve.wait_ge(s_out, n + 1)
                        dve.tensor_reduce(smax[b % 2][:, :], S[b % 3][:, :, :], AX.X, ALU.max).then_inc(m_done, 1)
                    if b >= 3:
                        head_outputs(0, hf, b - 3)
                residual(0, hf, n0 + LN_B)
                ln(n0 + LN_C)
                cs = hf * 13
                for s in SL:
                    dve.wait_ge(ln_h, nth(s, n0 + (LN_C + 1)))
                    dve.tensor_reduce(amax[s][:, :], h[s][:, :, :], AX.X, ALU.max, apply_absolute_value=True).then_inc(c_step[s], 1)
                    act_scales(s, cs)
                    dve.tensor_scalar(deq[s][:, :], amax[s][:, :], 1.0 / 127.0, None, ALU.mult).then_inc(c_step[s], 1)
                    dve.wait_ge(c_step[s], cs + 5)
                    dve.tensor_tensor(yT[s][:, :, :], ident[:, :].unsqueeze(1).to_broadcast([P, G, P]),
                                      deq[s][:, :].unsqueeze(2).to_broadcast([P, G, P]), ALU.mult).then_inc(c_diag, 1)
                    for b in range(G):
                        ins = dve.tensor_scalar(h[s][:, b, :], h[s][:, b, :], asc[s][:, b:b + 1], MAGIC, ALU.mult, ALU.add)
                    ins.then_inc(c_step[s], 1)
                    dve.wait_ge(c_step[s], cs + 6)
                    dve.tensor_scalar(h[s][:, :, :], h[s][:, :, :], MAGIC, 127.0, ALU.subtract, ALU.min).then_inc(c_step[s], 1)
                    dve.wait_ge(c_step[s], cs + 7)
                    dve.tensor_scalar(hqb[s][:, :, :], h[s][:, :, :], -128.0, None, ALU.max).then_inc(c_q1, 1)
                for c in range(CH):
                    for s in SL:
                        dve.wait_ge(c_f1_mm, nth(s, hf * CH + c + 1))
                        if c == 0:
                            dve.wait_ge(c_rs, nth(s, hf + 1))
                        else:
                            dve.wait_ge(c_conv, nth(s, hf * CH + c))
                        dve.tensor_tensor(cbuf[s][:, :, 1:P + 1], bank4(4 * s + 2), rsb[s][:, :].rearrange("p (b t) -> p b t", b=G), ALU.mult).then_inc(c_deq, 1)
                    for s in SL:
                        dve.wait_ge(c_tap1, nth(s, hf * CH + c + 1))
                        dve.scalar_tensor_tensor(yT[s][:, :, :], cbuf[s][:, :, 0:P], conv[:, c, 0:1], yT[s][:, :, :], ALU.mult, ALU.add).then_inc(f_conv, 1)
                        dve.wait_ge(f_conv, nth(s, hf * CH + c + 1))
                        dve.scalar_tensor_tensor(yT[s][:, :, :], cbuf[s][:, :, 2:P + 2], conv[:, c, 2:3], yT[s][:, :, :], ALU.mult, ALU.add).then_inc(c_conv, 1)
                for s in SL:
                    dve.wait_ge(c_silu, nth(s, hf * CH + CH))
                    dve.tensor_reduce(amax[s][:, :], big[s][:, :, :], AX.X, ALU.max, apply_absolute_value=True).then_inc(c_step[s], 1)
                    act_scales(s, cs + 7)
                    dve.wait_ge(c_step[s], cs + 11)
                    for b in range(G):
                        ins = dve.tensor_scalar(big[s][:, b, :], big[s][:, b, :], asc[s][:, b:b + 1], MAGIC, ALU.mult, ALU.add)
                    ins.then_inc(c_step[s], 1)
                    dve.tensor_scalar(deq[s][:, :], amax[s][:, :], wscale[:, 1:2], 1.0 / 127.0, ALU.mult, ALU.mult)
                    dve.wait_ge(c_step[s], cs + 12)
                    dve.tensor_scalar(q2b[s][:, :, :], big[s][:, :, :], MAGIC, 127.0, ALU.subtract, ALU.min).then_inc(c_step[s], 1)
                    dve.wait_ge(c_step[s], cs + 13)
                    dve.tensor_scalar(q2b[s][:, :, :], q2b[s][:, :, :], -128.0, None, ALU.max).then_inc(c_q2, 1)
                for s in SL:
                    dve.wait_ge(c_f2_mm, nth(s, hf + 1))
                    for b in range(G):
                        ins = dve.scalar_tensor_tensor(xs[s][:, b, :], bank4(4 * s + 2)[:, b, :], deq[s][:, b:b + 1], xs[s][:, b, :], ALU.mult, ALU.add)
                    ins.then_inc(x_upd, 1)
                ln(n0 + LN_D)
                values(1, hf)
                for s in SL:
                    dve.wait_ge(pk_done, nth(s, hf * 2 + 2))
                    dve.tensor_reduce(ksum[s][:, :], kT[s][:, :].rearrange("p (b t) -> p b t", b=G), AX.X, ALU.add).then_inc(ksum_done, 1)
                    dve.wait_ge(ksum_done, nth(s, hf + 1))
                    dve.tensor_tensor(kmean[s][:, :, :], ksum[s][:, :].unsqueeze(2).to_broadcast([P, G, H]),
                                      head_of.unsqueeze(1).to_broadcast([P, G, H]), ALU.mult).then_inc(kmean_done, 1)
                for b in range(NB + 3):
                    if b < NB:
                        above_mean(hf, b)
                    if b >= 3:
                        head_outputs(NB, hf, b - 3)
                    if 1 <= b <= NB:
                        short_way(hf, b - 1)
                    if b < NB:
                        dve.wait_ge(s_out, hf * (2 * NB) + (NB + b + 1))
                        if b >= 2:
                            dve.wait_ge(sub_done, hf * (2 * NB) + (NB + b - 1))
                        dve.tensor_reduce(smax[b % 2][:, :], S[b % 3][:, :, :], AX.X, ALU.max).then_inc(m_done, 1)
                    if 1 <= b <= NB:
                        mark_kept(hf, b - 1)
                residual(1, hf, n0 + LN_D)
                ln(n0 + LN_E)
                for s in SL:
                    e = hf * 5
                    sc = bank(4 + s)[:, 0:2 * G * ED].rearrange("p (a e) -> p a e", a=2 * G)
                    dve.wait_ge(e_s_mm, nth(s, hf + 1))
                    dve.tensor_reduce(sm[s][:, :], sc, AX.X, ALU.max).then_inc(e_step[s], 1)
                    dve.wait_ge(e_step[s], e + 1)
                    dve.tensor_tensor(se[s][:, :, :], sc, sm[s][:, :].unsqueeze(2).to_broadcast([P, 2 * G, ED]), ALU.subtract).then_inc(e_sub, 1)
                for s in SL:
                    e = hf * 5
                    dve.wait_ge(e_exp, nth(s, hf + 1))
                    dve.tensor_reduce(sm[s][:, :], se[s][:, :, :], AX.X, ALU.add).then_inc(e_step[s], 1)
                    dve.wait_ge(e_step[s], e + 2)
                    dve.reciprocal(sm[s][:, :], sm[s][:, :]).then_inc(e_step[s], 1)
                    dve.wait_ge(e_step[s], e + 3)
                    dve.tensor_tensor(se[s][:, :, :], se[s][:, :, :], sm[s][:, :].unsqueeze(2).to_broadcast([P, 2 * G, ED]), ALU.mult).then_inc(e_step[s], 1)
                    dve.wait_ge(e_step[s], e + 4)
                    dve.transpose(seT[s][:, :, :].rearrange("p a e -> p (a e)"), se[s][:, :, :].rearrange("p a e -> p (a e)")).then_inc(e_step[s], 1)
                for s in SL:
                    dve.wait_ge(e_o_mm, nth(s, hf + 1))
                    dve.scalar_tensor_tensor(h[s][:, :, :], bank4(s), 2.0, rowe[:, 8, :].unsqueeze(1).to_broadcast([P, G, P]), ALU.mult, ALU.mult).then_inc(e_out, 1)
                    dve.wait_ge(e_out, nth(s, hf + 1))
                    dve.wait_ge(e_xb, nth(s, hf + 1))
                    dve.tensor_tensor(xs[s][:, :, :], h[s][:, :, :], xb[s][:, :, :], ALU.add).then_inc(x_upd, 1)
                    dve.wait_ge(x_upd, nth(s, n0 + (LN_E + 1)))
                for s in SL:
                    dve.sem_inc(ctx_used[s], 1)
                ln(n0 + LN_M)
                with dve.Fori(0, NEXP // 2) as p:
                    n = (hf * (NEXP // 2) + p) * 16
                    for u in range(16):
                        s, c = u % 2, u % 8 // 2
                        dve.wait_ge(silu_done, n + u + 1)
                        if u == 8:
                            dve.wait_ge(d_mm, (hf * (NEXP // 2) + p) * 2 + 1)
                        dve.tensor_tensor(big[s][:, c, :], bank(4 + s), sg[s][:, :], ALU.mult).then_inc(hu_done, 1)
                for s in SL:
                    dve.wait_ge(yT_mm, nth(s, hf + 1))
                    dve.tensor_tensor(xs[s][:, :, :], bank4(2 + s), xs[s][:, :, :], ALU.add).then_inc(x_upd, 1)
                dve.wait_ge(stored, hf * (16 * SLOTS) + 16 * SLOTS)




def kernel(x, ctx_1024, mask_1x1xSxS2_ik0, **w):
    import concourse.bacc as _bacc
    from concourse.bass_utils import run_bass_kernel_spmd as _run

    def a(name):
        return np.asarray(w[name])

    def rows(*vs):
        return np.concatenate([np.asarray(v).reshape(1, -1) for v in vs], axis=1)

    def cols(*vs):
        return np.stack([np.asarray(v).reshape(-1) for v in vs], axis=1)

    def chunked(m):
        m = m.reshape(m.shape[:-2] + (CH, P, m.shape[-1]))
        return np.moveaxis(m, -3, -2).reshape(m.shape[:-3] + (P, CH * m.shape[-1]))

    arrow = np.concatenate([
        np.concatenate([a("L0_attn_bk"), a("L0_attn_bv"), a("L0_attn_bo"), a("L0_attn_b2")], axis=1),
        rows(a("L0_attn_lnf_s"), a("L0_attn_lnf_b"), a("L0_attn_lnf_s"), a("L0_attn_lnf_b"))], axis=0)
    wq4, wk4, wv4, wo4 = (a("L0_attn_W" + n) for n in "qkvo")
    b1 = a("L0_attn_b1").reshape(L, CH, P).transpose(0, 2, 1)
    qkv = a("L1_attn_w_qkv_w").reshape(H, 3, DH, P).transpose(1, 0, 2, 3).reshape(3, P, P)
    qkvb = a("L1_attn_w_qkv_b").reshape(H, 3, DH).transpose(1, 0, 2).reshape(3, P)

    r = np.arange(P)
    const = np.concatenate([r[:, None] // DH == r[None, :] // DH, r[:, None] // DH == np.arange(H)[None, :],
                            r[:, None] % 32 // DH == np.arange(4)[None, :], r[:, None] // 32 == np.arange(4)[None, :],
                            np.zeros((P, 1)) + np.arange(NEAR)[None, :] + 0.5], axis=1).astype(np.float32)
    half = P // 2
    freq = np.exp(np.arange(half, dtype=np.float32) * np.float32(-np.log(10000.0) / (half - 1))).astype(np.float32)
    ang = ((np.arange(P, dtype=np.float32) + np.float32(1.0))[:, None] * freq[None, :]).astype(np.float32)
    pos = np.concatenate([np.sin(ang), np.cos(ang)], axis=1).astype(np.float32)

    ins = {
        "x": x, "ctx": ctx_1024, "mask": np.asarray(mask_1x1xSxS2_ik0).reshape(P, P),
        "aw": np.concatenate([wq4, wk4, wv4, wo4, a("L0_attn_W1")], axis=2),
        "acolA": np.stack([a("L0_attn_ln1_s"), a("L0_attn_ln1_b"), a("L0_attn_bq")], axis=2),
        "acolB": np.concatenate([a("L0_attn_ln2_s")[:, :, None], a("L0_attn_ln2_b")[:, :, None], b1], axis=2),
        "arow": arrow, "w2a": chunked(a("L0_attn_W2")),
        "bw": np.concatenate([a("L0_xattn_W" + n).T for n in "qkvo"], axis=1),
        "bcol": cols(a("L0_xattn_bq"), a("L0_xattn_bk")), "brow": rows(a("L0_xattn_bv"), a("L0_xattn_bo")),
        "cw": np.concatenate([a("L0_ffn_w1").T, chunked(a("L0_ffn_w2").T)], axis=1),
        "cconv": chunked(np.concatenate([a("L0_ffn_conv_w").reshape(FH, 3), a("L0_ffn_conv_b").reshape(FH, 1)], axis=1)),
        "dw": np.concatenate([qkv[0].T, qkv[1].T, qkv[2].T, a("L1_attn_w_out_w").T], axis=1),
        "dcol": cols(qkvb[0], qkvb[1]), "drow": rows(qkvb[2], a("L1_attn_w_out_b")),
        "erow": rows(*(a("L1_xattn_" + n) for n in ("wqg", "bqg", "wql", "bql", "wkg", "bkg", "wkl", "bkl", "wp", "bp"))),
        "ecol": cols(*(a("L1_xattn_" + n) for n in ("wvg", "bvg", "wvl", "bvl"))),
        "mg": a("L1_ffn_Wg"), "mu": a("L1_ffn_Wu"), "md": chunked(a("L1_ffn_Wd")),
        "ident": np.eye(P, dtype=np.float32), "const": const, "pos": pos,
    }
    nc = _bacc.Bacc("TRN2", target_bir_lowering=False, num_devices=1)
    arrays, args = {}, []
    for name, v in ins.items():
        v = np.ascontiguousarray(v)
        arrays[f"in_{name}"] = v
        args.append(nc.dram_tensor(f"in_{name}", v.shape, mybir.dt.from_np(v.dtype), kind="ExternalInput").ap())
    out = nc.dram_tensor("out_x", (NSEQ, P, P), F32, kind="ExternalOutput").ap()
    decoder(nc, *args, out)
    res = _run(nc, [arrays], core_ids=[0])
    return res.results[0]["out_x"]
```

```python
from contextlib import ExitStack

import numpy as np

import concourse.bass as bass
from concourse import mybir

F32 = mybir.dt.float32
BF16 = mybir.dt.bfloat16
I32 = mybir.dt.int32
ALU = mybir.AluOpType
ACT = mybir.ActivationFunctionType
AX = mybir.AxisListType

P = 128
NSEQ = 16
SLOTS = 2
G = 4
HALVES = NSEQ // (SLOTS * G)
W = G * P
UNITS = 4
GU = SLOTS * G // UNITS
WU = GU * P
L = 4
H, DH = 16, 8
FH = 512
CH = FH // P
EH, ED = 4, 32
NEXP = 8
TOPK = 64
ROUNDS = TOPK // 8
EPS = 1e-5
EPS_ATTN = 1e-6
RSQRT_DH = float(1.0 / np.sqrt(np.float32(DH)))
MAGIC = 12582912.0
NEG = -1e9 * float(np.sqrt(DH))
TAKEN = -3.0e38
FAR = float(2 ** 100)
NEAR = 16
TSTEPS = 8
VA = DH + 2

LN_IN, LN_A, LN_F, LN_B, LN_C, LN_D, LN_E, LN_M = 0, 1, 2 * L + 1, 2 * L + 2, 2 * L + 3, 2 * L + 4, 2 * L + 5, 2 * L + 6
NLN = 2 * L + 7
TR_A, TR_B, TR_D, TR_M = 0, 2 * L, 2 * L + 1, 2 * L + 2
NTR = 2 * L + 3
NB = SLOTS * G


def decoder(nc, x, ctx, mask, aw, acolA, acolB, arow, w2a, bw, bcol, brow, cw, cconv, dw, dcol, drow,
            erow, ecol, mg, mu, md, ident_d, const_d, pos_d, out):
    stack = ExitStack()
    with stack:
        def sb(name, shape, dt=F32):
            return stack.enter_context(nc.sbuf_tensor(name, shape, dt))

        def sem(name):
            return stack.enter_context(nc.semaphore(name))

        def sems(name):
            return [sem(f"{name}{s}") for s in range(SLOTS)]

        def sbs(name, shape, dt=F32):
            return [sb(f"{name}{s}", shape, dt) for s in range(SLOTS)]

        psum = stack.enter_context(nc.psum_tensor("psum", [P, 8, 512], F32))

        def bank(k, n=1):
            return psum[:, k:k + n, :].rearrange("p a c -> p (a c)")

        def bank4(k):
            return psum[:, k, :].rearrange("p (b c) -> p b c", b=G)

        ident = sb("ident", [P, P])
        identb = sb("identb", [P, P], BF16)
        ones = sb("ones", [P, P])
        consts = sb("consts", [P, P + H + 4 + 4 + NEAR])
        same_head = consts[:, 0:P]
        head_of = consts[:, P:P + H]
        head_in_quad = consts[:, P + H:P + H + 4]
        quad_of = consts[:, P + H + 4:P + H + 8]
        half_count = consts[:, P + H + 8:P + H + 8 + NEAR]
        pos = sb("pos", [P, P])
        neg_half = sb("neg_half", [P, G])
        zeros = sb("zeros", [P, P])
        maskt = sb("maskt", [P, P], I32)

        wqkv = sb("wqkv", [P, 3 * P])
        wo = sb("wo", [P, P])
        w1 = sb("w1", [P, FH])
        w2 = sb("w2", [P, CH, P])
        colA = sb("colA", [P, 3])
        colB = sb("colB", [P, 2 + CH])
        rowkv = sb("rowkv", [P, 2 * P])
        rowo = sb("rowo", [P, P])
        row2 = sb("row2", [P, P])
        rowf = sb("rowf", [P, 2 * P])
        watt = [sb(f"watt{i}", [P, 4 * P]) for i in range(2)]
        catt = [sb(f"catt{i}", [P, 2]) for i in range(2)]
        ratt = [sb(f"ratt{i}", [P, 2 * P]) for i in range(2)]
        wcq = sb("wcq", [P, 2, FH], BF16)
        conv = sb("conv", [P, CH, 4])
        wsum = sb("wsum", [P, 2])
        wscale = sb("wscale", [P, 2])
        wrs = sb("wrs", [P, 2])
        rowe = sb("rowe", [P, 10, P])
        cole = sb("cole", [P, 4])
        wg = [sb(f"wg{k}", [P, FH]) for k in range(2)]
        wu = [sb(f"wu{k}", [P, FH]) for k in range(2)]
        wd = [sb(f"wd{k}", [P, CH, P]) for k in range(2)]

        xin = sbs("xin", [P, G, P])
        xs = sbs("xs", [P, G, P])
        xb = sbs("xb", [P, G, P])
        h = sbs("h", [P, G, P])
        hT = sbs("hT", [P, W])
        stats = sbs("stats", [P, G, 6])
        mv = sbs("mv", [P, G, 2])
        veps = sbs("veps", [P, G])
        rstd = sbs("rstd", [P, G])
        ctxt = sbs("ctxt", [P, G, P])
        ctxT = sbs("ctxT", [P, W])
        big = sbs("big", [P, CH, W])
        qT = sbs("qT", [P, W])
        kT = sbs("kT", [P, W])
        qe = sbs("qe", [P, W])
        kk = sbs("kk", [P, G, P])
        ke = sbs("ke", [P, G, P])
        kp = [t[:, 0, :].rearrange("p (b c) -> p b c", b=G) for t in big]
        vv = sbs("vv", [P, G, P + 2])
        kvs = sbs("kvs", [P, G, P + H])
        den = sbs("den", [P, G, H])
        at = sbs("at", [P, G, P])
        atT = hT
        vaug = sbs("vaug", [P, G, H, VA])
        hqb = [qe[s][:, 0:W // 2].bitcast(BF16).rearrange("p (b c) -> p b c", b=G) for s in range(SLOTS)]
        hqT = [qe[s][:, W // 2:W].bitcast(BF16) for s in range(SLOTS)]
        amax = sbs("amax", [P, G])
        asc = sbs("asc", [P, G])
        deq = sbs("deq", [P, G])
        rsb = [t[:, :, :].rearrange("p b c -> p (b c)") for t in ke]
        cbuf = sbs("cbuf", [P, G, P + 2])
        yT = kk
        kblk = [sb(f"kblk{i}", [P, 4, P]) for i in range(2)]
        S = [sb(f"S{i}", [P, H, P]) for i in range(3)]
        keep = sb("keep", [P, H, P], BF16)
        Wk = [sb(f"Wk{i}", [P, H, P]) for i in range(2)]
        far = [sb(f"far{i}", [P, H, P], BF16) for i in range(2)]
        wc_raw = far[0][:, :, :].rearrange("p h k -> p (h k)").bitcast(F32).rearrange("p (a c) -> p a c", a=2)
        own = [far[1][:, :, :].rearrange("p h k -> p (h k)").bitcast(F32)[:, i * 512:(i + 1) * 512].rearrange("p (j q) -> p j q", j=4) for i in range(2)]
        cnt, dist, above, ngr, fmul, fadd, okd, okh, theta = ([sb(f"{n}{i}", [P, H]) for i in range(2)] for n in (
            "cnt", "dist", "above", "ngr", "fmul", "fadd", "okd", "okh", "theta"))
        near = sb("near", [P, H, NEAR])
        hit = [sb(f"hit{i}", [P, H, NEAR]) for i in range(2)]
        same = sb("same", [P, H, NEAR])
        picked = sb("picked", [P, H])
        okq = [sb(f"okq{i}", [P, 4]) for i in range(2)]
        bad = [sb(f"bad{i}", [1, 5], I32) for i in range(2)]
        settled_f = [sb(f"settled_f{i}", [1, 1]) for i in range(2)]
        ksum = sbs("ksum", [P, G])
        kmean = sbs("kmean", [P, G, H])
        tmean = sbs("tmean", [P, G, H])
        E = [sb(f"E{i}", [P, H, P]) for i in range(2)]
        PT = [t[:, :, :].rearrange("p c t -> p (c t)").rearrange("p (h k) -> p h k", h=H) for t in big]
        q2b = [t[:, :, :].rearrange("p h k -> p (h k)")[:, 0:G * FH // 2].bitcast(BF16).rearrange("p (b c) -> p b c", b=G) for t in E]
        q2T = [t[:, :, :].rearrange("p h k -> p (h k)")[:, 0:G * FH // 2].bitcast(BF16).rearrange("p (c t) -> p c t", c=CH) for t in PT]
        smax = [sb(f"smax{i}", [P, H]) for i in range(2)]
        zden = [sb(f"zden{i}", [P, H]) for i in range(2)]
        se = sbs("se", [P, 2 * G, ED])
        sm = sbs("sm", [P, 2 * G])
        seT = sbs("seT", [P, 2 * G, ED])
        ablk = [Wk[0][:, 2 * G * s:2 * G * (s + 1), :] for s in range(SLOTS)]
        sg = qe

        consts_in, attw_in, cw_in, ew_in = sem("consts_in"), sem("attw_in"), sem("cw_in"), sem("ew_in")
        preset = sem("preset")
        x_in, ctx_in, xin_used, ctx_used = sems("x_in"), sems("ctx_in"), sems("xin_used"), sems("ctx_used")
        x_upd, ln_stats, ln_var, ln_veps, ln_rstd, ln_h = (sem(n) for n in ("x_upd", "ln_stats", "ln_var", "ln_veps", "ln_rstd", "ln_h"))
        hT_mm, hT_done = sem("hT_mm"), sem("hT_done")
        wqkv_in, wo_in, w1_in, w2_in, rowf_in = sem("wqkv_in"), sem("wo_in"), sem("w1_in"), sem("w2_in"), sem("rowf_in")
        q_mm, kv_mm, kvs_mm, lin_mm, atT_mm, wo_mm, w1_mm, w2_mm = (sem(n) for n in ("q_mm", "kv_mm", "kvs_mm", "lin_mm", "atT_mm", "wo_mm", "w1_mm", "w2_mm"))
        q_exp, q_pos, k_raw, v_raw, k_exp, k_relu, k_pos = (sem(n) for n in ("q_exp", "q_pos", "k_raw", "v_raw", "k_exp", "k_relu", "k_pos"))
        kv_sum, den_eps, den_inv, lin_done, atT_done, xbo_done, xb2_done, hid_done = (sem(n) for n in ("kv_sum", "den_eps", "den_inv", "lin_done", "atT_done", "xbo_done", "xb2_done", "hid_done"))
        f_scaled = sems("f_scaled")
        ctxT_mm, ctxT_done = sem("ctxT_mm"), sem("ctxT_done")
        pq_mm, pk_mm, pv_mm, pq_done, pk_done, pv_done = (sem(n) for n in ("pq_mm", "pk_mm", "pv_mm", "pq_done", "pk_done", "pv_done"))
        xba_done = sems("xba_done")
        kblk_done, s_mm, s_out, m_done, sub_done, exp_done, prob_done = (sem(n) for n in ("kblk_done", "s_mm", "s_out", "m_done", "sub_done", "exp_done", "prob_done"))
        pt_mm, pt_done, o_mm, z_done, o_done = (sem(n) for n in ("pt_mm", "pt_done", "o_mm", "z_done", "o_done"))
        x_sum, x_prob, x_own = sem("x_sum"), sem("x_prob"), sem("x_own")
        ksum_done, kmean_done, tmean_mm, tmean_done = (sem(n) for n in ("ksum_done", "kmean_done", "tmean_mm", "tmean_done"))
        t_side, far_done, z_mul, z_ready, keep_done, t_step, ok_done, bad_mm, bad_done = (sem(n) for n in ("t_side", "far_done", "z_mul", "z_ready", "keep_done", "t_step", "ok_done", "bad_mm", "bad_done"))
        oT_mm, oT_done, ao_mm = sem("oT_mm"), sem("oT_done"), sem("ao_mm")
        wq_sem = sem("wq_step")
        wsum_mm, wq_done = sem("wsum_mm"), sem("wq_done")
        c_step = sems("c_step")
        c_q1, c_q1T_mm, c_q1T, c_diag, c_rs_mm, c_rs, c_f1_mm, c_deq, c_tap1, c_conv, c_yT_mm, c_silu = (sem(n) for n in (
            "c_q1", "c_q1T_mm", "c_q1T", "c_diag", "c_rs_mm", "c_rs", "c_f1_mm", "c_deq", "c_tap1", "c_conv", "c_yT_mm", "c_silu"))
        f_conv, s_preset = sem("f_conv"), sem("s_preset")
        c_q2, c_q2T_mm, c_q2T, c_f2_mm = sem("c_q2"), sem("c_q2T_mm"), sem("c_q2T"), sem("c_f2_mm")
        e_mul, e_qk, e_v, e_step = sems("e_mul"), sems("e_qk"), sems("e_v"), sems("e_step")
        e_s_mm, e_sub, e_exp, e_blk, e_o_mm, e_out, e_xb = (sem(n) for n in ("e_s_mm", "e_sub", "e_exp", "e_blk", "e_o_mm", "e_out", "e_xb"))
        wexp_in = [sem("wexp0_in"), sem("wexp1_in")]
        gu_mm, silu_done, hu_done, d_mm, y_mm, y_copy, yT_mm = sem("gu_mm"), sem("silu_done"), sem("hu_done"), sem("d_mm"), sem("y_mm"), sem("y_copy"), sem("yT_mm")
        stored = sem("stored")
        met_pool, met_dve, met_sp = sem("met_pool"), sem("met_dve"), sem("met_sp")

        def nth(s, n):
            return n * SLOTS + (s - (SLOTS - 1))

        def nth_unit(u, n):
            return n * UNITS + (u - (UNITS - 1))

        def both(s, n):
            return nth_unit(2 * s + 1, n)

        def part(tiles, u):
            return tiles[u // 2][:, GU * (u % 2):GU * (u % 2 + 1)]

        def cols(u):
            return slice(WU * (u % 2), WU * (u % 2 + 1))

        def met(eng):
            eng.sem_inc({nc.gpsimd: met_pool, nc.vector: met_dve, nc.sync: met_sp}[eng], 1)

        block = stack.enter_context(nc.Block())
        SL = range(SLOTS)
        UN = range(UNITS)
        xv = x.rearrange("b t d -> t b d")
        cv = ctx.rearrange("b t d -> t b d")
        ov = out.rearrange("b t d -> t b d")

        @block.sync
        def _(sp):
            for dst, src in ((ident[:, :], ident_d), (consts[:, :], const_d), (pos[:, :], pos_d), (maskt[:, :], mask)):
                sp.dma_start(dst, src).then_inc(consts_in, 16)
            sp.dma_start(rowf[:, :], arow[L:L + 1, 0:2 * P].to_broadcast([P, 2 * P])).then_inc(rowf_in, 16)

            def load_x(s, first):
                sp.dma_start(xin[s][:, :, :], xv[:, bass.ds(first, G), :]).then_inc(x_in[s], 16)

            def load_ctx(s, first):
                sp.dma_start(ctxt[s][:, :, :], cv[:, bass.ds(first, G), :]).then_inc(ctx_in[s], 16)

            def layer(t, l):
                return t[bass.ds(l, 1)].rearrange("o p c -> (o p) c")

            def row(l, a, b):
                return arow[bass.ds(l, 1), a * P:b * P].to_broadcast([P, (b - a) * P])

            def load_qkv(l):
                sp.dma_start(wqkv[:, :], layer(aw, l)[:, 0:3 * P]).then_inc(wqkv_in, 16)
                sp.dma_start(colA[:, :], layer(acolA, l)).then_inc(wqkv_in, 16)
                sp.dma_start(rowkv[:, :], row(l, 0, 2)).then_inc(wqkv_in, 16)

            def load_out(l):
                sp.dma_start(wo[:, :], layer(aw, l)[:, 3 * P:4 * P]).then_inc(wo_in, 16)
                sp.dma_start(rowo[:, :], row(l, 2, 3)).then_inc(wo_in, 16)

            def load_up(l):
                sp.dma_start(w1[:, :], layer(aw, l)[:, 4 * P:8 * P]).then_inc(w1_in, 16)
                sp.dma_start(colB[:, :], layer(acolB, l)).then_inc(w1_in, 16)

            def load_down(l):
                sp.dma_start(w2[:, :, :].rearrange("p a c -> p (a c)"), layer(w2a, l)).then_inc(w2_in, 16)
                sp.dma_start(row2[:, :], row(l, 3, 4)).then_inc(w2_in, 16)

            def load_expert(k, e):
                sp.dma_start(wg[k][:, :], layer(mg, e)).then_inc(wexp_in[k], 16)
                sp.dma_start(wu[k][:, :], layer(mu, e)).then_inc(wexp_in[k], 16)
                sp.dma_start(wd[k][:, :, :].rearrange("p a c -> p (a c)"), layer(md, e)).then_inc(wexp_in[k], 16)

            for s in SL:
                load_x(s, s * G)
            for load in (load_qkv, load_out, load_up, load_down):
                load(0)
            for s in SL:
                load_ctx(s, s * G)
            for k in range(2):
                load_expert(k, k)
            with sp.Fori(0, HALVES) as hf:
                after = [sp.snap(((HALVES - 1) - hf) * NB + s * G) for s in SL]
                with sp.Fori(0, L) as l:
                    i = hf * L + l
                    nl = sp.snap((l + 1) % L)
                    sp.wait_ge(lin_mm, i * UNITS + UNITS)
                    load_qkv(nl)
                    sp.wait_ge(w1_mm, i * (UNITS * CH) + UNITS * CH)
                    load_out(nl)
                    sp.wait_ge(hid_done, i * (UNITS * CH) + UNITS * CH)
                    load_up(nl)
                    sp.wait_ge(w2_mm, i * UNITS + UNITS)
                    sp.wait_ge(xb2_done, i * 2 + 2)
                    load_down(nl)
                for s in SL:
                    sp.wait_ge(xin_used[s], hf + 1)
                    met(sp)
                    load_x(s, after[s])
                for s in SL:
                    sp.wait_ge(ctx_used[s], hf + 1)
                    load_ctx(s, after[s])
                with sp.Fori(0, NEXP // 2) as p:
                    n = hf * (NEXP // 2) + p
                    ne = [sp.snap((p * 2 + (k + 2)) % NEXP) for k in range(2)]
                    for k in range(2):
                        sp.wait_ge(d_mm, n * 2 + (k + 1))
                        load_expert(k, ne[k])
                for s in SL:
                    sp.wait_ge(x_upd, both(s, hf * NLN + NLN))
                    sp.dma_start(ov[:, bass.ds(hf * NB + s * G, G), :], xs[s][:, :, :]).then_inc(stored, 16)
            sp.wait_ge(stored, HALVES * 16 * SLOTS)

        @block.gpsimd
        def _(pool):
            for i in range(2):
                pool.dma_start(watt[i][:, :], (bw, dw)[i]).then_inc(attw_in, 16)
                pool.dma_start(catt[i][:, :], (bcol, dcol)[i]).then_inc(attw_in, 16)
                pool.dma_start(ratt[i][:, :], (brow, drow)[i].to_broadcast([P, 2 * P])).then_inc(attw_in, 16)
            pool.dma_start(wc_raw[:, :, :].rearrange("p a c -> p (a c)"), cw).then_inc(cw_in, 16)
            pool.dma_start(conv[:, :, :].rearrange("p a c -> p (a c)"), cconv).then_inc(cw_in, 16)
            pool.dma_start(rowe[:, :, :].rearrange("p a c -> p (a c)"), erow.to_broadcast([P, 10 * P])).then_inc(ew_in, 16)
            pool.dma_start(cole[:, :], ecol).then_inc(ew_in, 16)
            pool.memset(neg_half[:, :], -0.5)
            pool.memset(ones[:, :], 1.0)
            for s in SL:
                pool.memset(vv[s][:, :, P:P + 2], 1.0)
                pool.memset(vaug[s][:, :, :, DH:VA], 1.0)
                pool.memset(cbuf[s][:, :, 0:1], 0.0)
                pool.memset(cbuf[s][:, :, P + 1:P + 2], 0.0)
            pool.memset(zeros[:, :], 0.0).then_inc(preset, 1)
            pool.wait_ge(preset, 1)
            pool.wait_ge(consts_in, 64)

            def ln_rsqrt(s, n):
                pool.wait_ge(ln_var, nth(s, n + 1))
                met(pool)
                pool.tensor_scalar(veps[s][:, :], mv[s][:, :, 1], EPS, None, ALU.add).then_inc(ln_veps, 1)
                pool.wait_ge(ln_veps, nth(s, n + 1))
                pool.tensor_tensor(rstd[s][:, :], veps[s][:, :], neg_half[:, :], ALU.pow).then_inc(ln_rstd, 1)

            def bc(row):
                return row.unsqueeze(1).to_broadcast([P, G, P])

            def core(off, hf, att):
                def spread(b):
                    s, c = b // G, b % G
                    if c == 0:
                        pool.wait_ge(pk_done, nth(s, hf * 2 + att + 1))
                    if b >= 2:
                        pool.wait_ge(s_mm, hf * (2 * NB) + (off + b - 1))
                    pool.tensor_tensor(kblk[b % 2][:, :, :],
                                       kT[s][:, c * P:(c + 1) * P].unsqueeze(1).to_broadcast([P, 4, P]),
                                       head_in_quad.unsqueeze(2).to_broadcast([P, 4, P]), ALU.mult).then_inc(kblk_done, 1)

                def candidates(b):
                    t = b % 2
                    n = hf * NB + b
                    pool.wait_ge(t_side, (hf * NB + b) * 4 + 3)
                    if b >= 2:
                        pool.wait_ge(prob_done, n - 1)
                    pool.tensor_tensor(Wk[t][:, :, :], S[b % 3][:, :, :], ngr[t][:, :].unsqueeze(2).to_broadcast([P, H, P]), ALU.mult).then_inc(z_mul, 1)
                    pool.wait_ge(z_mul, n + 1)
                    pool.wait_ge(far_done, n + 1)
                    pool.tensor_tensor(Wk[t][:, :, :], Wk[t][:, :, :], far[t][:, :, :], ALU.subtract).then_inc(z_ready, 1)

                for b in range(2):
                    spread(b)
                if att == 1:
                    candidates(0)
                for b in range(NB + 1):
                    if b + 2 < NB and att == 1:
                        spread(b + 2)
                    if b < NB:
                        pool.wait_ge(m_done, hf * (2 * NB) + (off + b + 1))
                        if b >= 2:
                            pool.wait_ge(pt_mm, hf * (8 * NB) + 4 * (off + b - 1))
                        pool.tensor_tensor(E[b % 2][:, :, :], S[b % 3][:, :, :],
                                           smax[b % 2][:, :].unsqueeze(2).to_broadcast([P, H, P]), ALU.subtract).then_inc(sub_done, 1)
                    if att == 0 and b >= 1:
                        a = b - 1
                        pool.wait_ge(z_done, hf * (2 * NB) + (a + 1))
                        pool.tensor_tensor(E[a % 2][:, :, :], E[a % 2][:, :, :], zden[a % 2][:, :].unsqueeze(2).to_broadcast([P, H, P]), ALU.mult).then_inc(x_prob, 1)
                    if b + 2 < NB and att == 0:
                        spread(b + 2)
                    if b >= 1 and att == 1:
                        pool.wait_ge(keep_done, hf * NB + b)
                        pool.wait_ge(exp_done, hf * (2 * NB) + (NB + b))
                        pool.tensor_tensor(E[(b - 1) % 2][:, :, :], E[(b - 1) % 2][:, :, :], keep[:, :, :], ALU.mult).then_inc(prob_done, 1)
                    if b + 1 < NB and att == 1:
                        candidates(b + 1)

            with pool.Fori(0, HALVES) as hf:
                n0 = hf * NLN
                for s in SL:
                    ln_rsqrt(s, n0 + LN_IN)
                with pool.Fori(0, L) as l:
                    i = hf * L + l
                    for s in SL:
                        ln_rsqrt(s, n0 + l * 2 + LN_A)
                    for u in UN:
                        pool.wait_ge(k_raw, nth_unit(u, i + 1))
                        met(pool)
                        pool.tensor_scalar(part(kp, u), part(kk, u), 0.0, None, ALU.max).then_inc(k_relu, 1)
                    pool.wait_ge(wo_in, i * 32 + 32)
                    for s in SL:
                        pool.tensor_tensor(xb[s][:, :, :], xs[s][:, :, :], bc(rowo[:, :]), ALU.add).then_inc(xbo_done, 1)
                    for s in SL:
                        ln_rsqrt(s, n0 + l * 2 + (LN_A + 1))
                    pool.wait_ge(w2_in, i * 32 + 32)
                    for s in SL:
                        pool.tensor_tensor(xb[s][:, :, :], xs[s][:, :, :], bc(row2[:, :]), ALU.add).then_inc(xb2_done, 1)
                for s in SL:
                    ln_rsqrt(s, n0 + LN_F)
                for s in SL:
                    ln_rsqrt(s, n0 + LN_B)
                    if s == 0:
                        pool.wait_ge(attw_in, 16 * 6)
                    pool.tensor_tensor(xb[s][:, :, :], xs[s][:, :, :], bc(ratt[0][:, P:2 * P]), ALU.add).then_inc(xba_done[s], 1)
                core(0, hf, 0)
                for s in SL:
                    ln_rsqrt(s, n0 + LN_C)
                for s in SL:
                    ln_rsqrt(s, n0 + LN_D)
                    pool.tensor_tensor(xb[s][:, :, :], xs[s][:, :, :], bc(ratt[1][:, P:2 * P]), ALU.add).then_inc(xba_done[s], 1)
                    pool.wait_ge(ln_h, both(s, n0 + (LN_D + 1)))
                    pool.wait_ge(xba_done[s], hf * 3 + 2)
                    pool.tensor_tensor(xb[s][:, :, :], xb[s][:, :, :], h[s][:, :, :], ALU.add).then_inc(xba_done[s], 1)
                core(NB, hf, 1)
                pool.wait_ge(ew_in, 32)
                for s in SL:
                    ln_rsqrt(s, n0 + LN_E)
                    pool.tensor_tensor(xb[s][:, :, :], xs[s][:, :, :], bc(rowe[:, 9, :]), ALU.add).then_inc(e_xb, 1)
                for s in SL:
                    for j in (2, 3, 0, 1):
                        src = h[s] if j < 2 else ctxt[s]
                        if j == 0:
                            pool.wait_ge(ln_h, both(s, n0 + (LN_E + 1)))
                        if j == 2:
                            pool.wait_ge(ctx_in[s], hf * 16 + 16)
                        t = big[s][:, j, :].rearrange("p (b c) -> p b c", b=G)
                        pool.tensor_tensor(t, src[:, :, :], bc(rowe[:, 2 * j, :]), ALU.mult).then_inc(e_mul[s], 1)
                    for k, j in enumerate((2, 3, 0, 1)):
                        t = big[s][:, j, :].rearrange("p (b c) -> p b c", b=G)
                        pool.wait_ge(e_mul[s], hf * 4 + k + 1)
                        pool.tensor_tensor(t, t, bc(rowe[:, 2 * j + 1, :]), ALU.add).then_inc(e_qk[s], 1)
                for s in SL:
                    pool.wait_ge(e_step[s], hf * 5 + 5)
                    pool.tensor_tensor(ablk[s][:, :, :].rearrange("p a (q e) -> p a q e", q=EH),
                                       seT[s][:, :, :].unsqueeze(2).to_broadcast([P, 2 * G, EH, ED]),
                                       quad_of.unsqueeze(1).unsqueeze(3).to_broadcast([P, 2 * G, EH, ED]), ALU.mult).then_inc(e_blk, 1)
                for s in SL:
                    ln_rsqrt(s, n0 + LN_M)

        @block.scalar
        def _(act):
            def hT_copy(s, m, k):
                act.wait_ge(hT_mm, both(s, m + 1))
                act.copy(hT[s][:, :], bank(k)).then_inc(hT_done, 2)

            def hT_copy_unit(u, m, k, scale, bias):
                act.wait_ge(hT_mm, nth_unit(u, m + 1))
                act.activation(hT[u // 2][:, cols(u)], bank(k)[:, 0:WU], ACT.Identity, bias=bias, scale=scale).then_inc(hT_done, 1)

            def copy_probs(off, hf, a):
                for g in range(4):
                    act.wait_ge(pt_mm, hf * (8 * NB) + 4 * (off + a) + g + 1)
                    if g == 0 and a >= 2:
                        act.wait_ge(o_mm, hf * (2 * NB) + (off + a - 1))
                    act.copy(PT[a % 2][:, 4 * g:4 * g + 4, :].rearrange("p h k -> p (h k)"), bank(4 + g % 2)).then_inc(pt_done, 1)

            def exponentials(off, hf, a):
                act.wait_ge(sub_done, hf * (2 * NB) + (off + a + 1))
                act.activation(E[a % 2][:, :, :], E[a % 2][:, :, :], ACT.Exp, scale=RSQRT_DH).then_inc(exp_done, 1)

            def core_cross(hf):
                for b in range(NB + 2):
                    if 1 <= b <= NB:
                        exponentials(0, hf, b - 1)
                    if b >= 2:
                        copy_probs(0, hf, b - 2)

            def core_topk(hf):
                def scores_out(b):
                    act.wait_ge(s_mm, hf * (2 * NB) + (NB + b + 1))
                    if b >= 3:
                        act.wait_ge(prob_done, hf * NB + (b - 2))
                    act.copy(S[b % 3][:, :, :].rearrange("p h k -> p (h k)"), bank(0, 4)).then_inc(s_out, 1)

                scores_out(0)
                for b in range(NB + 2):
                    if 1 <= b <= NB:
                        exponentials(NB, hf, b - 1)
                    if b >= 2:
                        copy_probs(NB, hf, b - 2)
                    if b < NB:
                        act.wait_ge(t_side, hf * (4 * NB) + 4 * (b + 1))
                        for hd in range(H):
                            ins = act.activation(far[b % 2][:, hd, :], far[b % 2][:, hd, :], ACT.Identity,
                                                 bias=fadd[b % 2][:, hd:hd + 1], scale=fmul[b % 2][:, hd:hd + 1])
                        ins.then_inc(far_done, 1)
                    if b + 1 < NB:
                        scores_out(b + 1)

            act.wait_ge(preset, 1)
            with act.Fori(0, HALVES) as hf:
                with act.Fori(0, L) as l:
                    i = hf * L + l
                    m = hf * NTR + l * 2
                    act.wait_ge(wqkv_in, i * 48 + 48)
                    for u in UN:
                        hT_copy_unit(u, m, 2 * u, colA[:, 0:1], colA[:, 1:2])
                    for u in UN:
                        act.wait_ge(q_mm, nth_unit(u, i + 1))
                        act.activation(qe[u // 2][:, cols(u)], bank(2 * u + 1)[:, 0:WU], ACT.Exp, bias=colA[:, 2:3])
                        act.activation(qT[u // 2][:, cols(u)], bank(2 * u + 1)[:, 0:WU], ACT.Relu, bias=colA[:, 2:3]).then_inc(q_exp, 1)
                        act.wait_ge(k_raw, nth_unit(u, i + 1))
                        act.activation(part(ke, u), part(kk, u), ACT.Exp).then_inc(k_exp, 1)
                    for u in UN:
                        act.wait_ge(atT_mm, nth_unit(u, i + 1))
                        act.copy(atT[u // 2][:, cols(u)], bank(2 * u)[:, 0:WU]).then_inc(atT_done, 1)
                    act.wait_ge(w1_in, i * 32 + 32)
                    for u in UN:
                        hT_copy_unit(u, m + 1, 2 * u, colB[:, 0:1], colB[:, 1:2])
                    for c in range(CH):
                        for u in UN:
                            act.wait_ge(w1_mm, nth_unit(u, i * CH + c + 1))
                            act.activation(big[u // 2][:, c, cols(u)], bank(2 * u + (1, 0)[c % 2])[:, 0:WU], ACT.Relu,
                                           bias=colB[:, 2 + c:3 + c]).then_inc(hid_done, 1)
                act.wait_ge(attw_in, 16 * 6)
                for s in SL:
                    act.wait_ge(ctxT_mm, nth(s, hf + 1))
                    act.copy(ctxT[s][:, :], bank(4 * s + 2)).then_inc(ctxT_done, 1)
                for s in SL:
                    hT_copy(s, hf * NTR + TR_B, 4 * s)
                for s in SL:
                    act.wait_ge(pk_mm, nth(s, hf * 2 + 1))
                    act.activation(kT[s][:, :], bank(4 * s + 2), ACT.Identity, bias=catt[0][:, 1:2]).then_inc(pk_done, 1)
                    act.wait_ge(pq_mm, nth(s, hf * 2 + 1))
                    act.activation(qT[s][:, :], bank(4 * s + 1), ACT.Identity, bias=catt[0][:, 0:1]).then_inc(pq_done, 1)
                core_cross(hf)
                act.wait_ge(cw_in, 32)
                act.wait_ge(wq_done, 1)
                for s in SL:
                    act.wait_ge(c_q1T_mm, nth(s, hf + 1))
                    act.copy(hqT[s][:, :], bank(4 * s).bitcast(BF16)[:, 0:W]).then_inc(c_q1T, 1)
                    act.wait_ge(c_rs_mm, nth(s, hf + 1))
                    act.activation(rsb[s][:, :], bank(4 * s + 1), ACT.Copy, scale=wscale[:, 0:1]).then_inc(c_rs, 1)
                for c in range(CH):
                    for s in SL:
                        act.wait_ge(c_deq, nth(s, hf * CH + c + 1))
                        if c >= 1:
                            act.wait_ge(c_yT_mm, nth(s, hf * CH + c))
                        act.activation(yT[s][:, :, :], cbuf[s][:, :, 1:P + 1], ACT.Identity, bias=conv[:, c, 3:4], scale=conv[:, c, 1:2]).then_inc(c_tap1, 1)
                    for s in SL:
                        act.wait_ge(c_yT_mm, nth(s, hf * CH + c + 1))
                        act.activation(big[s][:, :, c * P:(c + 1) * P], bank4(4 * s + 3), ACT.Silu).then_inc(c_silu, 1)
                for c in range(CH):
                    for s in SL:
                        act.wait_ge(c_q2T_mm, nth(s, hf * CH + c + 1))
                        act.copy(q2T[s][:, c, :], bank(4 * s + c % 2).bitcast(BF16)[:, 0:W]).then_inc(c_q2T, 1)
                for s in SL:
                    hT_copy(s, hf * NTR + TR_D, 4 * s)
                for s in SL:
                    act.wait_ge(pk_mm, nth(s, hf * 2 + 2))
                    act.activation(kT[s][:, :], bank(4 * s + 2), ACT.Identity, bias=catt[1][:, 1:2]).then_inc(pk_done, 1)
                    act.wait_ge(pq_mm, nth(s, hf * 2 + 2))
                    act.activation(qT[s][:, :], bank(4 * s + 1), ACT.Identity, bias=catt[1][:, 0:1]).then_inc(pq_done, 1)
                for s in SL:
                    act.wait_ge(tmean_mm, nth(s, hf + 1))
                    act.mul(tmean[s][:, :, :].rearrange("p b h -> p (b h)"), bank(4 * s + 1)[:, 0:G * H], 1.0 / P).then_inc(tmean_done, 1)
                core_topk(hf)
                for s in SL:
                    act.wait_ge(oT_mm, nth(s, hf + 1))
                    act.copy(atT[s][:, :], bank(s)).then_inc(oT_done, 1)
                act.wait_ge(ew_in, 32)
                for s in SL:
                    act.activation(qT[s][:, :], ctxT[s][:, :], ACT.Identity, bias=cole[:, 1:2], scale=cole[:, 0:1]).then_inc(e_v[s], 1)
                    act.activation(kT[s][:, :], ctxT[s][:, :], ACT.Identity, bias=cole[:, 3:4], scale=cole[:, 2:3]).then_inc(e_v[s], 1)
                for s in SL:
                    act.wait_ge(e_sub, nth(s, hf + 1))
                    act.activation(se[s][:, :, :], se[s][:, :, :], ACT.Exp, scale=float(P) ** -0.5).then_inc(e_exp, 1)
                for s in SL:
                    hT_copy(s, hf * NTR + TR_M, 6 + s)
                with act.Fori(0, NEXP // 2) as p:
                    n = (hf * (NEXP // 2) + p) * 16
                    for u in range(16):
                        s = u % 2
                        act.wait_ge(gu_mm, n + u + 1)
                        if u >= 2:
                            act.wait_ge(hu_done, n + u - 1)
                        act.activation(sg[s][:, :], bank(2 + s), ACT.Silu).then_inc(silu_done, 1)
                for s in SL:
                    act.wait_ge(y_mm, nth(s, hf + 1))
                    act.copy(sg[s][:, :], bank(s)).then_inc(y_copy, 1)

        @block.tensor
        def _(pe):
            def transposes(dst, src, eye, last_sem, step=1, n=G):
                for b in range(n):
                    mm = pe.transpose(dst[:, b * P:(b + 1) * P], src[:, b, :], eye)
                mm.then_inc(last_sem, step)

            def hT_tr(s, n, k):
                pe.wait_ge(ln_h, both(s, n + 1))
                transposes(bank(k), h[s], ident[:, :], hT_mm, 2)

            def hT_tr_unit(u, n, k):
                pe.wait_ge(ln_h, nth_unit(u, n + 1))
                transposes(bank(k), part(h, u), ident[:, :], hT_mm, 1, GU)

            def project(att, hf):
                w = watt[att]
                for s in SL:
                    pe.wait_ge(hT_done, both(s, hf * NTR + ((TR_B, TR_D)[att] + 1)))
                    kvT = ctxT[s] if att == 0 else hT[s]
                    pe.matmul(bank(4 * s + 2), w[:, P:2 * P], kvT[:, :], start=True, stop=True).then_inc(pk_mm, 1)
                    pe.matmul(bank(4 * s + 1), w[:, 0:P], hT[s][:, :], start=True, stop=True).then_inc(pq_mm, 1)
                    for b in range(G):
                        mm = pe.matmul(bank4(4 * s + 3)[:, b, :], kvT[:, b * P:(b + 1) * P], w[:, 2 * P:3 * P], start=True, stop=True)
                    mm.then_inc(pv_mm, 1)

            def mean_scores(hf):
                for s in SL:
                    pe.wait_ge(pq_done, nth(s, hf * 2 + 2))
                    pe.wait_ge(kmean_done, nth(s, hf + 1))
                    for b in range(G):
                        mm = pe.matmul(bank(4 * s + 1)[:, b * H:(b + 1) * H], qT[s][:, b * P:(b + 1) * P], kmean[s][:, b, :], start=True, stop=True)
                    mm.then_inc(tmean_mm, 1)

            def core(off, hf, att):
                probs = x_prob if att == 0 else prob_done
                pe.wait_ge(pv_done, nth(SLOTS - 1, hf * 2 + att + 1))
                pe.wait_ge(pq_done, nth(SLOTS - 1, hf * 2 + att + 1))
                if att == 1:
                    pe.wait_ge(tmean_done, nth(SLOTS - 1, hf + 1))

                def scores(b):
                    s, c = b // G, b % G
                    n = hf * (2 * NB) + (off + b)
                    pe.wait_ge(kblk_done, n + 1)
                    if b >= 1:
                        pe.wait_ge(s_out, n)
                    for q in range(4):
                        mm = pe.matmul(bank(q), qT[s][32 * q:32 * q + 32, c * P:(c + 1) * P],
                                       kblk[b % 2][32 * q:32 * q + 32, :, :].rearrange("p h k -> p (h k)"), start=True, stop=True)
                    mm.then_inc(s_mm, 1)

                def turn(a):
                    n = hf * (2 * NB) + (off + a)
                    pe.wait_ge(probs, hf * NB + (a + 1))
                    for g in range(4):
                        if a >= 1 or g >= 2:
                            pe.wait_ge(pt_done, n * 4 + (g - 1))
                        for j in range(4):
                            mm = pe.transpose(bank(4 + g % 2)[:, j * P:(j + 1) * P], E[a % 2][:, 4 * g + j, :], ident[:, :])
                        mm.then_inc(pt_mm, 1)

                def outputs(a):
                    s, c = a // G, a % G
                    n = hf * (2 * NB) + (off + a)
                    pe.wait_ge(pt_done, n * 4 + 4)
                    if a >= 2:
                        pe.wait_ge(o_done, n - 1)
                    if att == 0:
                        for q in range(4):
                            mm = pe.matmul(bank(6 + a % 2)[32 * q:32 * q + 32, :], vv[s][:, c, 32 * q:32 * q + 32],
                                           PT[a % 2][:, 4 * q:4 * q + 4, :].rearrange("p h k -> p (h k)"), start=True, stop=True)
                        mm.then_inc(o_mm, 1)
                        return
                    for hd in range(H):
                        mm = pe.matmul(bank(6 + a % 2)[:, hd * VA:(hd + 1) * VA], PT[a % 2][:, hd, :], vaug[s][:, c, hd, :], start=True, stop=True)
                    mm.then_inc(o_mm, 1)

                def settled_rows(b):
                    pe.wait_ge(ok_done, hf * NB + (b + 1))
                    pe.matmul(bank(6 + b % 2)[:, 200:204], ones[:, :], okq[b % 2][:, :], start=True, stop=True).then_inc(bad_mm, 1)

                scores(0)
                for b in range(NB + 2):
                    if b + 1 < NB and att == 1:
                        scores(b + 1)
                    if b >= 2:
                        turn(b - 2)
                        outputs(b - 2)
                    if b + 1 < NB and att == 0:
                        scores(b + 1)
                    if att == 1 and 1 <= b <= NB:
                        settled_rows(b - 1)
                for s in SL:
                    pe.wait_ge(o_done, hf * (2 * NB) + (off + G * (s + 1)))
                    if att == 1:
                        transposes(bank(s), at[s], ident[:, :], oT_mm)
                for s in SL:
                    if att == 1:
                        pe.wait_ge(oT_done, nth(s, hf + 1))
                    for b in range(G):
                        mm = pe.matmul(bank4(2 + s)[:, b, :], atT[s][:, b * P:(b + 1) * P], watt[att][:, 3 * P:4 * P], start=True, stop=True)
                    mm.then_inc(ao_mm, 1)

            pe.wait_ge(consts_in, 64)
            pe.wait_ge(preset, 1)
            pe.wait_ge(wq_sem, 2)
            pe.matmul(bank(7)[:, 0:2], ones[:, :], wsum[:, :], start=True, stop=True).then_inc(wsum_mm, 1)
            with pe.Fori(0, HALVES) as hf:
                n0 = hf * NLN
                with pe.Fori(0, L) as l:
                    i = hf * L + l
                    m = hf * NTR + l * 2
                    for u in UN:
                        hT_tr_unit(u, n0 + l * 2 + LN_A, 2 * u)
                    pe.wait_ge(wqkv_in, i * 48 + 48)
                    for u in UN:
                        s = u // 2
                        pe.wait_ge(hT_done, nth_unit(u, m + 1))
                        for b in range(GU):
                            mm = pe.matmul(bank(2 * u)[:, b * 2 * P:(b + 1) * 2 * P], hT[s][:, cols(u)][:, b * P:(b + 1) * P], wqkv[:, P:3 * P], start=True, stop=True)
                        mm.then_inc(kv_mm, 1)
                        pe.matmul(bank(2 * u + 1)[:, 0:WU], wqkv[:, 0:P], hT[s][:, cols(u)], start=True, stop=True).then_inc(q_mm, 1)
                    for u in UN:
                        pe.wait_ge(k_pos, nth_unit(u, i + 1))
                        pe.wait_ge(v_raw, nth_unit(u, i + 1))
                        for b in range(GU):
                            mm = pe.matmul(bank(2 * u)[:, b * 2 * P:b * 2 * P + P + 2], part(kp, u)[:, b, :], part(vv, u)[:, b, :], start=True, stop=True)
                        mm.then_inc(kvs_mm, 1)
                    for u in UN:
                        pe.wait_ge(q_pos, nth_unit(u, i + 1))
                        pe.wait_ge(kv_sum, nth_unit(u, i + 1))
                        for b in range(GU):
                            mm = pe.matmul(bank(2 * u + 1)[:, b * 2 * P:b * 2 * P + P + H], qT[u // 2][:, cols(u)][:, b * P:(b + 1) * P], part(kvs, u)[:, b, :], start=True, stop=True)
                        mm.then_inc(lin_mm, 1)
                    for u in UN:
                        pe.wait_ge(lin_done, nth_unit(u, i + 1))
                        transposes(bank(2 * u), part(at, u), ident[:, :], atT_mm, 1, GU)
                    pe.wait_ge(wo_in, i * 32 + 32)
                    for u in UN:
                        pe.wait_ge(atT_done, nth_unit(u, i + 1))
                        for b in range(GU):
                            mm = pe.matmul(bank(2 * u + 1)[:, b * P:(b + 1) * P], atT[u // 2][:, cols(u)][:, b * P:(b + 1) * P], wo[:, :], start=True, stop=True)
                        mm.then_inc(wo_mm, 1)
                    for u in UN:
                        hT_tr_unit(u, n0 + l * 2 + (LN_A + 1), 2 * u)
                    pe.wait_ge(w1_in, i * 32 + 32)
                    for c in range(CH):
                        for u in UN:
                            if c == 0:
                                pe.wait_ge(hT_done, nth_unit(u, m + 2))
                            if c >= 2:
                                pe.wait_ge(hid_done, nth_unit(u, i * CH + c - 1))
                            pe.matmul(bank(2 * u + (1, 0)[c % 2])[:, 0:WU], w1[:, c * P:(c + 1) * P], hT[u // 2][:, cols(u)], start=True, stop=True).then_inc(w1_mm, 1)
                    pe.wait_ge(w2_in, i * 32 + 32)
                    for u in UN:
                        pe.wait_ge(hid_done, nth_unit(u, i * CH + CH))
                        for b in range(GU):
                            for c in range(CH):
                                mm = pe.matmul(bank(2 * u + 1)[:, b * P:(b + 1) * P], big[u // 2][:, c, cols(u)][:, b * P:(b + 1) * P], w2[:, c, :], start=(c == 0), stop=(c == CH - 1))
                        mm.then_inc(w2_mm, 1)
                pe.wait_ge(attw_in, 16 * 6)
                for s in SL:
                    pe.wait_ge(ctx_in[s], hf * 16 + 16)
                    transposes(bank(4 * s + 2), ctxt[s], ident[:, :], ctxT_mm)
                for s in SL:
                    hT_tr(s, n0 + LN_B, 4 * s)
                for s in SL:
                    pe.wait_ge(ctxT_done, nth(s, hf + 1))
                project(0, hf)
                core(0, hf, 0)
                pe.wait_ge(wq_done, 1)
                for s in SL:
                    pe.wait_ge(c_q1, nth(s, hf + 1))
                    transposes(bank(4 * s).bitcast(BF16), hqb[s], identb[:, :], c_q1T_mm)
                    pe.wait_ge(c_diag, nth(s, hf + 1))
                    pe.matmul(bank(4 * s + 1), ones[:, :], yT[s][:, :, :].rearrange("p b t -> p (b t)"), start=True, stop=True).then_inc(c_rs_mm, 1)
                for c in range(CH):
                    for s in SL:
                        if c == 0:
                            pe.wait_ge(c_q1T, nth(s, hf + 1))
                        else:
                            pe.wait_ge(c_deq, nth(s, hf * CH + c))
                        pe.matmul(bank(4 * s + 2), wcq[:, 0, c * P:(c + 1) * P], hqT[s][:, :], start=True, stop=True).then_inc(c_f1_mm, 1)
                    for s in SL:
                        pe.wait_ge(c_conv, nth(s, hf * CH + c + 1))
                        if c >= 1:
                            pe.wait_ge(c_silu, nth(s, hf * CH + c))
                        transposes(bank(4 * s + 3), yT[s], ident[:, :], c_yT_mm)
                for c in range(CH):
                    for s in SL:
                        if c == 0:
                            pe.wait_ge(c_q2, nth(s, hf + 1))
                        if c >= 2:
                            pe.wait_ge(c_q2T, nth(s, hf * CH + c - 1))
                        for b in range(G):
                            mm = pe.transpose(bank(4 * s + c % 2).bitcast(BF16)[:, b * P:(b + 1) * P], q2b[s][:, b, c * P:(c + 1) * P], identb[:, :])
                        mm.then_inc(c_q2T_mm, 1)
                for s in SL:
                    pe.wait_ge(c_q2T, nth(s, hf * CH + CH))
                    for b in range(G):
                        for c in range(CH):
                            mm = pe.matmul(bank4(4 * s + 2)[:, b, :], q2T[s][:, c, b * P:(b + 1) * P], wcq[:, 1, c * P:(c + 1) * P], start=(c == 0), stop=(c == CH - 1))
                    mm.then_inc(c_f2_mm, 1)
                for s in SL:
                    hT_tr(s, n0 + LN_D, 4 * s)
                project(1, hf)
                mean_scores(hf)
                core(NB, hf, 1)
                for s in SL:
                    pe.wait_ge(e_qk[s], hf * 4 + 4)
                    for k in range(2):
                        for b in range(G):
                            for q in range(EH):
                                c = b * P + q * ED
                                mm = pe.matmul(bank(4 + s)[q * ED:(q + 1) * ED, (k * G + b) * ED:(k * G + b + 1) * ED],
                                               big[s][:, k, c:c + ED], big[s][:, 2 + k, c:c + ED], start=True, stop=True)
                    mm.then_inc(e_s_mm, 1)
                for s in SL:
                    pe.wait_ge(e_blk, nth(s, hf + 1))
                    pe.wait_ge(e_v[s], hf * 2 + 2)
                    for b in range(G):
                        pe.matmul(bank4(s)[:, b, :], qT[s][:, b * P:(b + 1) * P], ablk[s][:, b, :], start=True, stop=False)
                        mm = pe.matmul(bank4(s)[:, b, :], kT[s][:, b * P:(b + 1) * P], ablk[s][:, G + b, :], start=False, stop=True)
                    mm.then_inc(e_o_mm, 1)
                for s in SL:
                    hT_tr(s, n0 + LN_M, 6 + s)
                for s in SL:
                    pe.wait_ge(hT_done, both(s, hf * NTR + (TR_M + 1)))
                    pe.matmul(bank(s), zeros[:, :], hT[s][:, :], start=True, stop=False, skip_group_check=True)
                with pe.Fori(0, NEXP // 2) as p:
                    e = hf * (NEXP // 2) + p
                    n = e * 16
                    for u in range(16 + 2):
                        if u < 16:
                            k, c, s = u // 8, u % 8 // 2, u % 2
                            if u % 8 == 0:
                                pe.wait_ge(wexp_in[k], e * 48 + 48)
                            if u >= 2:
                                pe.wait_ge(hu_done, n + u - 1)
                            pe.matmul(bank(2 + s), wg[k][:, c * P:(c + 1) * P], hT[s][:, :], start=True, stop=True)
                            pe.matmul(bank(4 + s), wu[k][:, c * P:(c + 1) * P], hT[s][:, :], start=True, stop=True).then_inc(gu_mm, 1)
                        if u >= 2:
                            v = u - 2
                            k, c, s = v // 8, v % 8 // 2, v % 2
                            if u >= 16:
                                pe.wait_ge(hu_done, n + v + 1)
                            mm = pe.matmul(bank(s), wd[k][:, c, :], big[s][:, c, :], start=False, stop=True, skip_group_check=True)
                            if v % 8 == 7:
                                mm.then_inc(d_mm, 1)
                for s in SL:
                    mm = pe.matmul(bank(s), zeros[:, :], hT[s][:, :], start=False, stop=True, skip_group_check=True)
                    mm.then_inc(y_mm, 1)
                for s in SL:
                    pe.wait_ge(y_copy, nth(s, hf + 1))
                    transposes(bank(2 + s), sg[s][:, :].rearrange("p (b t) -> p b t", b=G), ident[:, :], yT_mm)

        @block.vector
        def _(dve):
            def layer_norm(s, n, src=None):
                src = xs[s] if src is None else src
                for b in range(G):
                    ins = dve.bn_stats(stats[s][:, b, :], src[:, b, :])
                ins.then_inc(ln_stats, 1)
                dve.wait_ge(ln_stats, nth(s, n + 1))
                met(dve)
                for b in range(G):
                    ins = dve.bn_aggr(mv[s][:, b, :], stats[s][:, b, :])
                ins.then_inc(ln_var, 1)

            def normalize(s, n, src=None):
                src = xs[s] if src is None else src
                dve.wait_ge(ln_rstd, nth(s, n + 1))
                for b in range(G):
                    ins = dve.tensor_scalar(h[s][:, b, :], src[:, b, :], mv[s][:, b, 0:1], rstd[s][:, b:b + 1], ALU.subtract, ALU.mult)
                    if b % GU == GU - 1:
                        ins.then_inc(ln_h, 1)

            def positive_keys(u, i):
                dve.wait_ge(k_exp, nth_unit(u, i + 1))
                dve.wait_ge(k_relu, nth_unit(u, i + 1))
                dve.scalar_tensor_tensor(part(kp, u), part(ke, u), 1.0, part(kp, u), ALU.min, ALU.add).then_inc(k_pos, 1)

            def add_unit(u, i, product, biased):
                dve.wait_ge(product, nth_unit(u, i + 1))
                dve.wait_ge(biased, nth(u // 2, i + 1))
                dve.tensor_tensor(part(xs, u), bank(2 * u + 1)[:, 0:WU].rearrange("p (b c) -> p b c", b=GU), part(xb, u), ALU.add).then_inc(x_upd, 1)

            def ln(n, update=None):
                for s in SL:
                    if update is not None:
                        update(s)
                    dve.wait_ge(x_upd, both(s, n))
                    layer_norm(s, n)
                for s in SL:
                    normalize(s, n)

            def values(att, hf):
                for s in SL:
                    dve.wait_ge(pv_mm, nth(s, hf * 2 + att + 1))
                    if att == 0:
                        dve.tensor_tensor(vv[s][:, :, 0:P], bank4(4 * s + 3), ratt[0][:, 0:P].unsqueeze(1).to_broadcast([P, G, P]), ALU.add).then_inc(pv_done, 1)
                        continue
                    for b in range(G):
                        ins = dve.tensor_tensor(vaug[s][:, b, :, 0:DH], bank4(4 * s + 3)[:, b, :].rearrange("p (h d) -> p h d", h=H),
                                                ratt[att][:, 0:P].rearrange("p (h d) -> p h d", h=H), ALU.add)
                    ins.then_inc(pv_done, 1)

            def cross_sums(hf, a):
                n = hf * NB + a
                dve.wait_ge(exp_done, hf * (2 * NB) + (a + 1))
                if a >= 2:
                    dve.wait_ge(x_prob, n - 1)
                dve.tensor_reduce(zden[a % 2][:, :], E[a % 2][:, :, :], AX.X, ALU.add).then_inc(x_sum, 1)
                dve.wait_ge(x_sum, n + 1)
                dve.reciprocal(zden[a % 2][:, :], zden[a % 2][:, :]).then_inc(z_done, 1)

            def cross_outputs(hf, a):
                s, c = a // G, a % G
                n = hf * (2 * NB) + a
                dve.wait_ge(o_mm, n + 1)
                dve.tensor_tensor(own[a % 2], bank(6 + a % 2).rearrange("p (j q) -> p j q", j=4),
                                  head_in_quad.unsqueeze(2).to_broadcast([P, 4, P]), ALU.mult).then_inc(x_own, 1)
                dve.wait_ge(x_own, hf * NB + (a + 1))
                dve.tensor_reduce(atT[s][:, c * P:(c + 1) * P], own[a % 2].rearrange("p j q -> p q j"), AX.X, ALU.add).then_inc(o_done, 1)

            def head_outputs(off, hf, a):
                n = hf * (2 * NB) + (off + a)
                dve.wait_ge(o_mm, n + 1)
                o = bank(6 + a % 2)[:, 0:H * VA].rearrange("p (h d) -> p h d", h=H)
                dve.reciprocal(zden[a % 2][:, :], o[:, :, DH]).then_inc(z_done, 1)
                dve.wait_ge(z_done, n + 1)
                dve.tensor_tensor(at[a // G][:, a % G, :].rearrange("p (h d) -> p h d", h=H), o[:, :, 0:DH],
                                  zden[a % 2][:, :].unsqueeze(2).to_broadcast([P, H, DH]), ALU.mult).then_inc(o_done, 1)


            def above_mean(hf, b):
                t, s, c = b % 2, b // G, b % G
                k = hf * (4 * NB) + 4 * b
                if c == 0:
                    dve.wait_ge(tmean_done, nth(s, hf + 1))
                dve.wait_ge(s_out, hf * (2 * NB) + (NB + b + 1))
                for hd in range(H):
                    ins = dve.tensor_scalar(far[t][:, hd, :], S[b % 3][:, hd, :], tmean[s][:, c, hd:hd + 1], 0.0, ALU.is_ge, ALU.add,
                                            accum_out=cnt[t][:, hd:hd + 1])
                ins.then_inc(t_side, 1)
                dve.wait_ge(t_side, k + 1)
                dve.tensor_scalar(above[t][:, :], cnt[t][:, :], float(TOPK), None, ALU.is_ge)
                dve.tensor_scalar(okd[t][:, :], cnt[t][:, :], -1.0, TOPK - 0.5, ALU.mult, ALU.add)
                dve.tensor_scalar(dist[t][:, :], cnt[t][:, :], TOPK - 0.5, None, ALU.subtract).then_inc(t_side, 1)
                dve.wait_ge(t_side, k + 2)
                dve.tensor_tensor(dist[t][:, :], dist[t][:, :], okd[t][:, :], ALU.max)
                dve.tensor_scalar(ngr[t][:, :], above[t][:, :], -2.0, 1.0, ALU.mult, ALU.add)
                dve.tensor_scalar(fmul[t][:, :], above[t][:, :], -2.0 * FAR, FAR, ALU.mult, ALU.add)
                dve.tensor_scalar(fadd[t][:, :], above[t][:, :], FAR, None, ALU.mult).then_inc(t_side, 1)
                dve.wait_ge(t_side, k + 3)
                dve.tensor_scalar(okd[t][:, :], dist[t][:, :], NEAR - 1.0, None, ALU.is_le)
                dve.tensor_tensor(hit[t][:, :, :], half_count.unsqueeze(1).to_broadcast([P, H, NEAR]),
                                  dist[t][:, :].unsqueeze(2).to_broadcast([P, H, NEAR]), ALU.is_equal).then_inc(t_side, 1)

            def short_way(hf, b):
                t = b % 2
                k = (hf * NB + b) * TSTEPS
                dve.wait_ge(z_ready, hf * NB + (b + 1))
                met(dve)
                for hd in range(H):
                    ins = dve.max(near[:, hd, 0:8], Wk[t][:, hd, :])
                ins.then_inc(t_step, 1)
                dve.wait_ge(t_step, k + 1)
                met(dve)
                for hd in range(H):
                    ins = dve.match_replace(Wk[t][:, hd, :], near[:, hd, 0:8], Wk[t][:, hd, :], TAKEN)
                ins.then_inc(t_step, 1)
                dve.wait_ge(t_step, k + 2)
                met(dve)
                for hd in range(H):
                    ins = dve.max(near[:, hd, 8:16], Wk[t][:, hd, :])
                ins.then_inc(t_step, 1)
                dve.wait_ge(t_step, k + 3)
                dve.tensor_tensor(same[:, :, :], hit[t][:, :, :], near[:, :, :], ALU.mult).then_inc(t_step, 1)
                dve.wait_ge(t_step, k + 4)
                dve.tensor_reduce(picked[:, :], same[:, :, :], AX.X, ALU.add).then_inc(t_step, 1)
                dve.wait_ge(t_step, k + 5)
                dve.tensor_tensor(theta[t][:, :], picked[:, :], ngr[t][:, :], ALU.mult)
                dve.tensor_tensor(same[:, :, :], near[:, :, :], picked[:, :].unsqueeze(2).to_broadcast([P, H, NEAR]), ALU.is_equal).then_inc(t_step, 1)
                dve.wait_ge(t_step, k + 6)
                dve.tensor_reduce(okh[t][:, :], same[:, :, :], AX.X, ALU.add).then_inc(t_step, 1)
                dve.wait_ge(t_step, k + 7)
                dve.scalar_tensor_tensor(okh[t][:, :], okh[t][:, :], 1.0, okd[t][:, :], ALU.is_equal, ALU.mult).then_inc(t_step, 1)
                dve.wait_ge(t_step, k + 8)
                dve.tensor_reduce(okq[t][:, :], okh[t][:, :].rearrange("p (q j) -> p q j", j=4), AX.X, ALU.add).then_inc(ok_done, 1)

            def long_way(b, q):
                t = b % 2
                heads = range(4 * q, 4 * q + 4)
                dve.drain()
                for r in range(ROUNDS):
                    src = S[b % 3] if r == 0 else Wk[t]
                    for hd in heads:
                        dve.max(near[:, hd, 0:8], src[:, hd, :])
                    dve.drain()
                    for hd in heads:
                        dve.match_replace(Wk[t][:, hd, :], near[:, hd, 0:8], src[:, hd, :], TAKEN)
                    dve.drain()
                for hd in heads:
                    dve.tensor_scalar(keep[:, hd, :], Wk[t][:, hd, :], TAKEN, None, ALU.is_equal)

            def mark_kept(hf, b):
                t = b % 2
                n = hf * NB + b
                if b >= 1:
                    dve.wait_ge(prob_done, n)
                dve.tensor_tensor(keep[:, :, :], S[b % 3][:, :, :], theta[t][:, :].unsqueeze(2).to_broadcast([P, H, P]), ALU.is_ge)
                dve.wait_ge(bad_mm, n + 1)
                dve.tensor_scalar(bad[t][0:1, 0:4], bank(6 + t)[0:1, 200:204], -1.0, float(4 * P), ALU.mult, ALU.add)
                dve.tensor_reduce(settled_f[t][0:1, 0:1], bank(6 + t)[0:1, 200:204], AX.X, ALU.add).then_inc(bad_done, 1)
                dve.wait_ge(bad_done, n * 2 + 1)
                dve.tensor_scalar(bad[t][0:1, 4:5], settled_f[t][0:1, 0:1], 1.0, None, ALU.mult).then_inc(bad_done, 1)
                dve.wait_ge(bad_done, n * 2 + 2)
                met(dve)
                settled = dve.value_load(bad[t][0:1, 4:5], min_val=0, max_val=H * P)
                with dve.If(settled < H * P):
                    for q in range(4):
                        unsettled = dve.value_load(bad[t][0:1, q:q + 1], min_val=0, max_val=4 * P)
                        with dve.If(unsettled > 0):
                            long_way(b, q)
                dve.drain()
                dve.sem_inc(keep_done, 1)

            def residual(att, hf, n):
                for s in SL:
                    dve.wait_ge(ao_mm, nth(s, hf * 2 + att + 1))
                    dve.wait_ge(xba_done[s], hf * 3 + (1, 3)[att])
                    dve.tensor_tensor(xs[s][:, :, :], bank4(2 + s), xb[s][:, :, :], ALU.add).then_inc(x_upd, 2)

            def act_scales(s, n):
                dve.wait_ge(c_step[s], n + 1)
                dve.tensor_scalar(amax[s][:, :], amax[s][:, :], 1e-5, None, ALU.max).then_inc(c_step[s], 1)
                dve.wait_ge(c_step[s], n + 2)
                dve.reciprocal(asc[s][:, :], amax[s][:, :]).then_inc(c_step[s], 1)
                dve.wait_ge(c_step[s], n + 3)
                dve.tensor_scalar(asc[s][:, :], asc[s][:, :], 127.0, None, ALU.mult).then_inc(c_step[s], 1)

            dve.wait_ge(consts_in, 64)
            dve.wait_ge(preset, 1)
            dve.tensor_copy(identb[:, :], ident[:, :])
            dve.wait_ge(cw_in, 32)
            for k in range(2):
                dve.tensor_reduce(wsum[:, k:k + 1], wc_raw[:, k, :], AX.X, ALU.add, apply_absolute_value=True).then_inc(wq_sem, 1)
            dve.wait_ge(wsum_mm, 1)
            dve.tensor_scalar(wscale[:, :], bank(7)[:, 0:2], 1.0 / (P * FH), 1e-5, ALU.mult, ALU.max).then_inc(wq_sem, 1)
            dve.wait_ge(wq_sem, 3)
            dve.reciprocal(wrs[:, :], wscale[:, :]).then_inc(wq_sem, 1)
            dve.wait_ge(wq_sem, 4)
            for k in range(2):
                dve.tensor_scalar(wc_raw[:, k, :], wc_raw[:, k, :], wrs[:, k:k + 1], MAGIC, ALU.mult, ALU.add).then_inc(wq_sem, 1)
            dve.wait_ge(wq_sem, 6)
            dve.tensor_scalar(wc_raw[:, :, :], wc_raw[:, :, :], MAGIC, 1.0, ALU.subtract, ALU.min).then_inc(wq_sem, 1)
            dve.wait_ge(wq_sem, 7)
            dve.tensor_scalar(wcq[:, :, :], wc_raw[:, :, :], -1.0, None, ALU.max).then_inc(wq_done, 1)
            dve.wait_ge(rowf_in, 16)
            dve.wait_ge(attw_in, 16 * 6)
            dve.wait_ge(ew_in, 32)

            with dve.Fori(0, HALVES) as hf:
                n0 = hf * NLN
                for s in SL:
                    dve.wait_ge(x_in[s], hf * 16 + 16)
                    layer_norm(s, n0 + LN_IN, xin[s])
                for s in SL:
                    normalize(s, n0 + LN_IN, xin[s])
                    dve.wait_ge(ln_h, both(s, n0 + (LN_IN + 1)))
                    dve.scalar_tensor_tensor(xs[s][:, :, :], h[s][:, :, :], float(np.sqrt(P)), pos[:, :].unsqueeze(1).to_broadcast([P, G, P]),
                                             ALU.mult, ALU.add).then_inc(x_upd, 2)
                ln(n0 + LN_A)
                with dve.Fori(0, L) as l:
                    i = hf * L + l
                    dve.wait_ge(wqkv_in, i * 48 + 48)
                    for u in UN:
                        dve.wait_ge(kv_mm, nth_unit(u, i + 1))
                        kv = bank(2 * u).rearrange("p (b c) -> p b c", b=GU)
                        dve.tensor_tensor(part(kk, u), kv[:, :, 0:P], rowkv[:, 0:P].unsqueeze(1).to_broadcast([P, GU, P]), ALU.add).then_inc(k_raw, 1)
                        dve.tensor_tensor(part(vv, u)[:, :, 0:P], kv[:, :, P:2 * P], rowkv[:, P:2 * P].unsqueeze(1).to_broadcast([P, GU, P]), ALU.add).then_inc(v_raw, 1)
                        if u >= 1:
                            positive_keys(u - 1, i)
                    positive_keys(UNITS - 1, i)
                    for u in UN:
                        q = qT[u // 2][:, cols(u)]
                        dve.wait_ge(q_exp, nth_unit(u, i + 1))
                        dve.scalar_tensor_tensor(q, qe[u // 2][:, cols(u)], 1.0, q, ALU.min, ALU.add).then_inc(q_pos, 1)
                    for u in UN:
                        dve.wait_ge(kvs_mm, nth_unit(u, i + 1))
                        kv = bank(2 * u).rearrange("p (b c) -> p b c", b=GU)
                        dve.tensor_tensor(part(kvs, u)[:, :, 0:P], kv[:, :, 0:P], same_head.unsqueeze(1).to_broadcast([P, GU, P]), ALU.mult)
                        dve.tensor_tensor(part(kvs, u)[:, :, P:P + H], kv[:, :, P:P + 1].to_broadcast([P, GU, H]),
                                          head_of.unsqueeze(1).to_broadcast([P, GU, H]), ALU.mult).then_inc(kv_sum, 1)
                    for s in SL:
                        for u in (2 * s, 2 * s + 1):
                            dve.wait_ge(lin_mm, nth_unit(u, i + 1))
                            o = bank(2 * u + 1).rearrange("p (b c) -> p b c", b=GU)
                            dve.tensor_scalar(part(den, u), o[:, :, P:P + H], EPS_ATTN, None, ALU.add).then_inc(den_eps, 1)
                        for u in (2 * s, 2 * s + 1):
                            dve.wait_ge(den_eps, nth_unit(u, i + 1))
                            dve.reciprocal(part(den, u), part(den, u)).then_inc(den_inv, 1)
                        for u in (2 * s, 2 * s + 1):
                            o = bank(2 * u + 1).rearrange("p (b c) -> p b c", b=GU)
                            dve.wait_ge(den_inv, nth_unit(u, i + 1))
                            dve.tensor_tensor(part(at, u).rearrange("p b (h d) -> p b h d", h=H), o[:, :, 0:P].rearrange("p b (h d) -> p b h d", h=H),
                                              part(den, u).unsqueeze(3).to_broadcast([P, GU, H, DH]), ALU.mult).then_inc(lin_done, 1)

                    def attended(s):
                        for u in (2 * s, 2 * s + 1):
                            add_unit(u, i, wo_mm, xbo_done)

                    def fed_forward(s):
                        for u in (2 * s, 2 * s + 1):
                            add_unit(u, i, w2_mm, xb2_done)

                    ln(n0 + l * 2 + (LN_A + 1), attended)
                    ln(n0 + l * 2 + (LN_A + 2), fed_forward)
                for s in SL:
                    dve.wait_ge(ln_h, both(s, n0 + (LN_F + 1)))
                    dve.tensor_tensor(h[s][:, :, :], h[s][:, :, :], rowf[:, 0:P].unsqueeze(1).to_broadcast([P, G, P]), ALU.mult).then_inc(f_scaled[s], 1)
                    dve.wait_ge(f_scaled[s], hf * 2 + 1)
                    dve.tensor_tensor(h[s][:, :, :], h[s][:, :, :], rowf[:, P:2 * P].unsqueeze(1).to_broadcast([P, G, P]), ALU.add).then_inc(f_scaled[s], 1)
                    dve.wait_ge(f_scaled[s], hf * 2 + 2)
                    dve.tensor_tensor(xs[s][:, :, :], xin[s][:, :, :], h[s][:, :, :], ALU.add).then_inc(x_upd, 2)
                    dve.wait_ge(x_upd, both(s, n0 + (LN_F + 1)))
                    dve.sem_inc(xin_used[s], 1)
                for t in range(3):
                    dve.memset(S[t][:, :, :], NEG).then_inc(s_preset, 1)
                ln(n0 + LN_B)
                values(0, hf)
                for b in range(NB + 3):
                    if b < NB:
                        n = hf * (2 * NB) + b
                        dve.wait_ge(s_mm, n + 1)
                        if b == 0:
                            dve.wait_ge(s_preset, hf * 3 + 3)
                        if b >= 2:
                            dve.wait_ge(sub_done, n - 1)
                        met(dve)
                        dve.copy_predicated(S[b % 3][:, :, :], maskt[:, :].unsqueeze(1).to_broadcast([P, H, P]),
                                            bank(0, 4).rearrange("p (h k) -> p h k", h=H)).then_inc(s_out, 1)
                        dve.wait_ge(s_out, n + 1)
                        dve.tensor_reduce(smax[b % 2][:, :], S[b % 3][:, :, :], AX.X, ALU.max).then_inc(m_done, 1)
                    if 1 <= b <= NB:
                        cross_sums(hf, b - 1)
                    if b >= 3:
                        cross_outputs(hf, b - 3)
                residual(0, hf, n0 + LN_B)
                ln(n0 + LN_C)
                cs = hf * 13
                for s in SL:
                    dve.wait_ge(ln_h, both(s, n0 + (LN_C + 1)))
                    dve.tensor_reduce(amax[s][:, :], h[s][:, :, :], AX.X, ALU.max, apply_absolute_value=True).then_inc(c_step[s], 1)
                    act_scales(s, cs)
                    dve.tensor_scalar(deq[s][:, :], amax[s][:, :], 1.0 / 127.0, None, ALU.mult).then_inc(c_step[s], 1)
                    dve.wait_ge(c_step[s], cs + 5)
                    dve.tensor_tensor(yT[s][:, :, :], ident[:, :].unsqueeze(1).to_broadcast([P, G, P]),
                                      deq[s][:, :].unsqueeze(2).to_broadcast([P, G, P]), ALU.mult).then_inc(c_diag, 1)
                    for b in range(G):
                        ins = dve.tensor_scalar(h[s][:, b, :], h[s][:, b, :], asc[s][:, b:b + 1], MAGIC, ALU.mult, ALU.add)
                    ins.then_inc(c_step[s], 1)
                    dve.wait_ge(c_step[s], cs + 6)
                    dve.tensor_scalar(h[s][:, :, :], h[s][:, :, :], MAGIC, 127.0, ALU.subtract, ALU.min).then_inc(c_step[s], 1)
                    dve.wait_ge(c_step[s], cs + 7)
                    dve.tensor_scalar(hqb[s][:, :, :], h[s][:, :, :], -128.0, None, ALU.max).then_inc(c_q1, 1)
                for c in range(CH):
                    for s in SL:
                        dve.wait_ge(c_f1_mm, nth(s, hf * CH + c + 1))
                        if c == 0:
                            dve.wait_ge(c_rs, nth(s, hf + 1))
                        else:
                            dve.wait_ge(c_conv, nth(s, hf * CH + c))
                        dve.tensor_tensor(cbuf[s][:, :, 1:P + 1], bank4(4 * s + 2), rsb[s][:, :].rearrange("p (b t) -> p b t", b=G), ALU.mult).then_inc(c_deq, 1)
                    for s in SL:
                        dve.wait_ge(c_tap1, nth(s, hf * CH + c + 1))
                        dve.scalar_tensor_tensor(yT[s][:, :, :], cbuf[s][:, :, 0:P], conv[:, c, 0:1], yT[s][:, :, :], ALU.mult, ALU.add).then_inc(f_conv, 1)
                        dve.wait_ge(f_conv, nth(s, hf * CH + c + 1))
                        dve.scalar_tensor_tensor(yT[s][:, :, :], cbuf[s][:, :, 2:P + 2], conv[:, c, 2:3], yT[s][:, :, :], ALU.mult, ALU.add).then_inc(c_conv, 1)
                for s in SL:
                    dve.wait_ge(c_silu, nth(s, hf * CH + CH))
                    dve.tensor_reduce(amax[s][:, :], big[s][:, :, :], AX.X, ALU.max, apply_absolute_value=True).then_inc(c_step[s], 1)
                    act_scales(s, cs + 7)
                    dve.wait_ge(c_step[s], cs + 11)
                    for b in range(G):
                        ins = dve.tensor_scalar(big[s][:, b, :], big[s][:, b, :], asc[s][:, b:b + 1], MAGIC, ALU.mult, ALU.add)
                    ins.then_inc(c_step[s], 1)
                    dve.tensor_scalar(deq[s][:, :], amax[s][:, :], wscale[:, 1:2], 1.0 / 127.0, ALU.mult, ALU.mult)
                    dve.wait_ge(c_step[s], cs + 12)
                    dve.tensor_scalar(q2b[s][:, :, :], big[s][:, :, :], MAGIC, 127.0, ALU.subtract, ALU.min).then_inc(c_step[s], 1)
                    dve.wait_ge(c_step[s], cs + 13)
                    dve.tensor_scalar(q2b[s][:, :, :], q2b[s][:, :, :], -128.0, None, ALU.max).then_inc(c_q2, 1)
                for s in SL:
                    dve.wait_ge(c_f2_mm, nth(s, hf + 1))
                    for b in range(G):
                        ins = dve.scalar_tensor_tensor(xs[s][:, b, :], bank4(4 * s + 2)[:, b, :], deq[s][:, b:b + 1], xs[s][:, b, :], ALU.mult, ALU.add)
                    ins.then_inc(x_upd, 2)
                ln(n0 + LN_D)
                values(1, hf)
                for s in SL:
                    dve.wait_ge(pk_done, nth(s, hf * 2 + 2))
                    dve.tensor_reduce(ksum[s][:, :], kT[s][:, :].rearrange("p (b t) -> p b t", b=G), AX.X, ALU.add).then_inc(ksum_done, 1)
                    dve.wait_ge(ksum_done, nth(s, hf + 1))
                    dve.tensor_tensor(kmean[s][:, :, :], ksum[s][:, :].unsqueeze(2).to_broadcast([P, G, H]),
                                      head_of.unsqueeze(1).to_broadcast([P, G, H]), ALU.mult).then_inc(kmean_done, 1)
                for b in range(NB + 3):
                    if b < NB:
                        above_mean(hf, b)
                    if b >= 3:
                        head_outputs(NB, hf, b - 3)
                    if 1 <= b <= NB:
                        short_way(hf, b - 1)
                    if b < NB:
                        dve.wait_ge(s_out, hf * (2 * NB) + (NB + b + 1))
                        if b >= 2:
                            dve.wait_ge(sub_done, hf * (2 * NB) + (NB + b - 1))
                        dve.tensor_reduce(smax[b % 2][:, :], S[b % 3][:, :, :], AX.X, ALU.max).then_inc(m_done, 1)
                    if 1 <= b <= NB:
                        mark_kept(hf, b - 1)
                residual(1, hf, n0 + LN_D)
                ln(n0 + LN_E)
                for s in SL:
                    e = hf * 5
                    sc = bank(4 + s)[:, 0:2 * G * ED].rearrange("p (a e) -> p a e", a=2 * G)
                    dve.wait_ge(e_s_mm, nth(s, hf + 1))
                    dve.tensor_reduce(sm[s][:, :], sc, AX.X, ALU.max).then_inc(e_step[s], 1)
                    dve.wait_ge(e_step[s], e + 1)
                    dve.tensor_tensor(se[s][:, :, :], sc, sm[s][:, :].unsqueeze(2).to_broadcast([P, 2 * G, ED]), ALU.subtract).then_inc(e_sub, 1)
                for s in SL:
                    e = hf * 5
                    dve.wait_ge(e_exp, nth(s, hf + 1))
                    dve.tensor_reduce(sm[s][:, :], se[s][:, :, :], AX.X, ALU.add).then_inc(e_step[s], 1)
                    dve.wait_ge(e_step[s], e + 2)
                    dve.reciprocal(sm[s][:, :], sm[s][:, :]).then_inc(e_step[s], 1)
                    dve.wait_ge(e_step[s], e + 3)
                    dve.tensor_tensor(se[s][:, :, :], se[s][:, :, :], sm[s][:, :].unsqueeze(2).to_broadcast([P, 2 * G, ED]), ALU.mult).then_inc(e_step[s], 1)
                    dve.wait_ge(e_step[s], e + 4)
                    dve.transpose(seT[s][:, :, :].rearrange("p a e -> p (a e)"), se[s][:, :, :].rearrange("p a e -> p (a e)")).then_inc(e_step[s], 1)
                for s in SL:
                    dve.wait_ge(e_o_mm, nth(s, hf + 1))
                    dve.scalar_tensor_tensor(h[s][:, :, :], bank4(s), 2.0, rowe[:, 8, :].unsqueeze(1).to_broadcast([P, G, P]), ALU.mult, ALU.mult).then_inc(e_out, 1)
                    dve.wait_ge(e_out, nth(s, hf + 1))
                    dve.wait_ge(e_xb, nth(s, hf + 1))
                    dve.tensor_tensor(xs[s][:, :, :], h[s][:, :, :], xb[s][:, :, :], ALU.add).then_inc(x_upd, 2)
                    dve.wait_ge(x_upd, both(s, n0 + (LN_E + 1)))
                for s in SL:
                    dve.sem_inc(ctx_used[s], 1)
                ln(n0 + LN_M)
                with dve.Fori(0, NEXP // 2) as p:
                    n = (hf * (NEXP // 2) + p) * 16
                    for u in range(16):
                        s, c = u % 2, u % 8 // 2
                        dve.wait_ge(silu_done, n + u + 1)
                        if u == 8:
                            dve.wait_ge(d_mm, (hf * (NEXP // 2) + p) * 2 + 1)
                        dve.tensor_tensor(big[s][:, c, :], bank(4 + s), sg[s][:, :], ALU.mult).then_inc(hu_done, 1)
                for s in SL:
                    dve.wait_ge(yT_mm, nth(s, hf + 1))
                    dve.tensor_tensor(xs[s][:, :, :], bank4(2 + s), xs[s][:, :, :], ALU.add).then_inc(x_upd, 2)
                dve.wait_ge(stored, hf * (16 * SLOTS) + 16 * SLOTS)




def kernel(x, ctx_1024, mask_1x1xSxS2_ik0, **w):
    import concourse.bacc as _bacc
    from concourse.bass_utils import run_bass_kernel_spmd as _run

    def a(name):
        return np.asarray(w[name])

    def rows(*vs):
        return np.concatenate([np.asarray(v).reshape(1, -1) for v in vs], axis=1)

    def cols(*vs):
        return np.stack([np.asarray(v).reshape(-1) for v in vs], axis=1)

    def chunked(m):
        m = m.reshape(m.shape[:-2] + (CH, P, m.shape[-1]))
        return np.moveaxis(m, -3, -2).reshape(m.shape[:-3] + (P, CH * m.shape[-1]))

    arrow = np.concatenate([
        np.concatenate([a("L0_attn_bk"), a("L0_attn_bv"), a("L0_attn_bo"), a("L0_attn_b2")], axis=1),
        rows(a("L0_attn_lnf_s"), a("L0_attn_lnf_b"), a("L0_attn_lnf_s"), a("L0_attn_lnf_b"))], axis=0)
    wq4, wk4, wv4, wo4 = (a("L0_attn_W" + n) for n in "qkvo")
    b1 = a("L0_attn_b1").reshape(L, CH, P).transpose(0, 2, 1)
    qkv = a("L1_attn_w_qkv_w").reshape(H, 3, DH, P).transpose(1, 0, 2, 3).reshape(3, P, P)
    qkvb = a("L1_attn_w_qkv_b").reshape(H, 3, DH).transpose(1, 0, 2).reshape(3, P)

    r = np.arange(P)
    const = np.concatenate([r[:, None] // DH == r[None, :] // DH, r[:, None] // DH == np.arange(H)[None, :],
                            r[:, None] % 32 // DH == np.arange(4)[None, :], r[:, None] // 32 == np.arange(4)[None, :],
                            np.zeros((P, 1)) + np.arange(NEAR)[None, :] + 0.5], axis=1).astype(np.float32)
    half = P // 2
    freq = np.exp(np.arange(half, dtype=np.float32) * np.float32(-np.log(10000.0) / (half - 1))).astype(np.float32)
    ang = ((np.arange(P, dtype=np.float32) + np.float32(1.0))[:, None] * freq[None, :]).astype(np.float32)
    pos = np.concatenate([np.sin(ang), np.cos(ang)], axis=1).astype(np.float32)

    ins = {
        "x": x, "ctx": ctx_1024, "mask": np.asarray(mask_1x1xSxS2_ik0).reshape(P, P),
        "aw": np.concatenate([wq4, wk4, wv4, wo4, a("L0_attn_W1")], axis=2),
        "acolA": np.stack([a("L0_attn_ln1_s"), a("L0_attn_ln1_b"), a("L0_attn_bq")], axis=2),
        "acolB": np.concatenate([a("L0_attn_ln2_s")[:, :, None], a("L0_attn_ln2_b")[:, :, None], b1], axis=2),
        "arow": arrow, "w2a": chunked(a("L0_attn_W2")),
        "bw": np.concatenate([a("L0_xattn_W" + n).T for n in "qkvo"], axis=1),
        "bcol": cols(a("L0_xattn_bq"), a("L0_xattn_bk")), "brow": rows(a("L0_xattn_bv"), a("L0_xattn_bo")),
        "cw": np.concatenate([a("L0_ffn_w1").T, chunked(a("L0_ffn_w2").T)], axis=1),
        "cconv": chunked(np.concatenate([a("L0_ffn_conv_w").reshape(FH, 3), a("L0_ffn_conv_b").reshape(FH, 1)], axis=1)),
        "dw": np.concatenate([qkv[0].T, qkv[1].T, qkv[2].T, a("L1_attn_w_out_w").T], axis=1),
        "dcol": cols(qkvb[0], qkvb[1]), "drow": rows(qkvb[2], a("L1_attn_w_out_b")),
        "erow": rows(*(a("L1_xattn_" + n) for n in ("wqg", "bqg", "wql", "bql", "wkg", "bkg", "wkl", "bkl", "wp", "bp"))),
        "ecol": cols(*(a("L1_xattn_" + n) for n in ("wvg", "bvg", "wvl", "bvl"))),
        "mg": a("L1_ffn_Wg"), "mu": a("L1_ffn_Wu"), "md": chunked(a("L1_ffn_Wd")),
        "ident": np.eye(P, dtype=np.float32), "const": const, "pos": pos,
    }
    nc = _bacc.Bacc("TRN2", target_bir_lowering=False, num_devices=1)
    arrays, args = {}, []
    for name, v in ins.items():
        v = np.ascontiguousarray(v)
        arrays[f"in_{name}"] = v
        args.append(nc.dram_tensor(f"in_{name}", v.shape, mybir.dt.from_np(v.dtype), kind="ExternalInput").ap())
    out = nc.dram_tensor("out_x", (NSEQ, P, P), F32, kind="ExternalOutput").ap()
    decoder(nc, *args, out)
    res = _run(nc, [arrays], core_ids=[0])
    return res.results[0]["out_x"]
```

```python
from contextlib import ExitStack

import numpy as np

import concourse.bass as bass
from concourse import mybir

F32 = mybir.dt.float32
BF16 = mybir.dt.bfloat16
I32 = mybir.dt.int32
ALU = mybir.AluOpType
ACT = mybir.ActivationFunctionType
AX = mybir.AxisListType

P = 128
NSEQ = 16
SLOTS = 2
G = 4
HALVES = NSEQ // (SLOTS * G)
W = G * P
UNITS = 4
GU = SLOTS * G // UNITS
WU = GU * P
L = 4
H, DH = 16, 8
FH = 512
CH = FH // P
EH, ED = 4, 32
NEXP = 8
TOPK = 64
ROUNDS = TOPK // 8
EPS = 1e-5
EPS_ATTN = 1e-6
RSQRT_DH = float(1.0 / np.sqrt(np.float32(DH)))
MAGIC = 12582912.0
NEG = -1e9 * float(np.sqrt(DH))
TAKEN = -3.0e38
FAR = float(2 ** 100)
NEAR = 16
TSTEPS = 8
VA = DH + 2

LN_IN, LN_A, LN_F, LN_B, LN_C, LN_D, LN_E, LN_M = 0, 1, 2 * L + 1, 2 * L + 2, 2 * L + 3, 2 * L + 4, 2 * L + 5, 2 * L + 6
NLN = 2 * L + 7
TR_A, TR_B, TR_D, TR_M = 0, 2 * L, 2 * L + 1, 2 * L + 2
NTR = 2 * L + 3
NB = SLOTS * G


def decoder(nc, x, ctx, mask, aw, acolA, acolB, arow, w2a, bw, bcol, brow, cw, cconv, dw, dcol, drow,
            erow, ecol, mg, mu, md, ident_d, const_d, pos_d, out):
    stack = ExitStack()
    with stack:
        def sb(name, shape, dt=F32):
            return stack.enter_context(nc.sbuf_tensor(name, shape, dt))

        def sem(name):
            return stack.enter_context(nc.semaphore(name))

        def sems(name):
            return [sem(f"{name}{s}") for s in range(SLOTS)]

        def sbs(name, shape, dt=F32):
            return [sb(f"{name}{s}", shape, dt) for s in range(SLOTS)]

        psum = stack.enter_context(nc.psum_tensor("psum", [P, 8, 512], F32))

        def bank(k, n=1):
            return psum[:, k:k + n, :].rearrange("p a c -> p (a c)")

        def bank4(k):
            return psum[:, k, :].rearrange("p (b c) -> p b c", b=G)

        ident = sb("ident", [P, P])
        identb = sb("identb", [P, P], BF16)
        ones = sb("ones", [P, P])
        consts = sb("consts", [P, P + H + 4 + 4 + NEAR])
        same_head = consts[:, 0:P]
        head_of = consts[:, P:P + H]
        head_in_quad = consts[:, P + H:P + H + 4]
        quad_of = consts[:, P + H + 4:P + H + 8]
        half_count = consts[:, P + H + 8:P + H + 8 + NEAR]
        pos = sb("pos", [P, P])
        neg_half = sb("neg_half", [P, G])
        zeros = sb("zeros", [P, P], BF16)
        zero_row = zeros[:, :].unsqueeze(1).to_broadcast([P, G, P])
        maskt = sb("maskt", [P, P], I32)

        wqkv = sb("wqkv", [P, 3 * P])
        wo = sb("wo", [P, P])
        w1 = sb("w1", [P, FH])
        w2 = sb("w2", [P, CH, P])
        colA = sb("colA", [P, 3])
        colB = sb("colB", [P, 2 + CH])
        rowkv = sb("rowkv", [P, 2 * P])
        rowo = sb("rowo", [P, P])
        row2 = sb("row2", [P, P])
        rowf = sb("rowf", [P, 2 * P])
        watt = [sb(f"watt{i}", [P, 4 * P]) for i in range(2)]
        catt = [sb(f"catt{i}", [P, 2]) for i in range(2)]
        ratt = [sb(f"ratt{i}", [P, 2 * P]) for i in range(2)]
        wcq = sb("wcq", [P, 2, FH], BF16)
        conv = sb("conv", [P, CH, 4])
        wsum = sb("wsum", [P, 2])
        wscale = sb("wscale", [P, 2])
        wrs = sb("wrs", [P, 2])
        rowe = sb("rowe", [P, 10, P])
        cole = sb("cole", [P, 4])
        wg = [sb(f"wg{k}", [P, FH]) for k in range(2)]
        wu = [sb(f"wu{k}", [P, FH]) for k in range(2)]
        wd = [sb(f"wd{k}", [P, CH, P]) for k in range(2)]

        xin = sbs("xin", [P, G, P])
        xs = sbs("xs", [P, G, P])
        xb = sbs("xb", [P, G, P])
        h = sbs("h", [P, G, P])
        hT = sbs("hT", [P, W])
        stats = sbs("stats", [P, G, 6])
        mv = sbs("mv", [P, G, 2])
        veps = sbs("veps", [P, G])
        rstd = sbs("rstd", [P, G])
        ctxt = sbs("ctxt", [P, G, P])
        ctxT = sbs("ctxT", [P, W])
        big = sbs("big", [P, CH, W])
        qT = sbs("qT", [P, W])
        kT = sbs("kT", [P, W])
        qe = sbs("qe", [P, W])
        kk = sbs("kk", [P, G, P])
        ke = sbs("ke", [P, G, P])
        kp = [t[:, 0, :].rearrange("p (b c) -> p b c", b=G) for t in big]
        vv = sbs("vv", [P, G, P + 2])
        kvs = sbs("kvs", [P, G, P + H])
        den = sbs("den", [P, G, H])
        at = sbs("at", [P, G, P])
        atT = hT
        vaug = sbs("vaug", [P, G, H, VA])
        hqb = [qe[s][:, 0:W // 2].bitcast(BF16).rearrange("p (b c) -> p b c", b=G) for s in range(SLOTS)]
        hqT = [qe[s][:, W // 2:W].bitcast(BF16) for s in range(SLOTS)]
        amax = sbs("amax", [P, G])
        cmax = sbs("cmax", [P, G, CH])
        asc = sbs("asc", [P, G])
        deq = sbs("deq", [P, G])
        rsb = [t[:, :, :].rearrange("p b c -> p (b c)") for t in ke]
        cbuf = sbs("cbuf", [P, G, P + 2])
        yT = kk
        kblk = [sb(f"kblk{i}", [P, 4, P]) for i in range(2)]
        S = [sb(f"S{i}", [P, H, P]) for i in range(3)]
        keep = sb("keep", [P, H, P], BF16)
        Wk = [sb(f"Wk{i}", [P, H, P]) for i in range(2)]
        far = [sb(f"far{i}", [P, H, P], BF16) for i in range(2)]
        wc_raw = far[0][:, :, :].rearrange("p h k -> p (h k)").bitcast(F32).rearrange("p (a c) -> p a c", a=2)
        own = [far[1][:, :, :].rearrange("p h k -> p (h k)").bitcast(F32)[:, i * 512:(i + 1) * 512].rearrange("p (j q) -> p j q", j=4) for i in range(2)]
        cnt, dist, above, ngr, fmul, fadd, okd, okh, theta = ([sb(f"{n}{i}", [P, H]) for i in range(2)] for n in (
            "cnt", "dist", "above", "ngr", "fmul", "fadd", "okd", "okh", "theta"))
        near = sb("near", [P, H, NEAR])
        hit = [sb(f"hit{i}", [P, H, NEAR]) for i in range(2)]
        same = sb("same", [P, H, NEAR])
        picked = sb("picked", [P, H])
        okq = [sb(f"okq{i}", [P, 4]) for i in range(2)]
        bad = [sb(f"bad{i}", [1, 5], I32) for i in range(2)]
        settled_f = [sb(f"settled_f{i}", [1, 1]) for i in range(2)]
        ksum = sbs("ksum", [P, G])
        kmean = sbs("kmean", [P, G, H])
        tmean = sbs("tmean", [P, G, H])
        E = [sb(f"E{i}", [P, H, P]) for i in range(2)]
        PT = [t[:, :, :].rearrange("p c t -> p (c t)").rearrange("p (h k) -> p h k", h=H) for t in big]
        q2b = [t[:, :, :].rearrange("p h k -> p (h k)")[:, 0:G * FH // 2].bitcast(BF16).rearrange("p (b c) -> p b c", b=G) for t in E]
        q2T = [t[:, :, :].rearrange("p h k -> p (h k)")[:, 0:G * FH // 2].bitcast(BF16).rearrange("p (c t) -> p c t", c=CH) for t in PT]
        smax = [sb(f"smax{i}", [P, H]) for i in range(2)]
        zden = [sb(f"zden{i}", [P, H]) for i in range(2)]
        se = sbs("se", [P, 2 * G, ED])
        sm = sbs("sm", [P, 2 * G])
        seT = sbs("seT", [P, 2 * G, ED])
        ablk = [Wk[0][:, 2 * G * s:2 * G * (s + 1), :] for s in range(SLOTS)]
        sg = qe

        def channels(s, j):
            return big[s][:, j, :].rearrange("p (b c) -> p b c", b=G)

        consts_in, attw_in, cw_in, ew_in = sem("consts_in"), sem("attw_in"), sem("cw_in"), sem("ew_in")
        preset = sem("preset")
        x_in, ctx_in, xin_used, ctx_used = sems("x_in"), sems("ctx_in"), sems("xin_used"), sems("ctx_used")
        x_upd, ln_stats, ln_var, ln_veps, ln_rstd, ln_h = (sem(n) for n in ("x_upd", "ln_stats", "ln_var", "ln_veps", "ln_rstd", "ln_h"))
        hT_mm, hT_done = sem("hT_mm"), sem("hT_done")
        wqkv_in, wo_in, w1_in, w2_in, rowf_in = sem("wqkv_in"), sem("wo_in"), sem("w1_in"), sem("w2_in"), sem("rowf_in")
        q_mm, kv_mm, kvs_mm, lin_mm, atT_mm, wo_mm, w1_mm, w2_mm = (sem(n) for n in ("q_mm", "kv_mm", "kvs_mm", "lin_mm", "atT_mm", "wo_mm", "w1_mm", "w2_mm"))
        q_exp, q_pos, k_raw, v_raw, k_exp, k_relu, k_pos = (sem(n) for n in ("q_exp", "q_pos", "k_raw", "v_raw", "k_exp", "k_relu", "k_pos"))
        kv_sum, den_eps, den_inv, lin_done, atT_done, xbo_done, xb2_done, hid_done = (sem(n) for n in ("kv_sum", "den_eps", "den_inv", "lin_done", "atT_done", "xbo_done", "xb2_done", "hid_done"))
        f_scaled = sems("f_scaled")
        ctxT_mm, ctxT_done = sem("ctxT_mm"), sem("ctxT_done")
        pq_mm, pk_mm, pv_mm, pq_done, pk_done, pv_done = (sem(n) for n in ("pq_mm", "pk_mm", "pv_mm", "pq_done", "pk_done", "pv_done"))
        xba_done = sems("xba_done")
        kblk_done, s_mm, s_out, m_done, sub_done, exp_done, prob_done = (sem(n) for n in ("kblk_done", "s_mm", "s_out", "m_done", "sub_done", "exp_done", "prob_done"))
        pt_mm, pt_done, o_mm, z_done, o_done = (sem(n) for n in ("pt_mm", "pt_done", "o_mm", "z_done", "o_done"))
        x_sum, x_prob, x_own = sem("x_sum"), sem("x_prob"), sem("x_own")
        ksum_done, kmean_done, tmean_mm, tmean_done = (sem(n) for n in ("ksum_done", "kmean_done", "tmean_mm", "tmean_done"))
        t_side, far_done, z_mul, z_ready, keep_done, t_step, ok_done, bad_mm, bad_done = (sem(n) for n in ("t_side", "far_done", "z_mul", "z_ready", "keep_done", "t_step", "ok_done", "bad_mm", "bad_done"))
        oT_mm, oT_done, ao_mm = sem("oT_mm"), sem("oT_done"), sem("ao_mm")
        wq_sem = sem("wq_step")
        wsum_mm, wq_done = sem("wsum_mm"), sem("wq_done")
        c_step = sems("c_step")
        c_q1, c_q1T_mm, c_q1T, c_diag, c_rs_mm, c_rs, c_f1_mm, c_deq, c_tap1, c_conv, c_yT_mm, c_silu = (sem(n) for n in (
            "c_q1", "c_q1T_mm", "c_q1T", "c_diag", "c_rs_mm", "c_rs", "c_f1_mm", "c_deq", "c_tap1", "c_conv", "c_yT_mm", "c_silu"))
        c_max = sem("c_max")
        f_conv, s_preset = sem("f_conv"), sem("s_preset")
        c_q2, c_q2T_mm, c_q2T, c_f2_mm = sem("c_q2"), sem("c_q2T_mm"), sem("c_q2T"), sem("c_f2_mm")
        e_mul, e_qk, e_v, e_step = sems("e_mul"), sems("e_qk"), sems("e_v"), sems("e_step")
        e_s_mm, e_sub, e_exp, e_blk, e_o_mm, e_out, e_xb = (sem(n) for n in ("e_s_mm", "e_sub", "e_exp", "e_blk", "e_o_mm", "e_out", "e_xb"))
        e_kmul, e_key1 = sem("e_kmul"), sem("e_key1")
        wexp_in = [sem("wexp0_in"), sem("wexp1_in")]
        gu_mm, silu_done, hu_done, d_mm, y_mm, y_copy, yT_mm = sem("gu_mm"), sem("silu_done"), sem("hu_done"), sem("d_mm"), sem("y_mm"), sem("y_copy"), sem("yT_mm")
        stored = sem("stored")
        met_pool, met_dve, met_sp = sem("met_pool"), sem("met_dve"), sem("met_sp")

        def nth(s, n):
            return n * SLOTS + (s - (SLOTS - 1))

        def nth_unit(u, n):
            return n * UNITS + (u - (UNITS - 1))

        def both(s, n):
            return nth_unit(2 * s + 1, n)

        def chunk(u, i, c):
            return i * (UNITS * CH) + (u // 2 * (2 * CH) + 2 * c + u % 2 + 1)

        def part(tiles, u):
            return tiles[u // 2][:, GU * (u % 2):GU * (u % 2 + 1)]

        def cols(u):
            return slice(WU * (u % 2), WU * (u % 2 + 1))

        def met(eng):
            eng.sem_inc({nc.gpsimd: met_pool, nc.vector: met_dve, nc.sync: met_sp}[eng], 1)

        block = stack.enter_context(nc.Block())
        SL = range(SLOTS)
        UN = range(UNITS)
        UNITS_OF = [range(2 * s, 2 * s + 2) for s in SL]
        xv = x.rearrange("b t d -> t b d")
        cv = ctx.rearrange("b t d -> t b d")
        ov = out.rearrange("b t d -> t b d")

        @block.sync
        def _(sp):
            def load_x(s, first):
                sp.dma_start(xin[s][:, :, :], xv[:, bass.ds(first, G), :]).then_inc(x_in[s], 16)

            def load_ctx(s, first):
                sp.dma_start(ctxt[s][:, :, :], cv[:, bass.ds(first, G), :]).then_inc(ctx_in[s], 16)

            def layer(t, l):
                return t[bass.ds(l, 1)].rearrange("o p c -> (o p) c")

            def row(l, a, b):
                return arow[bass.ds(l, 1), a * P:b * P].to_broadcast([P, (b - a) * P])

            def load_qkv(l):
                sp.dma_start(wqkv[:, :], layer(aw, l)[:, 0:3 * P]).then_inc(wqkv_in, 16)
                sp.dma_start(colA[:, :], layer(acolA, l)).then_inc(wqkv_in, 16)
                sp.dma_start(rowkv[:, :], row(l, 0, 2)).then_inc(wqkv_in, 16)

            def load_out(l):
                sp.dma_start(wo[:, :], layer(aw, l)[:, 3 * P:4 * P]).then_inc(wo_in, 16)
                sp.dma_start(rowo[:, :], row(l, 2, 3)).then_inc(wo_in, 16)

            def load_up(l):
                sp.dma_start(w1[:, :], layer(aw, l)[:, 4 * P:8 * P]).then_inc(w1_in, 16)
                sp.dma_start(colB[:, :], layer(acolB, l)).then_inc(w1_in, 16)

            def load_down(l):
                sp.dma_start(w2[:, :, :].rearrange("p a c -> p (a c)"), layer(w2a, l)).then_inc(w2_in, 16)
                sp.dma_start(row2[:, :], row(l, 3, 4)).then_inc(w2_in, 16)

            def load_expert(k, e):
                sp.dma_start(wg[k][:, :], layer(mg, e)).then_inc(wexp_in[k], 16)
                sp.dma_start(wu[k][:, :], layer(mu, e)).then_inc(wexp_in[k], 16)
                sp.dma_start(wd[k][:, :, :].rearrange("p a c -> p (a c)"), layer(md, e)).then_inc(wexp_in[k], 16)

            for s in SL:
                load_x(s, s * G)
            for dst, src in ((ident[:, :], ident_d), (consts[:, :], const_d), (pos[:, :], pos_d), (maskt[:, :], mask)):
                sp.dma_start(dst, src).then_inc(consts_in, 16)
            sp.dma_start(rowf[:, :], arow[L:L + 1, 0:2 * P].to_broadcast([P, 2 * P])).then_inc(rowf_in, 16)
            for load in (load_qkv, load_out, load_up, load_down):
                load(0)
            for s in SL:
                load_ctx(s, s * G)
            for k in range(2):
                load_expert(k, k)
            with sp.Fori(0, HALVES) as hf:
                after = [sp.snap(((HALVES - 1) - hf) * NB + s * G) for s in SL]
                with sp.Fori(0, L) as l:
                    i = hf * L + l
                    nl = sp.snap((l + 1) % L)
                    sp.wait_ge(lin_mm, i * UNITS + UNITS)
                    load_qkv(nl)
                    sp.wait_ge(w1_mm, i * (UNITS * CH) + UNITS * CH)
                    load_out(nl)
                    sp.wait_ge(hid_done, i * (UNITS * CH) + UNITS * CH)
                    load_up(nl)
                    sp.wait_ge(w2_mm, i * UNITS + UNITS)
                    sp.wait_ge(xb2_done, i * 2 + 2)
                    load_down(nl)
                for s in SL:
                    sp.wait_ge(xin_used[s], hf + 1)
                    met(sp)
                    load_x(s, after[s])
                for s in SL:
                    sp.wait_ge(ctx_used[s], hf + 1)
                    load_ctx(s, after[s])
                with sp.Fori(0, NEXP // 2) as p:
                    n = hf * (NEXP // 2) + p
                    ne = [sp.snap((p * 2 + (k + 2)) % NEXP) for k in range(2)]
                    for k in range(2):
                        sp.wait_ge(d_mm, n * 2 + (k + 1))
                        load_expert(k, ne[k])
                for s in SL:
                    sp.wait_ge(x_upd, both(s, hf * NLN + NLN))
                    sp.dma_start(ov[:, bass.ds(hf * NB + s * G, G), :], xs[s][:, :, :]).then_inc(stored, 16)
            sp.wait_ge(stored, 1 + HALVES * 16 * SLOTS)

        @block.gpsimd
        def _(pool):
            pool.dma_start(wc_raw[:, :, :].rearrange("p a c -> p (a c)"), cw).then_inc(cw_in, 16)
            pool.dma_start(conv[:, :, :].rearrange("p a c -> p (a c)"), cconv).then_inc(cw_in, 16)
            pool.memset(neg_half[:, :], -0.5)
            pool.memset(ones[:, :], 1.0)
            for s in SL:
                pool.memset(vv[s][:, :, P:P + 2], 1.0)
                pool.memset(vaug[s][:, :, :, DH:VA], 1.0)
                pool.memset(cbuf[s][:, :, 0:1], 0.0)
                pool.memset(cbuf[s][:, :, P + 1:P + 2], 0.0)
            pool.memset(zeros[:, :], 0.0).then_inc(preset, 1)
            for i in range(2):
                pool.dma_start(watt[i][:, :], (bw, dw)[i]).then_inc(attw_in, 16)
                pool.dma_start(catt[i][:, :], (bcol, dcol)[i]).then_inc(attw_in, 16)
                pool.dma_start(ratt[i][:, :], (brow, drow)[i].to_broadcast([P, 2 * P])).then_inc(attw_in, 16)
            pool.dma_start(rowe[:, :, :].rearrange("p a c -> p (a c)"), erow.to_broadcast([P, 10 * P])).then_inc(ew_in, 16)
            pool.dma_start(cole[:, :], ecol).then_inc(ew_in, 16)
            pool.wait_ge(preset, 1)
            pool.wait_ge(consts_in, 64)

            def ln_rsqrt(s, n):
                pool.wait_ge(ln_var, nth(s, n + 1))
                met(pool)
                pool.tensor_scalar(veps[s][:, :], mv[s][:, :, 1], EPS, None, ALU.add).then_inc(ln_veps, 1)
                pool.wait_ge(ln_veps, nth(s, n + 1))
                pool.tensor_tensor(rstd[s][:, :], veps[s][:, :], neg_half[:, :], ALU.pow).then_inc(ln_rstd, 1)

            def bc(row):
                return row.unsqueeze(1).to_broadcast([P, G, P])

            def core(off, hf, att):
                def spread(b):
                    s, c = b // G, b % G
                    if c == 0:
                        pool.wait_ge(pk_done, nth(s, hf * 2 + att + 1))
                    if b >= 2:
                        pool.wait_ge(s_mm, hf * (2 * NB) + (off + b - 1))
                    pool.tensor_tensor(kblk[b % 2][:, :, :],
                                       kT[s][:, c * P:(c + 1) * P].unsqueeze(1).to_broadcast([P, 4, P]),
                                       head_in_quad.unsqueeze(2).to_broadcast([P, 4, P]), ALU.mult).then_inc(kblk_done, 1)

                def candidates(b):
                    t = b % 2
                    n = hf * NB + b
                    pool.wait_ge(t_side, (hf * NB + b) * 4 + 3)
                    if b >= 2:
                        pool.wait_ge(prob_done, n - 1)
                    pool.tensor_tensor(Wk[t][:, :, :], S[b % 3][:, :, :], ngr[t][:, :].unsqueeze(2).to_broadcast([P, H, P]), ALU.mult).then_inc(z_mul, 1)
                    pool.wait_ge(z_mul, n + 1)
                    pool.wait_ge(far_done, n + 1)
                    pool.tensor_tensor(Wk[t][:, :, :], Wk[t][:, :, :], far[t][:, :, :], ALU.subtract).then_inc(z_ready, 1)

                for b in range(2):
                    spread(b)
                if att == 0:
                    pool.wait_ge(attw_in, 16 * 6)
                for s in SL:
                    pool.tensor_tensor(xb[s][:, :, :], xs[s][:, :, :], bc(ratt[att][:, P:2 * P]), ALU.add).then_inc(xba_done[s], 1)
                    if att == 1:
                        pool.wait_ge(ln_h, both(s, hf * NLN + (LN_D + 1)))
                        pool.wait_ge(xba_done[s], hf * 3 + 2)
                        pool.tensor_tensor(xb[s][:, :, :], xb[s][:, :, :], h[s][:, :, :], ALU.add).then_inc(xba_done[s], 1)
                if att == 1:
                    candidates(0)
                for b in range(NB + 1):
                    if b + 2 < NB and att == 1:
                        spread(b + 2)
                    if b < NB:
                        pool.wait_ge(m_done, hf * (2 * NB) + (off + b + 1))
                        if b >= 2:
                            pool.wait_ge(pt_mm, hf * (8 * NB) + 4 * (off + b - 1))
                        pool.tensor_tensor(E[b % 2][:, :, :], S[b % 3][:, :, :],
                                           smax[b % 2][:, :].unsqueeze(2).to_broadcast([P, H, P]), ALU.subtract).then_inc(sub_done, 1)
                    if att == 0 and 1 <= b < NB:
                        a = b - 1
                        pool.wait_ge(z_done, hf * (2 * NB) + (a + 1))
                        pool.tensor_tensor(E[a % 2][:, :, :], E[a % 2][:, :, :], zden[a % 2][:, :].unsqueeze(2).to_broadcast([P, H, P]), ALU.mult).then_inc(x_prob, 1)
                    if b + 2 < NB and att == 0:
                        spread(b + 2)
                    if 1 <= b < NB and att == 1:
                        pool.wait_ge(keep_done, hf * NB + b)
                        pool.wait_ge(exp_done, hf * (2 * NB) + (NB + b))
                        pool.tensor_tensor(E[(b - 1) % 2][:, :, :], E[(b - 1) % 2][:, :, :], keep[:, :, :], ALU.mult).then_inc(prob_done, 1)
                    if b + 1 < NB and att == 1:
                        candidates(b + 1)

            for s in SL:
                ln_rsqrt(s, LN_IN)
            with pool.Fori(0, HALVES) as hf:
                n0 = hf * NLN
                with pool.Fori(0, L) as l:
                    i = hf * L + l
                    for s in SL:
                        ln_rsqrt(s, n0 + l * 2 + LN_A)
                    for u in UN:
                        pool.wait_ge(k_raw, nth_unit(u, i + 1))
                        met(pool)
                        pool.tensor_scalar(part(kp, u), part(kk, u), 0.0, None, ALU.max).then_inc(k_relu, 1)
                    pool.wait_ge(wo_in, i * 32 + 32)
                    for s in SL:
                        pool.tensor_tensor(xb[s][:, :, :], xs[s][:, :, :], bc(rowo[:, :]), ALU.add).then_inc(xbo_done, 1)
                    for s in SL:
                        ln_rsqrt(s, n0 + l * 2 + (LN_A + 1))
                    pool.wait_ge(w2_in, i * 32 + 32)
                    for s in SL:
                        pool.tensor_tensor(xb[s][:, :, :], xs[s][:, :, :], bc(row2[:, :]), ALU.add).then_inc(xb2_done, 1)
                for s in SL:
                    ln_rsqrt(s, n0 + LN_F)
                for s in SL:
                    ln_rsqrt(s, n0 + LN_B)
                core(0, hf, 0)
                for s in SL:
                    ln_rsqrt(s, n0 + LN_C)
                for s in SL:
                    ln_rsqrt(s, n0 + LN_D)
                core(NB, hf, 1)
                pool.wait_ge(ew_in, 32)
                ln_rsqrt(0, n0 + LN_E)
                pool.wait_ge(ctx_in[1], hf * 16 + 16)
                pool.wait_ge(o_mm, hf * (2 * NB) + 2 * NB)
                for j in (2, 3):
                    pool.tensor_tensor(channels(1, j), ctxt[1][:, :, :], bc(rowe[:, 2 * j, :]), ALU.mult).then_inc(e_kmul, 1)
                for k, j in enumerate((2, 3)):
                    pool.wait_ge(e_kmul, hf * 2 + (k + 1))
                    pool.tensor_tensor(channels(1, j), channels(1, j), bc(rowe[:, 2 * j + 1, :]), ALU.add).then_inc(e_key1, 1)
                ln_rsqrt(1, n0 + LN_E)
                for s in SL:
                    pool.tensor_tensor(xb[s][:, :, :], xs[s][:, :, :], bc(rowe[:, 9, :]), ALU.add).then_inc(e_xb, 1)
                for s in SL:
                    pool.wait_ge(e_step[s], hf * 5 + 5)
                    pool.tensor_tensor(ablk[s][:, :, :].rearrange("p a (q e) -> p a q e", q=EH),
                                       seT[s][:, :, :].unsqueeze(2).to_broadcast([P, 2 * G, EH, ED]),
                                       quad_of.unsqueeze(1).unsqueeze(3).to_broadcast([P, 2 * G, EH, ED]), ALU.mult).then_inc(e_blk, 1)
                for s in SL:
                    ln_rsqrt(s, n0 + LN_M)
                for s in SL:
                    ln_rsqrt(s, n0 + (NLN + LN_IN))

        @block.scalar
        def _(act):
            def hT_copy(s, m, k):
                act.wait_ge(hT_mm, both(s, m + 1))
                act.copy(hT[s][:, :], bank(k)).then_inc(hT_done, 2)

            def hT_copy_unit(u, m, k, scale, bias):
                act.wait_ge(hT_mm, nth_unit(u, m + 1))
                act.activation(hT[u // 2][:, cols(u)], bank(k)[:, 0:WU], ACT.Identity, bias=bias, scale=scale).then_inc(hT_done, 1)

            def copy_probs(off, hf, a):
                for g in range(4):
                    act.wait_ge(pt_mm, hf * (8 * NB) + 4 * (off + a) + g + 1)
                    if g == 0 and a >= 2:
                        act.wait_ge(o_mm, hf * (2 * NB) + (off + a - 1))
                    act.copy(PT[a % 2][:, 4 * g:4 * g + 4, :].rearrange("p h k -> p (h k)"), bank(4 + g % 2)).then_inc(pt_done, 1)

            def exponentials(off, hf, a):
                act.wait_ge(sub_done, hf * (2 * NB) + (off + a + 1))
                act.activation(E[a % 2][:, :, :], E[a % 2][:, :, :], ACT.Exp, scale=RSQRT_DH).then_inc(exp_done, 1)

            def core_cross(hf):
                for b in range(NB + 2):
                    if 1 <= b <= NB:
                        exponentials(0, hf, b - 1)
                    if b >= 2:
                        copy_probs(0, hf, b - 2)

            def copy_outputs(s, hf):
                act.wait_ge(oT_mm, nth(s, hf + 1))
                act.copy(atT[s][:, :], bank(s)).then_inc(oT_done, 1)

            def projected(s, hf):
                hT_copy(s, hf * NTR + TR_D, 4 * s)
                act.wait_ge(pk_mm, nth(s, hf * 2 + 2))
                act.activation(kT[s][:, :], bank(4 * s + 2), ACT.Identity, bias=catt[1][:, 1:2]).then_inc(pk_done, 1)
                act.wait_ge(pq_mm, nth(s, hf * 2 + 2))
                act.activation(qT[s][:, :], bank(4 * s + 1), ACT.Identity, bias=catt[1][:, 0:1]).then_inc(pq_done, 1)

            def means_out(s, hf):
                act.wait_ge(tmean_mm, nth(s, hf + 1))
                act.mul(tmean[s][:, :, :].rearrange("p b h -> p (b h)"), bank(4 * s + 1)[:, 0:G * H], 1.0 / P).then_inc(tmean_done, 1)

            def core_topk(hf):
                def scores_out(b):
                    act.wait_ge(s_mm, hf * (2 * NB) + (NB + b + 1))
                    if b >= 3:
                        act.wait_ge(prob_done, hf * NB + (b - 2))
                    act.copy(S[b % 3][:, :, :].rearrange("p h k -> p (h k)"), bank(0, 4)).then_inc(s_out, 1)

                scores_out(0)
                projected(1, hf)
                for b in range(NB + 2):
                    if 1 <= b <= NB:
                        exponentials(NB, hf, b - 1)
                    if b == NB + 1:
                        copy_outputs(0, hf)
                    if b >= 2:
                        copy_probs(NB, hf, b - 2)
                    if b < NB:
                        act.wait_ge(t_side, hf * (4 * NB) + 4 * (b + 1))
                        for hd in range(H):
                            ins = act.activation(far[b % 2][:, hd, :], far[b % 2][:, hd, :], ACT.Identity,
                                                 bias=fadd[b % 2][:, hd:hd + 1], scale=fmul[b % 2][:, hd:hd + 1])
                        ins.then_inc(far_done, 1)
                    if b + 1 < NB:
                        scores_out(b + 1)
                    if b == 0:
                        means_out(1, hf)

            act.wait_ge(preset, 1)
            with act.Fori(0, HALVES) as hf:
                with act.Fori(0, L) as l:
                    i = hf * L + l
                    m = hf * NTR + l * 2
                    act.wait_ge(wqkv_in, i * 48 + 48)
                    for u in UNITS_OF[0]:
                        hT_copy_unit(u, m, 2 * u, colA[:, 0:1], colA[:, 1:2])
                    for u in UN:
                        if u == 1:
                            for v in UNITS_OF[1]:
                                hT_copy_unit(v, m, 2 * v, colA[:, 0:1], colA[:, 1:2])
                        act.wait_ge(q_mm, nth_unit(u, i + 1))
                        act.activation(qe[u // 2][:, cols(u)], bank(2 * u + 1)[:, 0:WU], ACT.Exp, bias=colA[:, 2:3])
                        act.activation(qT[u // 2][:, cols(u)], bank(2 * u + 1)[:, 0:WU], ACT.Relu, bias=colA[:, 2:3]).then_inc(q_exp, 1)
                        act.wait_ge(k_raw, nth_unit(u, i + 1))
                        act.activation(part(ke, u), part(kk, u), ACT.Exp).then_inc(k_exp, 1)
                    for u in UN:
                        act.wait_ge(atT_mm, nth_unit(u, i + 1))
                        act.copy(atT[u // 2][:, cols(u)], bank(2 * u)[:, 0:WU]).then_inc(atT_done, 1)
                    act.wait_ge(w1_in, i * 32 + 32)
                    for s in SL:
                        for u in UNITS_OF[s]:
                            hT_copy_unit(u, m + 1, 2 * u, colB[:, 0:1], colB[:, 1:2])
                        for c in range(CH):
                            for u in UNITS_OF[s]:
                                act.wait_ge(w1_mm, chunk(u, i, c))
                                act.activation(big[s][:, c, cols(u)], bank(2 * u + (1, 0)[c % 2])[:, 0:WU], ACT.Relu,
                                               bias=colB[:, 2 + c:3 + c]).then_inc(hid_done, 1)
                act.wait_ge(attw_in, 16 * 6)
                for s in SL:
                    act.wait_ge(ctxT_mm, nth(s, hf + 1))
                    act.copy(ctxT[s][:, :], bank(4 * s + 2)).then_inc(ctxT_done, 1)
                for s in SL:
                    act.wait_ge(pk_mm, nth(s, hf * 2 + 1))
                    act.activation(kT[s][:, :], bank(4 * s + 2), ACT.Identity, bias=catt[0][:, 1:2]).then_inc(pk_done, 1)
                for s in SL:
                    hT_copy(s, hf * NTR + TR_B, 4 * s)
                    act.wait_ge(pq_mm, nth(s, hf * 2 + 1))
                    act.activation(qT[s][:, :], bank(4 * s + 1), ACT.Identity, bias=catt[0][:, 0:1]).then_inc(pq_done, 1)
                core_cross(hf)
                act.wait_ge(cw_in, 32)
                act.wait_ge(wq_done, 1)
                for s in SL:
                    act.wait_ge(c_q1T_mm, nth(s, hf + 1))
                    act.copy(hqT[s][:, :], bank(4 * s).bitcast(BF16)[:, 0:W]).then_inc(c_q1T, 1)
                    act.wait_ge(c_rs_mm, nth(s, hf + 1))
                    act.activation(rsb[s][:, :], bank(4 * s + 1), ACT.Copy, scale=wscale[:, 0:1]).then_inc(c_rs, 1)
                for c in range(CH):
                    for s in SL:
                        act.wait_ge(c_deq, nth(s, hf * CH + c + 1))
                        if c >= 1:
                            act.wait_ge(c_yT_mm, nth(s, hf * CH + c))
                        act.activation(yT[s][:, :, :], cbuf[s][:, :, 1:P + 1], ACT.Identity, bias=conv[:, c, 3:4], scale=conv[:, c, 1:2]).then_inc(c_tap1, 1)
                    for s in SL:
                        act.wait_ge(c_yT_mm, nth(s, hf * CH + c + 1))
                        act.activation(big[s][:, :, c * P:(c + 1) * P], bank4(4 * s + 3), ACT.Silu).then_inc(c_silu, 1)
                for s in SL:
                    for c in range(CH):
                        act.wait_ge(c_q2T_mm, hf * (SLOTS * CH) + (s * CH + c + 1))
                        act.copy(q2T[s][:, c, :], bank(4 * s + c % 2).bitcast(BF16)[:, 0:W]).then_inc(c_q2T, 1)
                projected(0, hf)
                means_out(0, hf)
                core_topk(hf)
                copy_outputs(1, hf)
                act.wait_ge(ew_in, 32)
                for s in SL:
                    act.activation(qT[s][:, :], ctxT[s][:, :], ACT.Identity, bias=cole[:, 1:2], scale=cole[:, 0:1]).then_inc(e_v[s], 1)
                    act.activation(kT[s][:, :], ctxT[s][:, :], ACT.Identity, bias=cole[:, 3:4], scale=cole[:, 2:3]).then_inc(e_v[s], 1)
                for s in SL:
                    act.wait_ge(e_sub, nth(s, hf + 1))
                    act.activation(se[s][:, :, :], se[s][:, :, :], ACT.Exp, scale=float(P) ** -0.5).then_inc(e_exp, 1)
                for s in SL:
                    hT_copy(s, hf * NTR + TR_M, 6 + s)
                with act.Fori(0, NEXP // 2) as p:
                    n = (hf * (NEXP // 2) + p) * 16
                    for u in range(16):
                        s = u % 2
                        act.wait_ge(gu_mm, n + u + 1)
                        if u >= 2:
                            act.wait_ge(hu_done, n + u - 1)
                        act.activation(sg[s][:, :], bank(2 + s), ACT.Silu).then_inc(silu_done, 1)
                for s in SL:
                    act.wait_ge(y_mm, nth(s, hf + 1))
                    act.copy(sg[s][:, :], bank(s)).then_inc(y_copy, 1)

        @block.tensor
        def _(pe):
            def transposes(dst, src, eye, last_sem, step=1, n=G):
                for b in range(n):
                    mm = pe.transpose(dst[:, b * P:(b + 1) * P], src[:, b, :], eye)
                mm.then_inc(last_sem, step)

            def hT_tr(s, n, k):
                pe.wait_ge(ln_h, both(s, n + 1))
                transposes(bank(k), h[s], ident[:, :], hT_mm, 2)

            def hT_tr_unit(u, n, k):
                pe.wait_ge(ln_h, nth_unit(u, n + 1))
                transposes(bank(k), part(h, u), ident[:, :], hT_mm, 1, GU)

            def keys(att, s, kvT):
                pe.matmul(bank(4 * s + 2), watt[att][:, P:2 * P], kvT[:, :], start=True, stop=True).then_inc(pk_mm, 1)

            def queries(att, s):
                pe.matmul(bank(4 * s + 1), watt[att][:, 0:P], hT[s][:, :], start=True, stop=True).then_inc(pq_mm, 1)

            def values(att, s, kvT):
                for b in range(G):
                    mm = pe.matmul(bank4(4 * s + 3)[:, b, :], kvT[:, b * P:(b + 1) * P], watt[att][:, 2 * P:3 * P], start=True, stop=True)
                mm.then_inc(pv_mm, 1)

            def cross_queries(s, hf):
                hT_tr(s, hf * NLN + LN_B, 4 * s)
                pe.wait_ge(hT_done, both(s, hf * NTR + (TR_B + 1)))
                queries(0, s)

            def topk_projections(s, hf):
                hT_tr(s, hf * NLN + LN_D, 4 * s)
                pe.wait_ge(hT_done, both(s, hf * NTR + (TR_D + 1)))
                keys(1, s, hT[s])
                queries(1, s)
                values(1, s, hT[s])

            def mean_scores(s, hf):
                pe.wait_ge(pq_done, nth(s, hf * 2 + 2))
                pe.wait_ge(kmean_done, nth(s, hf + 1))
                for b in range(G):
                    mm = pe.matmul(bank(4 * s + 1)[:, b * H:(b + 1) * H], qT[s][:, b * P:(b + 1) * P], kmean[s][:, b, :], start=True, stop=True)
                mm.then_inc(tmean_mm, 1)

            def core(off, hf, att):
                probs = x_prob if att == 0 else prob_done

                def banks_free(s):
                    pe.wait_ge(pv_done, nth(s, hf * 2 + att + 1))
                    pe.wait_ge(pq_done, nth(s, hf * 2 + att + 1))
                    if att == 1:
                        pe.wait_ge(tmean_done, nth(s, hf + 1))

                def scores(b):
                    s, c = b // G, b % G
                    n = hf * (2 * NB) + (off + b)
                    pe.wait_ge(kblk_done, n + 1)
                    if b >= 1:
                        pe.wait_ge(s_out, n)
                    for q in range(4):
                        mm = pe.matmul(bank(q), qT[s][32 * q:32 * q + 32, c * P:(c + 1) * P],
                                       kblk[b % 2][32 * q:32 * q + 32, :, :].rearrange("p h k -> p (h k)"), start=True, stop=True)
                    mm.then_inc(s_mm, 1)

                def turn(a):
                    n = hf * (2 * NB) + (off + a)
                    pe.wait_ge(probs, hf * NB + (a + 1))
                    for g in range(4):
                        if a >= 1 or g >= 2:
                            pe.wait_ge(pt_done, n * 4 + (g - 1))
                        for j in range(4):
                            mm = pe.transpose(bank(4 + g % 2)[:, j * P:(j + 1) * P], E[a % 2][:, 4 * g + j, :], ident[:, :])
                        mm.then_inc(pt_mm, 1)

                def outputs(a):
                    s, c = a // G, a % G
                    n = hf * (2 * NB) + (off + a)
                    pe.wait_ge(pt_done, n * 4 + 4)
                    if a >= 2:
                        pe.wait_ge(o_done, n - 1)
                    if att == 0:
                        for q in range(4):
                            mm = pe.matmul(bank(6 + a % 2)[32 * q:32 * q + 32, :], vv[s][:, c, 32 * q:32 * q + 32],
                                           PT[a % 2][:, 4 * q:4 * q + 4, :].rearrange("p h k -> p (h k)"), start=True, stop=True)
                        mm.then_inc(o_mm, 1)
                        return
                    for hd in range(H):
                        mm = pe.matmul(bank(6 + a % 2)[:, hd * VA:(hd + 1) * VA], PT[a % 2][:, hd, :], vaug[s][:, c, hd, :], start=True, stop=True)
                    mm.then_inc(o_mm, 1)

                def settled_rows(b):
                    pe.wait_ge(ok_done, hf * NB + (b + 1))
                    pe.matmul(bank(6 + b % 2)[:, 200:204], ones[:, :], okq[b % 2][:, :], start=True, stop=True).then_inc(bad_mm, 1)

                def turn_outputs(s):
                    pe.wait_ge(o_done, hf * (2 * NB) + (off + G * (s + 1)))
                    if att == 1:
                        transposes(bank(s), at[s], ident[:, :], oT_mm)

                def project_outputs(s):
                    if att == 1:
                        pe.wait_ge(oT_done, nth(s, hf + 1))
                    for b in range(G):
                        mm = pe.matmul(bank4(2 + s)[:, b, :], atT[s][:, b * P:(b + 1) * P], watt[att][:, 3 * P:4 * P], start=True, stop=True)
                    mm.then_inc(ao_mm, 1)

                banks_free(0)
                scores(0)
                if att == 0:
                    cross_queries(1, hf)
                else:
                    topk_projections(1, hf)
                for b in range(NB + 2):
                    if b + 1 < NB and att == 1:
                        scores(b + 1)
                    if b == 0 and att == 1:
                        mean_scores(1, hf)
                    if b == 2:
                        banks_free(1)
                    if b == NB + 1:
                        pe.wait_ge(s_out, hf * (2 * NB) + (off + NB))
                        turn_outputs(0)
                    if b >= 2:
                        turn(b - 2)
                    if b == NB + 1:
                        project_outputs(0)
                    if b >= 2:
                        outputs(b - 2)
                    if b + 1 < NB and att == 0:
                        scores(b + 1)
                    if att == 1 and 1 <= b <= NB:
                        settled_rows(b - 1)
                turn_outputs(1)
                project_outputs(1)

            pe.wait_ge(consts_in, 64)
            pe.wait_ge(preset, 1)
            pe.wait_ge(wq_sem, 2)
            pe.matmul(bank(7)[:, 0:2], ones[:, :], wsum[:, :], start=True, stop=True).then_inc(wsum_mm, 1)
            with pe.Fori(0, HALVES) as hf:
                n0 = hf * NLN
                with pe.Fori(0, L) as l:
                    i = hf * L + l
                    m = hf * NTR + l * 2
                    for s in SL:
                        for u in UNITS_OF[s]:
                            hT_tr_unit(u, n0 + l * 2 + LN_A, 2 * u)
                        if s == 0:
                            pe.wait_ge(wqkv_in, i * 48 + 48)
                        for u in UNITS_OF[s]:
                            pe.wait_ge(hT_done, nth_unit(u, m + 1))
                            for b in range(GU):
                                mm = pe.matmul(bank(2 * u)[:, b * 2 * P:(b + 1) * 2 * P], hT[s][:, cols(u)][:, b * P:(b + 1) * P], wqkv[:, P:3 * P], start=True, stop=True)
                            mm.then_inc(kv_mm, 1)
                            pe.matmul(bank(2 * u + 1)[:, 0:WU], wqkv[:, 0:P], hT[s][:, cols(u)], start=True, stop=True).then_inc(q_mm, 1)
                    for u in UN:
                        pe.wait_ge(k_pos, nth_unit(u, i + 1))
                        pe.wait_ge(v_raw, nth_unit(u, i + 1))
                        for b in range(GU):
                            mm = pe.matmul(bank(2 * u)[:, b * 2 * P:b * 2 * P + P + 2], part(kp, u)[:, b, :], part(vv, u)[:, b, :], start=True, stop=True)
                        mm.then_inc(kvs_mm, 1)
                    for u in UN:
                        pe.wait_ge(q_pos, nth_unit(u, i + 1))
                        pe.wait_ge(kv_sum, nth_unit(u, i + 1))
                        for b in range(GU):
                            mm = pe.matmul(bank(2 * u + 1)[:, b * 2 * P:b * 2 * P + P + H], qT[u // 2][:, cols(u)][:, b * P:(b + 1) * P], part(kvs, u)[:, b, :], start=True, stop=True)
                        mm.then_inc(lin_mm, 1)
                    for u in UN:
                        pe.wait_ge(lin_done, nth_unit(u, i + 1))
                        transposes(bank(2 * u), part(at, u), ident[:, :], atT_mm, 1, GU)
                    pe.wait_ge(wo_in, i * 32 + 32)
                    for u in UN:
                        pe.wait_ge(atT_done, nth_unit(u, i + 1))
                        for b in range(GU):
                            mm = pe.matmul(bank(2 * u + 1)[:, b * P:(b + 1) * P], atT[u // 2][:, cols(u)][:, b * P:(b + 1) * P], wo[:, :], start=True, stop=True)
                        mm.then_inc(wo_mm, 1)

                    def turn_up(s):
                        for u in UNITS_OF[s]:
                            hT_tr_unit(u, n0 + l * 2 + (LN_A + 1), 2 * u)

                    def up(s):
                        for c in range(CH):
                            for u in UNITS_OF[s]:
                                if c == 0:
                                    pe.wait_ge(hT_done, nth_unit(u, m + 2))
                                if c >= 2:
                                    pe.wait_ge(hid_done, chunk(u, i, c - 2))
                                pe.matmul(bank(2 * u + (1, 0)[c % 2])[:, 0:WU], w1[:, c * P:(c + 1) * P], hT[s][:, cols(u)], start=True, stop=True).then_inc(w1_mm, 1)

                    def down(s):
                        for u in UNITS_OF[s]:
                            pe.wait_ge(hid_done, chunk(u, i, CH - 1))
                            for b in range(GU):
                                for c in range(CH):
                                    mm = pe.matmul(bank(2 * u + 1)[:, b * P:(b + 1) * P], big[s][:, c, cols(u)][:, b * P:(b + 1) * P], w2[:, c, :], start=(c == 0), stop=(c == CH - 1))
                            mm.then_inc(w2_mm, 1)

                    turn_up(0)
                    pe.wait_ge(w1_in, i * 32 + 32)
                    up(0)
                    turn_up(1)
                    pe.wait_ge(w2_in, i * 32 + 32)
                    down(0)
                    up(1)
                    down(1)
                pe.wait_ge(attw_in, 16 * 6)
                for s in SL:
                    pe.wait_ge(ctx_in[s], hf * 16 + 16)
                    transposes(bank(4 * s + 2), ctxt[s], ident[:, :], ctxT_mm)
                for s in SL:
                    pe.wait_ge(ctxT_done, nth(s, hf + 1))
                    keys(0, s, ctxT[s])
                    pe.wait_ge(x_upd, both(s, n0 + LN_F))
                    values(0, s, ctxT[s])
                cross_queries(0, hf)
                core(0, hf, 0)
                pe.wait_ge(wq_done, 1)
                for s in SL:
                    pe.wait_ge(c_q1, nth(s, hf + 1))
                    transposes(bank(4 * s).bitcast(BF16), hqb[s], identb[:, :], c_q1T_mm)
                    pe.wait_ge(c_diag, nth(s, hf + 1))
                    pe.matmul(bank(4 * s + 1), ones[:, :], yT[s][:, :, :].rearrange("p b t -> p (b t)"), start=True, stop=True).then_inc(c_rs_mm, 1)

                def first(c):
                    for s in SL:
                        if c == 0:
                            pe.wait_ge(c_q1T, nth(s, hf + 1))
                        else:
                            pe.wait_ge(c_deq, nth(s, hf * CH + c))
                        pe.matmul(bank(4 * s + 2), wcq[:, 0, c * P:(c + 1) * P], hqT[s][:, :], start=True, stop=True).then_inc(c_f1_mm, 1)

                first(0)
                for c in range(CH):
                    if c + 1 < CH:
                        first(c + 1)
                    for s in SL:
                        pe.wait_ge(c_conv, nth(s, hf * CH + c + 1))
                        if c >= 1:
                            pe.wait_ge(c_silu, nth(s, hf * CH + c))
                        transposes(bank(4 * s + 3), yT[s], ident[:, :], c_yT_mm)
                for s in SL:
                    pe.wait_ge(c_q2, nth(s, hf + 1))
                    for c in range(CH):
                        if c >= 2:
                            pe.wait_ge(c_q2T, hf * (SLOTS * CH) + (s * CH + c - 1))
                        for b in range(G):
                            mm = pe.transpose(bank(4 * s + c % 2).bitcast(BF16)[:, b * P:(b + 1) * P], q2b[s][:, b, c * P:(c + 1) * P], identb[:, :])
                        mm.then_inc(c_q2T_mm, 1)
                    pe.wait_ge(c_q2T, hf * (SLOTS * CH) + (s + 1) * CH)
                    for b in range(G):
                        for c in range(CH):
                            mm = pe.matmul(bank4(4 * s + 2)[:, b, :], q2T[s][:, c, b * P:(b + 1) * P], wcq[:, 1, c * P:(c + 1) * P], start=(c == 0), stop=(c == CH - 1))
                    mm.then_inc(c_f2_mm, 1)
                topk_projections(0, hf)
                mean_scores(0, hf)
                core(NB, hf, 1)
                for s in SL:
                    pe.wait_ge(e_qk[s], (hf * 4 + 4, hf * 2 + 2)[s])
                    if s == 1:
                        pe.wait_ge(e_key1, hf * 2 + 2)
                    for k in range(2):
                        for b in range(G):
                            for q in range(EH):
                                c = b * P + q * ED
                                mm = pe.matmul(bank(4 + s)[q * ED:(q + 1) * ED, (k * G + b) * ED:(k * G + b + 1) * ED],
                                               big[s][:, k, c:c + ED], big[s][:, 2 + k, c:c + ED], start=True, stop=True)
                    mm.then_inc(e_s_mm, 1)
                for s in SL:
                    pe.wait_ge(e_blk, nth(s, hf + 1))
                    pe.wait_ge(e_v[s], hf * 2 + 2)
                    for b in range(G):
                        pe.matmul(bank4(s)[:, b, :], qT[s][:, b * P:(b + 1) * P], ablk[s][:, b, :], start=True, stop=False)
                        mm = pe.matmul(bank4(s)[:, b, :], kT[s][:, b * P:(b + 1) * P], ablk[s][:, G + b, :], start=False, stop=True)
                    mm.then_inc(e_o_mm, 1)
                for s in SL:
                    hT_tr(s, n0 + LN_M, 6 + s)
                    if s == 1:
                        for k in SL:
                            pe.wait_ge(hT_done, both(k, hf * NTR + (TR_M + 1)))
                    pe.matmul(bank(s), zeros[:, :], zero_row, start=True, stop=False, skip_group_check=True)
                with pe.Fori(0, NEXP // 2) as p:
                    e = hf * (NEXP // 2) + p
                    n = e * 16
                    for u in range(16 + 2):
                        if u < 16:
                            k, c, s = u // 8, u % 8 // 2, u % 2
                            if u % 8 == 0:
                                pe.wait_ge(wexp_in[k], e * 48 + 48)
                            if u >= 2:
                                pe.wait_ge(hu_done, n + u - 1)
                            pe.matmul(bank(2 + s), wg[k][:, c * P:(c + 1) * P], hT[s][:, :], start=True, stop=True)
                            pe.matmul(bank(4 + s), wu[k][:, c * P:(c + 1) * P], hT[s][:, :], start=True, stop=True).then_inc(gu_mm, 1)
                        if u >= 2:
                            v = u - 2
                            k, c, s = v // 8, v % 8 // 2, v % 2
                            if u >= 16:
                                pe.wait_ge(hu_done, n + v + 1)
                            mm = pe.matmul(bank(s), wd[k][:, c, :], big[s][:, c, :], start=False, stop=True, skip_group_check=True)
                            if v % 8 == 7:
                                mm.then_inc(d_mm, 1)
                for s in SL:
                    mm = pe.matmul(bank(s), zeros[:, :], zero_row, start=False, stop=True, skip_group_check=True)
                    mm.then_inc(y_mm, 1)
                for s in SL:
                    pe.wait_ge(y_copy, nth(s, hf + 1))
                    transposes(bank(2 + s), sg[s][:, :].rearrange("p (b t) -> p b t", b=G), ident[:, :], yT_mm)

        @block.vector
        def _(dve):
            def layer_norm(s, n, src=None):
                src = xs[s] if src is None else src
                for b in range(G):
                    ins = dve.bn_stats(stats[s][:, b, :], src[:, b, :])
                ins.then_inc(ln_stats, 1)
                dve.wait_ge(ln_stats, nth(s, n + 1))
                met(dve)
                for b in range(G):
                    ins = dve.bn_aggr(mv[s][:, b, :], stats[s][:, b, :])
                ins.then_inc(ln_var, 1)

            def normalize(s, n, src=None):
                src = xs[s] if src is None else src
                dve.wait_ge(ln_rstd, nth(s, n + 1))
                for b in range(G):
                    ins = dve.tensor_scalar(h[s][:, b, :], src[:, b, :], mv[s][:, b, 0:1], rstd[s][:, b:b + 1], ALU.subtract, ALU.mult)
                    if b % GU == GU - 1:
                        ins.then_inc(ln_h, 1)

            def positive_keys(u, i):
                dve.wait_ge(k_exp, nth_unit(u, i + 1))
                dve.wait_ge(k_relu, nth_unit(u, i + 1))
                dve.scalar_tensor_tensor(part(kp, u), part(ke, u), 1.0, part(kp, u), ALU.min, ALU.add).then_inc(k_pos, 1)

            def positive_queries(u, i):
                q = qT[u // 2][:, cols(u)]
                dve.wait_ge(q_exp, nth_unit(u, i + 1))
                dve.scalar_tensor_tensor(q, qe[u // 2][:, cols(u)], 1.0, q, ALU.min, ALU.add).then_inc(q_pos, 1)

            def add_unit(u, i, product, biased):
                dve.wait_ge(product, nth_unit(u, i + 1))
                dve.wait_ge(biased, nth(u // 2, i + 1))
                dve.tensor_tensor(part(xs, u), bank(2 * u + 1)[:, 0:WU].rearrange("p (b c) -> p b c", b=GU), part(xb, u), ALU.add).then_inc(x_upd, 1)

            def ln(n, update=None, meanwhile=None):
                for s in SL:
                    if update is not None:
                        update(s)
                    dve.wait_ge(x_upd, both(s, n))
                    layer_norm(s, n)
                for s in SL:
                    if s == 1 and meanwhile is not None:
                        meanwhile()
                    if s == 1 or update is None:
                        normalize(s, n)


            def cross_sums(hf, a):
                n = hf * NB + a
                dve.wait_ge(exp_done, hf * (2 * NB) + (a + 1))
                if a >= 2:
                    dve.wait_ge(x_prob, n - 1)
                dve.tensor_reduce(zden[a % 2][:, :], E[a % 2][:, :, :], AX.X, ALU.add).then_inc(x_sum, 1)
                dve.wait_ge(x_sum, n + 1)
                dve.reciprocal(zden[a % 2][:, :], zden[a % 2][:, :]).then_inc(z_done, 1)

            def cross_outputs(hf, a):
                s, c = a // G, a % G
                n = hf * (2 * NB) + a
                dve.wait_ge(o_mm, n + 1)
                dve.tensor_tensor(own[a % 2], bank(6 + a % 2).rearrange("p (j q) -> p j q", j=4),
                                  head_in_quad.unsqueeze(2).to_broadcast([P, 4, P]), ALU.mult).then_inc(x_own, 1)
                dve.wait_ge(x_own, hf * NB + (a + 1))
                dve.tensor_reduce(atT[s][:, c * P:(c + 1) * P], own[a % 2].rearrange("p j q -> p q j"), AX.X, ALU.add).then_inc(o_done, 1)

            def head_outputs(off, hf, a):
                n = hf * (2 * NB) + (off + a)
                dve.wait_ge(o_mm, n + 1)
                o = bank(6 + a % 2)[:, 0:H * VA].rearrange("p (h d) -> p h d", h=H)
                dve.reciprocal(zden[a % 2][:, :], o[:, :, DH]).then_inc(z_done, 1)
                dve.wait_ge(z_done, n + 1)
                dve.tensor_tensor(at[a // G][:, a % G, :].rearrange("p (h d) -> p h d", h=H), o[:, :, 0:DH],
                                  zden[a % 2][:, :].unsqueeze(2).to_broadcast([P, H, DH]), ALU.mult).then_inc(o_done, 1)


            def above_mean(hf, b):
                t, s, c = b % 2, b // G, b % G
                k = hf * (4 * NB) + 4 * b
                if c == 0:
                    dve.wait_ge(tmean_done, nth(s, hf + 1))
                dve.wait_ge(s_out, hf * (2 * NB) + (NB + b + 1))
                for hd in range(H):
                    ins = dve.tensor_scalar(far[t][:, hd, :], S[b % 3][:, hd, :], tmean[s][:, c, hd:hd + 1], 0.0, ALU.is_ge, ALU.add,
                                            accum_out=cnt[t][:, hd:hd + 1])
                ins.then_inc(t_side, 1)
                dve.wait_ge(t_side, k + 1)
                dve.tensor_scalar(above[t][:, :], cnt[t][:, :], float(TOPK), None, ALU.is_ge)
                dve.tensor_scalar(okd[t][:, :], cnt[t][:, :], -1.0, TOPK - 0.5, ALU.mult, ALU.add)
                dve.tensor_scalar(dist[t][:, :], cnt[t][:, :], TOPK - 0.5, None, ALU.subtract).then_inc(t_side, 1)
                dve.wait_ge(t_side, k + 2)
                dve.tensor_tensor(dist[t][:, :], dist[t][:, :], okd[t][:, :], ALU.max)
                dve.tensor_scalar(ngr[t][:, :], above[t][:, :], -2.0, 1.0, ALU.mult, ALU.add)
                dve.tensor_scalar(fmul[t][:, :], above[t][:, :], -2.0 * FAR, FAR, ALU.mult, ALU.add)
                dve.tensor_scalar(fadd[t][:, :], above[t][:, :], FAR, None, ALU.mult).then_inc(t_side, 1)
                dve.wait_ge(t_side, k + 3)
                dve.tensor_scalar(okd[t][:, :], dist[t][:, :], NEAR - 1.0, None, ALU.is_le)
                dve.tensor_tensor(hit[t][:, :, :], half_count.unsqueeze(1).to_broadcast([P, H, NEAR]),
                                  dist[t][:, :].unsqueeze(2).to_broadcast([P, H, NEAR]), ALU.is_equal).then_inc(t_side, 1)

            def short_way(hf, b):
                t = b % 2
                k = (hf * NB + b) * TSTEPS
                dve.wait_ge(z_ready, hf * NB + (b + 1))
                met(dve)
                for hd in range(H):
                    ins = dve.max(near[:, hd, 0:8], Wk[t][:, hd, :])
                ins.then_inc(t_step, 1)
                dve.wait_ge(t_step, k + 1)
                met(dve)
                for hd in range(H):
                    ins = dve.match_replace(Wk[t][:, hd, :], near[:, hd, 0:8], Wk[t][:, hd, :], TAKEN)
                ins.then_inc(t_step, 1)
                dve.wait_ge(t_step, k + 2)
                met(dve)
                for hd in range(H):
                    ins = dve.max(near[:, hd, 8:16], Wk[t][:, hd, :])
                ins.then_inc(t_step, 1)
                dve.wait_ge(t_step, k + 3)
                dve.tensor_tensor(same[:, :, :], hit[t][:, :, :], near[:, :, :], ALU.mult).then_inc(t_step, 1)
                dve.wait_ge(t_step, k + 4)
                dve.tensor_reduce(picked[:, :], same[:, :, :], AX.X, ALU.add).then_inc(t_step, 1)
                dve.wait_ge(t_step, k + 5)
                dve.tensor_tensor(theta[t][:, :], picked[:, :], ngr[t][:, :], ALU.mult)
                dve.tensor_tensor(same[:, :, :], near[:, :, :], picked[:, :].unsqueeze(2).to_broadcast([P, H, NEAR]), ALU.is_equal).then_inc(t_step, 1)
                dve.wait_ge(t_step, k + 6)
                dve.tensor_reduce(okh[t][:, :], same[:, :, :], AX.X, ALU.add).then_inc(t_step, 1)
                dve.wait_ge(t_step, k + 7)
                dve.scalar_tensor_tensor(okh[t][:, :], okh[t][:, :], 1.0, okd[t][:, :], ALU.is_equal, ALU.mult).then_inc(t_step, 1)
                dve.wait_ge(t_step, k + 8)
                dve.tensor_reduce(okq[t][:, :], okh[t][:, :].rearrange("p (q j) -> p q j", j=4), AX.X, ALU.add).then_inc(ok_done, 1)

            def long_way(b, q):
                t = b % 2
                heads = range(4 * q, 4 * q + 4)
                dve.drain()
                for r in range(ROUNDS):
                    src = S[b % 3] if r == 0 else Wk[t]
                    for hd in heads:
                        dve.max(near[:, hd, 0:8], src[:, hd, :])
                    dve.drain()
                    for hd in heads:
                        dve.match_replace(Wk[t][:, hd, :], near[:, hd, 0:8], src[:, hd, :], TAKEN)
                    dve.drain()
                for hd in heads:
                    dve.tensor_scalar(keep[:, hd, :], Wk[t][:, hd, :], TAKEN, None, ALU.is_equal)

            def mark_kept(hf, b):
                t = b % 2
                n = hf * NB + b
                if b >= 1:
                    dve.wait_ge(prob_done, n)
                dve.tensor_tensor(keep[:, :, :], S[b % 3][:, :, :], theta[t][:, :].unsqueeze(2).to_broadcast([P, H, P]), ALU.is_ge)
                dve.wait_ge(bad_mm, n + 1)
                dve.tensor_scalar(bad[t][0:1, 0:4], bank(6 + t)[0:1, 200:204], -1.0, float(4 * P), ALU.mult, ALU.add)
                dve.tensor_reduce(settled_f[t][0:1, 0:1], bank(6 + t)[0:1, 200:204], AX.X, ALU.add).then_inc(bad_done, 1)
                dve.wait_ge(bad_done, n * 2 + 1)
                dve.tensor_scalar(bad[t][0:1, 4:5], settled_f[t][0:1, 0:1], 1.0, None, ALU.mult).then_inc(bad_done, 1)
                dve.wait_ge(bad_done, n * 2 + 2)
                met(dve)
                settled = dve.value_load(bad[t][0:1, 4:5], min_val=0, max_val=H * P)
                with dve.If(settled < H * P):
                    for q in range(4):
                        unsettled = dve.value_load(bad[t][0:1, q:q + 1], min_val=0, max_val=4 * P)
                        with dve.If(unsettled > 0):
                            long_way(b, q)
                dve.drain()
                dve.sem_inc(keep_done, 1)

            def residual(att, hf, s):
                dve.wait_ge(ao_mm, nth(s, hf * 2 + att + 1))
                dve.wait_ge(xba_done[s], hf * 3 + (1, 3)[att])
                dve.tensor_tensor(xs[s][:, :, :], bank4(2 + s), xb[s][:, :, :], ALU.add).then_inc(x_upd, 2)

            def act_scales(s, n):
                dve.wait_ge(c_step[s], n + 1)
                dve.tensor_scalar(amax[s][:, :], amax[s][:, :], 1e-5, None, ALU.max).then_inc(c_step[s], 1)
                dve.wait_ge(c_step[s], n + 2)
                dve.reciprocal(asc[s][:, :], amax[s][:, :]).then_inc(c_step[s], 1)
                dve.wait_ge(c_step[s], n + 3)
                dve.tensor_scalar(asc[s][:, :], asc[s][:, :], 127.0, None, ALU.mult).then_inc(c_step[s], 1)

            dve.wait_ge(consts_in, 64)
            dve.wait_ge(preset, 1)
            dve.tensor_copy(identb[:, :], ident[:, :])
            dve.sem_inc(stored, 1)
            dve.wait_ge(cw_in, 32)
            for k in range(2):
                dve.tensor_reduce(wsum[:, k:k + 1], wc_raw[:, k, :], AX.X, ALU.add, apply_absolute_value=True).then_inc(wq_sem, 1)
            dve.wait_ge(wsum_mm, 1)
            dve.tensor_scalar(wscale[:, :], bank(7)[:, 0:2], 1.0 / (P * FH), 1e-5, ALU.mult, ALU.max).then_inc(wq_sem, 1)
            dve.wait_ge(wq_sem, 3)
            dve.reciprocal(wrs[:, :], wscale[:, :]).then_inc(wq_sem, 1)
            dve.wait_ge(wq_sem, 4)
            for k in range(2):
                dve.tensor_scalar(wc_raw[:, k, :], wc_raw[:, k, :], wrs[:, k:k + 1], MAGIC, ALU.mult, ALU.add).then_inc(wq_sem, 1)
            dve.wait_ge(wq_sem, 6)
            dve.tensor_scalar(wc_raw[:, :, :], wc_raw[:, :, :], MAGIC, 1.0, ALU.subtract, ALU.min).then_inc(wq_sem, 1)
            dve.wait_ge(wq_sem, 7)
            dve.tensor_scalar(wcq[:, :, :], wc_raw[:, :, :], -1.0, None, ALU.max).then_inc(wq_done, 1)

            for s in SL:
                dve.wait_ge(x_in[s], 16)
                layer_norm(s, LN_IN, xin[s])
            for s in SL:
                normalize(s, LN_IN, xin[s])
            with dve.Fori(0, HALVES) as hf:
                n0 = hf * NLN

                def embedded(s):
                    dve.wait_ge(ln_h, both(s, n0 + (LN_IN + 1)))
                    if s == 1:
                        normalize(0, n0 + LN_A)
                    if s == 0:
                        dve.wait_ge(stored, hf * (16 * SLOTS) + 1)
                    dve.scalar_tensor_tensor(xs[s][:, :, :], h[s][:, :, :], float(np.sqrt(P)), pos[:, :].unsqueeze(1).to_broadcast([P, G, P]),
                                             ALU.mult, ALU.add).then_inc(x_upd, 2)

                ln(n0 + LN_A, embedded)
                with dve.Fori(0, L) as l:
                    i = hf * L + l
                    dve.wait_ge(wqkv_in, i * 48 + 48)
                    for u in UN:
                        dve.wait_ge(kv_mm, nth_unit(u, i + 1))
                        kv = bank(2 * u).rearrange("p (b c) -> p b c", b=GU)
                        dve.tensor_tensor(part(kk, u), kv[:, :, 0:P], rowkv[:, 0:P].unsqueeze(1).to_broadcast([P, GU, P]), ALU.add).then_inc(k_raw, 1)
                        dve.tensor_tensor(part(vv, u)[:, :, 0:P], kv[:, :, P:2 * P], rowkv[:, P:2 * P].unsqueeze(1).to_broadcast([P, GU, P]), ALU.add).then_inc(v_raw, 1)
                        if u >= 1:
                            positive_keys(u - 1, i)
                            positive_queries(u - 1, i)
                    positive_keys(UNITS - 1, i)
                    positive_queries(UNITS - 1, i)
                    for u in UN:
                        dve.wait_ge(kvs_mm, nth_unit(u, i + 1))
                        kv = bank(2 * u).rearrange("p (b c) -> p b c", b=GU)
                        dve.tensor_tensor(part(kvs, u)[:, :, 0:P], kv[:, :, 0:P], same_head.unsqueeze(1).to_broadcast([P, GU, P]), ALU.mult)
                        dve.tensor_tensor(part(kvs, u)[:, :, P:P + H], kv[:, :, P:P + 1].to_broadcast([P, GU, H]),
                                          head_of.unsqueeze(1).to_broadcast([P, GU, H]), ALU.mult).then_inc(kv_sum, 1)
                    for s in SL:
                        for u in UNITS_OF[s]:
                            dve.wait_ge(lin_mm, nth_unit(u, i + 1))
                            o = bank(2 * u + 1).rearrange("p (b c) -> p b c", b=GU)
                            dve.tensor_scalar(part(den, u), o[:, :, P:P + H], EPS_ATTN, None, ALU.add).then_inc(den_eps, 1)
                        for u in UNITS_OF[s]:
                            dve.wait_ge(den_eps, nth_unit(u, i + 1))
                            dve.reciprocal(part(den, u), part(den, u)).then_inc(den_inv, 1)
                        for u in UNITS_OF[s]:
                            o = bank(2 * u + 1).rearrange("p (b c) -> p b c", b=GU)
                            dve.wait_ge(den_inv, nth_unit(u, i + 1))
                            dve.tensor_tensor(part(at, u).rearrange("p b (h d) -> p b h d", h=H), o[:, :, 0:P].rearrange("p b (h d) -> p b h d", h=H),
                                              part(den, u).unsqueeze(3).to_broadcast([P, GU, H, DH]), ALU.mult).then_inc(lin_done, 1)

                    def attended(s):
                        for u in UNITS_OF[s]:
                            add_unit(u, i, wo_mm, xbo_done)
                        if s == 1:
                            normalize(0, n0 + l * 2 + (LN_A + 1))

                    def fed_forward(s):
                        if s == 1:
                            normalize(0, n0 + l * 2 + (LN_A + 2))
                        for u in UNITS_OF[s]:
                            add_unit(u, i, w2_mm, xb2_done)

                    ln(n0 + l * 2 + (LN_A + 1), attended)
                    ln(n0 + l * 2 + (LN_A + 2), fed_forward)
                dve.wait_ge(rowf_in, 16)

                def cross_values(s):
                    dve.wait_ge(attw_in, 16 * 6)
                    dve.wait_ge(pv_mm, nth(s, hf * 2 + 1))
                    dve.tensor_tensor(vv[s][:, :, 0:P], bank4(4 * s + 3), ratt[0][:, 0:P].unsqueeze(1).to_broadcast([P, G, P]), ALU.add).then_inc(pv_done, 1)

                def encoded(s):
                    dve.wait_ge(ln_h, both(s, n0 + (LN_F + 1)))
                    dve.tensor_tensor(h[s][:, :, :], h[s][:, :, :], rowf[:, 0:P].unsqueeze(1).to_broadcast([P, G, P]), ALU.mult).then_inc(f_scaled[s], 1)
                    dve.wait_ge(f_scaled[s], hf * 2 + 1)
                    dve.tensor_tensor(h[s][:, :, :], h[s][:, :, :], rowf[:, P:2 * P].unsqueeze(1).to_broadcast([P, G, P]), ALU.add).then_inc(f_scaled[s], 1)
                    if s == 1:
                        normalize(0, n0 + LN_B)
                        cross_values(0)
                    dve.wait_ge(f_scaled[s], hf * 2 + 2)
                    dve.tensor_tensor(xs[s][:, :, :], xin[s][:, :, :], h[s][:, :, :], ALU.add).then_inc(x_upd, 2)
                ln(n0 + LN_B, encoded)
                for s in SL:
                    dve.sem_inc(xin_used[s], 1)
                cross_values(1)
                for t in range(2):
                    dve.memset(S[t][:, :, :], NEG).then_inc(s_preset, 1)
                for b in range(NB + 2):
                    if b < NB:
                        n = hf * (2 * NB) + b
                        dve.wait_ge(s_mm, n + 1)
                        if b < 3:
                            dve.wait_ge(s_preset, hf * 3 + (b + 1))
                        if b >= 2:
                            dve.wait_ge(sub_done, n - 1)
                        met(dve)
                        dve.copy_predicated(S[b % 3][:, :, :], maskt[:, :].unsqueeze(1).to_broadcast([P, H, P]),
                                            bank(0, 4).rearrange("p (h k) -> p h k", h=H)).then_inc(s_out, 1)
                        dve.wait_ge(s_out, n + 1)
                        dve.tensor_reduce(smax[b % 2][:, :], S[b % 3][:, :, :], AX.X, ALU.max).then_inc(m_done, 1)
                    if b == 0:
                        dve.memset(S[2][:, :, :], NEG).then_inc(s_preset, 1)
                    if 1 <= b <= NB:
                        cross_sums(hf, b - 1)
                    if b >= 3:
                        cross_outputs(hf, b - 3)
                    if b == NB:
                        last = E[(NB - 1) % 2]
                        dve.wait_ge(z_done, hf * (2 * NB) + NB)
                        dve.wait_ge(x_prob, hf * NB + (NB - 1))
                        dve.tensor_tensor(last[:, :, :], last[:, :, :], zden[(NB - 1) % 2][:, :].unsqueeze(2).to_broadcast([P, H, P]), ALU.mult).then_inc(x_prob, 1)
                cs = hf * 13

                def quantize(s):
                    dve.wait_ge(ln_h, both(s, n0 + (LN_C + 1)))
                    dve.tensor_reduce(amax[s][:, :], h[s][:, :, :], AX.X, ALU.max, apply_absolute_value=True).then_inc(c_step[s], 1)
                    act_scales(s, cs)
                    dve.tensor_scalar(deq[s][:, :], amax[s][:, :], 1.0 / 127.0, None, ALU.mult).then_inc(c_step[s], 1)
                    dve.wait_ge(c_step[s], cs + 5)
                    dve.tensor_tensor(yT[s][:, :, :], ident[:, :].unsqueeze(1).to_broadcast([P, G, P]),
                                      deq[s][:, :].unsqueeze(2).to_broadcast([P, G, P]), ALU.mult).then_inc(c_diag, 1)
                    for b in range(G):
                        ins = dve.tensor_scalar(h[s][:, b, :], h[s][:, b, :], asc[s][:, b:b + 1], MAGIC, ALU.mult, ALU.add)
                    ins.then_inc(c_step[s], 1)
                    dve.wait_ge(c_step[s], cs + 6)
                    dve.tensor_scalar(h[s][:, :, :], h[s][:, :, :], MAGIC, 127.0, ALU.subtract, ALU.min).then_inc(c_step[s], 1)
                    dve.wait_ge(c_step[s], cs + 7)
                    dve.tensor_scalar(hqb[s][:, :, :], h[s][:, :, :], -128.0, None, ALU.max).then_inc(c_q1, 1)

                def crossed(s):
                    if s == 1:
                        cross_outputs(hf, NB - 1)
                        normalize(0, n0 + LN_C)
                        quantize(0)
                    residual(0, hf, s)

                ln(n0 + LN_C, crossed)
                quantize(1)

                def chunk_max(s, c):
                    dve.wait_ge(c_silu, nth(s, hf * CH + c + 1))
                    dve.tensor_reduce(cmax[s][:, :, c], big[s][:, :, c * P:(c + 1) * P], AX.X, ALU.max, apply_absolute_value=True).then_inc(c_max, 1)

                for c in range(CH):
                    for s in SL:
                        dve.wait_ge(c_f1_mm, nth(s, hf * CH + c + 1))
                        if c == 0:
                            dve.wait_ge(c_rs, nth(s, hf + 1))
                        else:
                            dve.wait_ge(c_conv, nth(s, hf * CH + c))
                        dve.tensor_tensor(cbuf[s][:, :, 1:P + 1], bank4(4 * s + 2), rsb[s][:, :].rearrange("p (b t) -> p b t", b=G), ALU.mult).then_inc(c_deq, 1)
                    if c >= 1:
                        for s in SL:
                            chunk_max(s, c - 1)
                    for s in SL:
                        dve.wait_ge(c_tap1, nth(s, hf * CH + c + 1))
                        dve.scalar_tensor_tensor(yT[s][:, :, :], cbuf[s][:, :, 0:P], conv[:, c, 0:1], yT[s][:, :, :], ALU.mult, ALU.add).then_inc(f_conv, 1)
                        dve.wait_ge(f_conv, nth(s, hf * CH + c + 1))
                        dve.scalar_tensor_tensor(yT[s][:, :, :], cbuf[s][:, :, 2:P + 2], conv[:, c, 2:3], yT[s][:, :, :], ALU.mult, ALU.add).then_inc(c_conv, 1)
                for s in SL:
                    chunk_max(s, CH - 1)
                    dve.wait_ge(c_max, nth(s, hf * CH + CH))
                    dve.tensor_reduce(amax[s][:, :], cmax[s][:, :, :], AX.X, ALU.max).then_inc(c_step[s], 1)
                    act_scales(s, cs + 7)
                    dve.wait_ge(c_step[s], cs + 11)
                    for b in range(G):
                        ins = dve.tensor_scalar(big[s][:, b, :], big[s][:, b, :], asc[s][:, b:b + 1], MAGIC, ALU.mult, ALU.add)
                    ins.then_inc(c_step[s], 1)
                    dve.tensor_scalar(deq[s][:, :], amax[s][:, :], wscale[:, 1:2], 1.0 / 127.0, ALU.mult, ALU.mult)
                    dve.wait_ge(c_step[s], cs + 12)
                    dve.tensor_scalar(q2b[s][:, :, :], big[s][:, :, :], MAGIC, 127.0, ALU.subtract, ALU.min).then_inc(c_step[s], 1)
                    dve.wait_ge(c_step[s], cs + 13)
                    dve.tensor_scalar(q2b[s][:, :, :], q2b[s][:, :, :], -128.0, None, ALU.max).then_inc(c_q2, 1)

                def convolved(s):
                    if s == 1:
                        normalize(0, n0 + LN_D)
                    dve.wait_ge(c_f2_mm, nth(s, hf + 1))
                    for b in range(G):
                        ins = dve.scalar_tensor_tensor(xs[s][:, b, :], bank4(4 * s + 2)[:, b, :], deq[s][:, b:b + 1], xs[s][:, b, :], ALU.mult, ALU.add)
                    ins.then_inc(x_upd, 2)

                ln(n0 + LN_D, convolved)

                def topk_values(s):
                    dve.wait_ge(pk_done, nth(s, hf * 2 + 2))
                    dve.tensor_reduce(ksum[s][:, :], kT[s][:, :].rearrange("p (b t) -> p b t", b=G), AX.X, ALU.add).then_inc(ksum_done, 1)
                    dve.wait_ge(ksum_done, nth(s, hf + 1))
                    dve.tensor_tensor(kmean[s][:, :, :], ksum[s][:, :].unsqueeze(2).to_broadcast([P, G, H]),
                                      head_of.unsqueeze(1).to_broadcast([P, G, H]), ALU.mult).then_inc(kmean_done, 1)
                    dve.wait_ge(pv_mm, nth(s, hf * 2 + 2))
                    for b in range(G):
                        ins = dve.tensor_tensor(vaug[s][:, b, :, 0:DH], bank4(4 * s + 3)[:, b, :].rearrange("p (h d) -> p h d", h=H),
                                                ratt[1][:, 0:P].rearrange("p (h d) -> p h d", h=H), ALU.add)
                    ins.then_inc(pv_done, 1)

                topk_values(0)
                for b in range(NB + 2):
                    if b < NB:
                        above_mean(hf, b)
                    if b == 0:
                        topk_values(1)
                    if b >= 3:
                        head_outputs(NB, hf, b - 3)
                    if 1 <= b <= NB:
                        short_way(hf, b - 1)
                    if b < NB:
                        dve.wait_ge(s_out, hf * (2 * NB) + (NB + b + 1))
                        if b >= 2:
                            dve.wait_ge(sub_done, hf * (2 * NB) + (NB + b - 1))
                        dve.tensor_reduce(smax[b % 2][:, :], S[b % 3][:, :, :], AX.X, ALU.max).then_inc(m_done, 1)
                    if 1 <= b <= NB:
                        mark_kept(hf, b - 1)
                    if b == NB:
                        last = E[(NB - 1) % 2]
                        dve.wait_ge(exp_done, hf * (2 * NB) + 2 * NB)
                        dve.tensor_tensor(last[:, :, :], last[:, :, :], keep[:, :, :], ALU.mult).then_inc(prob_done, 1)

                def scale_channels(s, src, js, n):
                    m = hf * (4, 2)[s] + n
                    for j in js:
                        dve.tensor_tensor(channels(s, j), src[s][:, :, :], rowe[:, 2 * j, :].unsqueeze(1).to_broadcast([P, G, P]), ALU.mult).then_inc(e_mul[s], 1)
                    for k, j in enumerate(js):
                        dve.wait_ge(e_mul[s], m + (k + 1))
                        dve.tensor_tensor(channels(s, j), channels(s, j), rowe[:, 2 * j + 1, :].unsqueeze(1).to_broadcast([P, G, P]), ALU.add).then_inc(e_qk[s], 1)

                def attended_topk(s):
                    if s == 1:
                        head_outputs(NB, hf, NB - 1)
                        normalize(0, n0 + LN_E)
                        dve.wait_ge(ln_h, both(0, n0 + (LN_E + 1)))
                        scale_channels(0, h, (0, 1), 2)
                    residual(1, hf, s)

                e = hf * 5

                def channel_scores(s):
                    sc = bank(4 + s)[:, 0:2 * G * ED].rearrange("p (a e) -> p a e", a=2 * G)
                    dve.wait_ge(e_s_mm, nth(s, hf + 1))
                    dve.tensor_reduce(sm[s][:, :], sc, AX.X, ALU.max).then_inc(e_step[s], 1)
                    dve.wait_ge(e_step[s], e + 1)
                    dve.tensor_tensor(se[s][:, :, :], sc, sm[s][:, :].unsqueeze(2).to_broadcast([P, 2 * G, ED]), ALU.subtract).then_inc(e_sub, 1)

                def channel_weights(s):
                    dve.wait_ge(e_exp, nth(s, hf + 1))
                    dve.tensor_reduce(sm[s][:, :], se[s][:, :, :], AX.X, ALU.add).then_inc(e_step[s], 1)
                    dve.wait_ge(e_step[s], e + 2)
                    dve.reciprocal(sm[s][:, :], sm[s][:, :]).then_inc(e_step[s], 1)
                    dve.wait_ge(e_step[s], e + 3)
                    dve.tensor_tensor(se[s][:, :, :], se[s][:, :, :], sm[s][:, :].unsqueeze(2).to_broadcast([P, 2 * G, ED]), ALU.mult).then_inc(e_step[s], 1)
                    dve.wait_ge(e_step[s], e + 4)
                    dve.transpose(seT[s][:, :, :].rearrange("p a e -> p (a e)"), se[s][:, :, :].rearrange("p a e -> p (a e)")).then_inc(e_step[s], 1)

                dve.wait_ge(o_mm, hf * (2 * NB) + 2 * NB - 1)
                dve.wait_ge(ew_in, 32)
                scale_channels(0, ctxt, (2, 3), 0)
                ln(n0 + LN_E, attended_topk, lambda: channel_scores(0))
                dve.wait_ge(ln_h, both(1, n0 + (LN_E + 1)))
                scale_channels(1, h, (0, 1), 0)
                channel_weights(0)
                channel_scores(1)
                channel_weights(1)

                def attended_channels(s):
                    dve.wait_ge(e_o_mm, nth(s, hf + 1))
                    dve.scalar_tensor_tensor(h[s][:, :, :], bank4(s), 2.0, rowe[:, 8, :].unsqueeze(1).to_broadcast([P, G, P]), ALU.mult, ALU.mult).then_inc(e_out, 1)
                    if s == 1:
                        normalize(0, n0 + LN_M)
                    dve.wait_ge(e_out, nth(s, hf + 1))
                    dve.wait_ge(e_xb, nth(s, hf + 1))
                    dve.tensor_tensor(xs[s][:, :, :], h[s][:, :, :], xb[s][:, :, :], ALU.add).then_inc(x_upd, 2)

                ln(n0 + LN_M, attended_channels)
                for s in SL:
                    dve.sem_inc(ctx_used[s], 1)
                for s in SL:
                    dve.wait_ge(x_in[s], hf * 16 + 32)
                    layer_norm(s, n0 + (NLN + LN_IN), xin[s])
                with dve.Fori(0, NEXP // 2) as p:
                    n = (hf * (NEXP // 2) + p) * 16
                    for u in range(16):
                        s, c = u % 2, u % 8 // 2
                        dve.wait_ge(silu_done, n + u + 1)
                        if u == 8:
                            dve.wait_ge(d_mm, (hf * (NEXP // 2) + p) * 2 + 1)
                        dve.tensor_tensor(big[s][:, c, :], bank(4 + s), sg[s][:, :], ALU.mult).then_inc(hu_done, 1)
                for s in SL:
                    dve.wait_ge(hT_mm, both(s, hf * NTR + (TR_M + 1)))
                    normalize(s, n0 + (NLN + LN_IN), xin[s])
                for s in SL:
                    dve.wait_ge(yT_mm, nth(s, hf + 1))
                    dve.tensor_tensor(xs[s][:, :, :], bank4(2 + s), xs[s][:, :, :], ALU.add).then_inc(x_upd, 2)




def kernel(x, ctx_1024, mask_1x1xSxS2_ik0, **w):
    import concourse.bacc as _bacc
    from concourse.bass_utils import run_bass_kernel_spmd as _run

    def a(name):
        return np.asarray(w[name])

    def rows(*vs):
        return np.concatenate([np.asarray(v).reshape(1, -1) for v in vs], axis=1)

    def cols(*vs):
        return np.stack([np.asarray(v).reshape(-1) for v in vs], axis=1)

    def chunked(m):
        m = m.reshape(m.shape[:-2] + (CH, P, m.shape[-1]))
        return np.moveaxis(m, -3, -2).reshape(m.shape[:-3] + (P, CH * m.shape[-1]))

    arrow = np.concatenate([
        np.concatenate([a("L0_attn_bk"), a("L0_attn_bv"), a("L0_attn_bo"), a("L0_attn_b2")], axis=1),
        rows(a("L0_attn_lnf_s"), a("L0_attn_lnf_b"), a("L0_attn_lnf_s"), a("L0_attn_lnf_b"))], axis=0)
    wq4, wk4, wv4, wo4 = (a("L0_attn_W" + n) for n in "qkvo")
    b1 = a("L0_attn_b1").reshape(L, CH, P).transpose(0, 2, 1)
    qkv = a("L1_attn_w_qkv_w").reshape(H, 3, DH, P).transpose(1, 0, 2, 3).reshape(3, P, P)
    qkvb = a("L1_attn_w_qkv_b").reshape(H, 3, DH).transpose(1, 0, 2).reshape(3, P)

    r = np.arange(P)
    const = np.concatenate([r[:, None] // DH == r[None, :] // DH, r[:, None] // DH == np.arange(H)[None, :],
                            r[:, None] % 32 // DH == np.arange(4)[None, :], r[:, None] // 32 == np.arange(4)[None, :],
                            np.zeros((P, 1)) + np.arange(NEAR)[None, :] + 0.5], axis=1).astype(np.float32)
    half = P // 2
    freq = np.exp(np.arange(half, dtype=np.float32) * np.float32(-np.log(10000.0) / (half - 1))).astype(np.float32)
    ang = ((np.arange(P, dtype=np.float32) + np.float32(1.0))[:, None] * freq[None, :]).astype(np.float32)
    pos = np.concatenate([np.sin(ang), np.cos(ang)], axis=1).astype(np.float32)

    ins = {
        "x": x, "ctx": ctx_1024, "mask": np.asarray(mask_1x1xSxS2_ik0).reshape(P, P),
        "aw": np.concatenate([wq4, wk4, wv4, wo4, a("L0_attn_W1")], axis=2),
        "acolA": np.stack([a("L0_attn_ln1_s"), a("L0_attn_ln1_b"), a("L0_attn_bq")], axis=2),
        "acolB": np.concatenate([a("L0_attn_ln2_s")[:, :, None], a("L0_attn_ln2_b")[:, :, None], b1], axis=2),
        "arow": arrow, "w2a": chunked(a("L0_attn_W2")),
        "bw": np.concatenate([a("L0_xattn_W" + n).T for n in "qkvo"], axis=1),
        "bcol": cols(a("L0_xattn_bq"), a("L0_xattn_bk")), "brow": rows(a("L0_xattn_bv"), a("L0_xattn_bo")),
        "cw": np.concatenate([a("L0_ffn_w1").T, chunked(a("L0_ffn_w2").T)], axis=1),
        "cconv": chunked(np.concatenate([a("L0_ffn_conv_w").reshape(FH, 3), a("L0_ffn_conv_b").reshape(FH, 1)], axis=1)),
        "dw": np.concatenate([qkv[0].T, qkv[1].T, qkv[2].T, a("L1_attn_w_out_w").T], axis=1),
        "dcol": cols(qkvb[0], qkvb[1]), "drow": rows(qkvb[2], a("L1_attn_w_out_b")),
        "erow": rows(*(a("L1_xattn_" + n) for n in ("wqg", "bqg", "wql", "bql", "wkg", "bkg", "wkl", "bkl", "wp", "bp"))),
        "ecol": cols(*(a("L1_xattn_" + n) for n in ("wvg", "bvg", "wvl", "bvl"))),
        "mg": a("L1_ffn_Wg"), "mu": a("L1_ffn_Wu"), "md": chunked(a("L1_ffn_Wd")),
        "ident": np.eye(P, dtype=np.float32), "const": const, "pos": pos,
    }
    nc = _bacc.Bacc("TRN2", target_bir_lowering=False, num_devices=1)
    arrays, args = {}, []
    for name, v in ins.items():
        v = np.ascontiguousarray(v)
        arrays[f"in_{name}"] = v
        args.append(nc.dram_tensor(f"in_{name}", v.shape, mybir.dt.from_np(v.dtype), kind="ExternalInput").ap())
    out = nc.dram_tensor("out_x", (NSEQ, P, P), F32, kind="ExternalOutput").ap()
    decoder(nc, *args, out)
    res = _run(nc, [arrays], core_ids=[0])
    return res.results[0]["out_x"]
```
